# Optimizing a Trainium2 kernel written in Bass

```python
import numpy as np
import jax
import jax.numpy as jnp

def _softmax(x, axis=-1):
    return jax.nn.softmax(x, axis=axis)

def _gelu(x):
    return jax.nn.gelu(x, approximate=True)

def _silu(x):
    return jax.nn.silu(x)

def _sigmoid(x):
    return jax.nn.sigmoid(x)

def _layernorm(x, axis=-1, eps=1e-05):
    m = jnp.mean(x, axis=axis, keepdims=True)
    v = jnp.var(x, axis=axis, keepdims=True)
    return (x - m) / jnp.sqrt(v + eps)

def _scatter_add(tgt, idx, src, axis=0):
    return tgt.at[idx].add(src)

def _segment_sum(src, seg, n):
    return jax.ops.segment_sum(src, seg, n)
kernel_name = 'mk_gnn_resnorm_d4_gnn_r16_a17050'

def setup_inputs(seed: int=0):
    np.random.seed(seed)
    _w = jnp.asarray

    def _rec_inputs():
        import jax
        import jax.numpy as jnp
        _gk = jax.random.key(seed)
        x = -0.0002117 + 1 * jax.random.normal(jax.random.fold_in(_gk, 1), (3125, 512), jnp.float32)
        src = jax.random.randint(jax.random.fold_in(_gk, 2), (50000,), 0, 3125, jnp.int32)
        dst = jax.random.randint(jax.random.fold_in(_gk, 3), (50000,), 0, 3125, jnp.int32)
        _o = jnp.argsort(dst, stable=True)
        src = src[_o]
        dst = dst[_o]
        edge_weight = jax.random.uniform(jax.random.fold_in(_gk, 12), (50000,), jnp.float32, 0.0, 1)
        return (x, src, dst, edge_weight)
    x, src, dst, edge_weight = _rec_inputs()

    def _L0_gnn_setup():
        import jax, jax.numpy as jnp
        import numpy as np
        N = 3125
        E = 25000
        D_IN = 512
        D_OUT = 512
        LN_EPS = 1e-05
        key = jax.random.key(seed)
        ks = jax.random.split(key, 8)
        x = jax.random.normal(ks[0], (N, D_IN), dtype=jnp.float32)
        src = jax.random.randint(ks[1], (E,), 0, N, dtype=jnp.int32)
        dst = jnp.sort(jax.random.randint(ks[2], (E,), 0, N, dtype=jnp.int32))
        bound = 1.0 / np.sqrt(D_IN)
        W_self = jax.random.uniform(ks[3], (D_IN, D_OUT), minval=-bound, maxval=bound, dtype=jnp.float32)
        b_self = jax.random.uniform(ks[4], (D_OUT,), minval=-bound, maxval=bound, dtype=jnp.float32)
        W_neigh = jax.random.uniform(ks[5], (D_IN, D_OUT), minval=-bound, maxval=bound, dtype=jnp.float32)
        gamma = jnp.ones((D_OUT,), dtype=jnp.float32)
        beta = jnp.zeros((D_OUT,), dtype=jnp.float32)
        alpha = jnp.array(0.25, dtype=jnp.float32)
        return {'x': x, 'src': src, 'dst': dst, 'W_self': W_self, 'b_self': b_self, 'W_neigh': W_neigh, 'gamma': gamma, 'beta': beta, 'alpha': alpha}
    _L0_gnn_all = _L0_gnn_setup()
    _L0_gnn_in = {k: v for k, v in _L0_gnn_all.items() if k in ('W_self', 'b_self', 'W_neigh', 'gamma', 'beta', 'alpha')}
    del _L0_gnn_all

    def _L1_gnn_setup():
        import jax, jax.numpy as jnp
        import numpy as np
        N_NODES = 3125
        N_EDGES = 100000
        D_IN = 512
        D_OUT = 512
        key = jax.random.key(seed)
        k_x, k_w, k_b, k_r, k_c, k_e = jax.random.split(key, 6)
        x = jax.random.normal(k_x, (N_NODES, D_IN), dtype=jnp.float32)
        stdv = 1.0 / np.sqrt(D_OUT)
        weight = jax.random.uniform(k_w, (D_IN, D_OUT), minval=-stdv, maxval=stdv, dtype=jnp.float32)
        bias = jax.random.uniform(k_b, (D_OUT,), minval=-stdv, maxval=stdv, dtype=jnp.float32)
        row = jax.random.randint(k_r, (N_EDGES,), 0, N_NODES, dtype=jnp.int32)
        col = jax.random.randint(k_c, (N_EDGES,), 0, N_NODES, dtype=jnp.int32)
        edge_weight = jax.random.uniform(k_e, (N_EDGES,), dtype=jnp.float32)
        return {'x': x, 'weight': weight, 'bias': bias, 'row': row, 'col': col, 'edge_weight': edge_weight}
    _L1_gnn_all = _L1_gnn_setup()
    _L1_gnn_in = {k: v for k, v in _L1_gnn_all.items() if k in ('weight', 'bias')}
    del _L1_gnn_all

    def _L2_gnn_setup():
        import jax, jax.numpy as jnp
        import numpy as np
        N, E, D = (625, 10000, 512)

        def _sage_layer(h, src, dst, W_self, W_neigh, b, n_nodes):
            agg = jax.ops.segment_sum(h[src], dst, num_segments=n_nodes)
            deg = jax.ops.segment_sum(jnp.ones_like(dst, dtype=h.dtype), dst, num_segments=n_nodes)
            h_neigh = agg / jnp.maximum(deg, 1.0)[:, None]
            return jax.nn.relu(h @ W_self + h_neigh @ W_neigh + b)
        key = jax.random.key(seed)
        ks = jax.random.split(key, 8)
        scale = 1.0 / np.sqrt(D)
        return {'feats': jax.random.normal(ks[0], (N, D), dtype=jnp.float32), 'src': jax.random.randint(ks[1], (E,), 0, N, dtype=jnp.int32), 'dst': jax.random.randint(ks[2], (E,), 0, N, dtype=jnp.int32), 'W_self1': jax.random.normal(ks[3], (D, D), dtype=jnp.float32) * scale, 'W_neigh1': jax.random.normal(ks[4], (D, D), dtype=jnp.float32) * scale, 'b1': jnp.zeros((D,), dtype=jnp.float32), 'W_self2': jax.random.normal(ks[5], (D, D), dtype=jnp.float32) * scale, 'W_neigh2': jax.random.normal(ks[6], (D, D), dtype=jnp.float32) * scale, 'b2': jnp.zeros((D,), dtype=jnp.float32)}
    _L2_gnn_all = _L2_gnn_setup()
    _L2_gnn_in = {k: v for k, v in _L2_gnn_all.items() if k in ('W_self1', 'W_neigh1', 'b1', 'W_self2', 'W_neigh2', 'b2')}
    del _L2_gnn_all

    def _L3_gnn_setup():
        import jax, jax.numpy as jnp
        import numpy as np
        N, E, DM, H, DFF = (1250, 40000, 512, 8, 128)
        DK = DM // H

        def _layernorm(x, g, b, eps=1e-05):
            mu = jnp.mean(x, axis=-1, keepdims=True)
            var = jnp.mean(jnp.square(x - mu), axis=-1, keepdims=True)
            return (x - mu) * jax.lax.rsqrt(var + eps) * g + b
        key = jax.random.key(seed)
        ks = jax.random.split(key, 12)
        s = 0.02
        h = jax.random.normal(ks[0], (N, DM), dtype=jnp.float32)
        src = jax.random.randint(ks[1], (E,), 0, N, dtype=jnp.int32)
        dst = jnp.sort(jax.random.randint(ks[2], (E,), 0, N, dtype=jnp.int32))
        return {'h': h, 'src': src, 'dst': dst, 'Wq': jax.random.normal(ks[3], (DM, DM), dtype=jnp.float32) * s, 'Wk': jax.random.normal(ks[4], (DM, DM), dtype=jnp.float32) * s, 'Wv': jax.random.normal(ks[5], (DM, DM), dtype=jnp.float32) * s, 'Wo': jax.random.normal(ks[6], (DM, DM), dtype=jnp.float32) * s, 'ln1_g': jnp.ones((DM,), jnp.float32), 'ln1_b': jnp.zeros((DM,), jnp.float32), 'ln2_g': jnp.ones((DM,), jnp.float32), 'ln2_b': jnp.zeros((DM,), jnp.float32), 'W1': jax.random.normal(ks[7], (DM, DFF), dtype=jnp.float32) * s, 'b1': jnp.zeros((DFF,), jnp.float32), 'W2': jax.random.normal(ks[8], (DFF, DM), dtype=jnp.float32) * s, 'b2': jnp.zeros((DM,), jnp.float32)}
    _L3_gnn_all = _L3_gnn_setup()
    _L3_gnn_in = {k: v for k, v in _L3_gnn_all.items() if k in ('Wq', 'Wk', 'Wv', 'Wo', 'ln1_g', 'ln1_b', 'ln2_g', 'ln2_b', 'W1', 'b1', 'W2', 'b2')}
    del _L3_gnn_all
    return {'x': x, 'src': src, 'dst': dst, 'edge_weight': edge_weight, 'L0_gnn_W_self': _L0_gnn_in['W_self'], 'L0_gnn_b_self': _L0_gnn_in['b_self'], 'L0_gnn_W_neigh': _L0_gnn_in['W_neigh'], 'L0_gnn_gamma': _L0_gnn_in['gamma'], 'L0_gnn_beta': _L0_gnn_in['beta'], 'L0_gnn_alpha': _L0_gnn_in['alpha'], 'L1_gnn_weight': _L1_gnn_in['weight'], 'L1_gnn_bias': _L1_gnn_in['bias'], 'L2_gnn_W_self1': _L2_gnn_in['W_self1'], 'L2_gnn_W_neigh1': _L2_gnn_in['W_neigh1'], 'L2_gnn_b1': _L2_gnn_in['b1'], 'L2_gnn_W_self2': _L2_gnn_in['W_self2'], 'L2_gnn_W_neigh2': _L2_gnn_in['W_neigh2'], 'L2_gnn_b2': _L2_gnn_in['b2'], 'L3_gnn_Wq': _L3_gnn_in['Wq'], 'L3_gnn_Wk': _L3_gnn_in['Wk'], 'L3_gnn_Wv': _L3_gnn_in['Wv'], 'L3_gnn_Wo': _L3_gnn_in['Wo'], 'L3_gnn_ln1_g': _L3_gnn_in['ln1_g'], 'L3_gnn_ln1_b': _L3_gnn_in['ln1_b'], 'L3_gnn_ln2_g': _L3_gnn_in['ln2_g'], 'L3_gnn_ln2_b': _L3_gnn_in['ln2_b'], 'L3_gnn_W1': _L3_gnn_in['W1'], 'L3_gnn_b1': _L3_gnn_in['b1'], 'L3_gnn_W2': _L3_gnn_in['W2'], 'L3_gnn_b2': _L3_gnn_in['b2']}

def reference(x, src, dst, edge_weight, L0_gnn_W_self, L0_gnn_b_self, L0_gnn_W_neigh, L0_gnn_gamma, L0_gnn_beta, L0_gnn_alpha, L1_gnn_weight, L1_gnn_bias, L2_gnn_W_self1, L2_gnn_W_neigh1, L2_gnn_b1, L2_gnn_W_self2, L2_gnn_W_neigh2, L2_gnn_b2, L3_gnn_Wq, L3_gnn_Wk, L3_gnn_Wv, L3_gnn_Wo, L3_gnn_ln1_g, L3_gnn_ln1_b, L3_gnn_ln2_g, L3_gnn_ln2_b, L3_gnn_W1, L3_gnn_b1, L3_gnn_W2, L3_gnn_b2):
    import jax
    import jax.numpy as jnp

    def _L0_gnn_ref(x, src, dst, W_self, b_self, W_neigh, gamma, beta, alpha):
        import jax, jax.numpy as jnp
        import numpy as np
        N = 3125
        E = 25000
        D_IN = 512
        D_OUT = 512
        LN_EPS = 1e-05
        deg = jax.ops.segment_sum(jnp.ones_like(src, dtype=x.dtype), dst, num_segments=N)
        inv_deg = 1.0 / jnp.maximum(deg, 1.0)
        agg = jax.ops.segment_sum(x[src], dst, num_segments=N)
        neigh = agg * inv_deg[:, None]
        h = x @ W_self + b_self + neigh @ W_neigh
        mu = jnp.mean(h, axis=-1, keepdims=True)
        var = jnp.mean(jnp.square(h - mu), axis=-1, keepdims=True)
        h = (h - mu) * jax.lax.rsqrt(var + LN_EPS) * gamma + beta
        h = jnp.where(h >= 0, h, alpha * h)
        return h + x

    def _L1_gnn_ref(x, weight, bias, row, col, edge_weight):
        import jax, jax.numpy as jnp
        import numpy as np
        N_NODES = 3125
        N_EDGES = 100000
        D_IN = 512
        D_OUT = 512
        support = x @ weight
        msgs = edge_weight[:, None] * support[col]
        out = jax.ops.segment_sum(msgs, row, num_segments=N_NODES)
        return out + bias

    def _L2_gnn_ref(feats, src, dst, W_self1, W_neigh1, b1, W_self2, W_neigh2, b2):
        import jax, jax.numpy as jnp
        import numpy as np
        N, E, D = (625, 10000, 512)

        def _sage_layer(h, src, dst, W_self, W_neigh, b, n_nodes):
            agg = jax.ops.segment_sum(h[src], dst, num_segments=n_nodes)
            deg = jax.ops.segment_sum(jnp.ones_like(dst, dtype=h.dtype), dst, num_segments=n_nodes)
            h_neigh = agg / jnp.maximum(deg, 1.0)[:, None]
            return jax.nn.relu(h @ W_self + h_neigh @ W_neigh + b)
        n_nodes = feats.shape[0]
        h = _sage_layer(feats, src, dst, W_self1, W_neigh1, b1, n_nodes)
        h = _sage_layer(h, src, dst, W_self2, W_neigh2, b2, n_nodes)
        return h

    def _L3_gnn_ref(h, src, dst, Wq, Wk, Wv, Wo, ln1_g, ln1_b, ln2_g, ln2_b, W1, b1, W2, b2):
        import jax, jax.numpy as jnp
        import numpy as np
        N, E, DM, H, DFF = (1250, 40000, 512, 8, 128)
        DK = DM // H

        def _layernorm(x, g, b, eps=1e-05):
            mu = jnp.mean(x, axis=-1, keepdims=True)
            var = jnp.mean(jnp.square(x - mu), axis=-1, keepdims=True)
            return (x - mu) * jax.lax.rsqrt(var + eps) * g + b
        n = h.shape[0]
        q = (h @ Wq).reshape(n, H, DK)
        k = (h @ Wk).reshape(n, H, DK)
        v = (h @ Wv).reshape(n, H, DK)
        e = jnp.einsum('ehd,ehd->eh', k[src], q[dst]) / np.sqrt(DK).astype(np.float32)
        m = jax.ops.segment_max(e, dst, num_segments=n)
        ex = jnp.exp(e - m[dst])
        z = jax.ops.segment_sum(ex, dst, num_segments=n)
        attn = ex / z[dst]
        a = jax.ops.segment_sum(attn[:, :, None] * v[src], dst, num_segments=n)
        a = a.reshape(n, DM)
        o = a @ Wo
        x = _layernorm(h + o, ln1_g, ln1_b)
        f = jax.nn.relu(x @ W1 + b1) @ W2 + b2
        return _layernorm(x + f, ln2_g, ln2_b)
    x = _layernorm(x + _L0_gnn_ref(x, src, dst, L0_gnn_W_self, L0_gnn_b_self, L0_gnn_W_neigh, L0_gnn_gamma, L0_gnn_beta, L0_gnn_alpha), axis=-1)
    x = _layernorm(x + _L1_gnn_ref(x, L1_gnn_weight, L1_gnn_bias, src, dst, edge_weight), axis=-1)
    x = _layernorm(x + _L2_gnn_ref(x, src, dst, L2_gnn_W_self1, L2_gnn_W_neigh1, L2_gnn_b1, L2_gnn_W_self2, L2_gnn_W_neigh2, L2_gnn_b2), axis=-1)
    x = _layernorm(x + _L3_gnn_ref(x, src, dst, L3_gnn_Wq, L3_gnn_Wk, L3_gnn_Wv, L3_gnn_Wo, L3_gnn_ln1_g, L3_gnn_ln1_b, L3_gnn_ln2_g, L3_gnn_ln2_b, L3_gnn_W1, L3_gnn_b1, L3_gnn_W2, L3_gnn_b2), axis=-1)
    return x

_drawn_inputs = setup_inputs


def setup_inputs(seed=0):
    import zlib

    import numpy as np

    out = dict(_drawn_inputs(seed))
    spreads = {'L0_gnn_gamma': (1.0, 0.2),
     'L0_gnn_beta': (0.0, 0.1),
     'L2_gnn_b1': (0.0, 0.1),
     'L2_gnn_b2': (0.0, 0.1),
     'L3_gnn_ln1_g': (1.0, 0.2),
     'L3_gnn_ln1_b': (0.0, 0.1),
     'L3_gnn_ln2_g': (1.0, 0.2),
     'L3_gnn_ln2_b': (0.0, 0.1),
     'L3_gnn_b1': (0.0, 0.8),
     'L3_gnn_b2': (0.0, 0.1)}
    factors = {'L1_gnn_bias': 3.159, 'L3_gnn_Wq': 8.0, 'L3_gnn_Wk': 8.0}
    for name, (base, spread) in spreads.items():
        noise = np.random.default_rng([zlib.crc32(name.encode()), seed]).standard_normal(out[name].shape)
        drawn = base * np.exp(spread * noise) if base else spread * noise
        out[name] = jnp.asarray(drawn.astype(out[name].dtype))
    for name, factor in factors.items():
        out[name] = (out[name] * factor).astype(out[name].dtype)
    return out
```

```python
from contextlib import ExitStack

import numpy as np
import concourse.bass as bass
from concourse import mybir

ALU = mybir.AluOpType
ACT = mybir.ActivationFunctionType
AX = mybir.AxisListType
F32 = mybir.dt.float32
I32 = mybir.dt.int32

P = 128
N = 3125
E = 50000
D = 512
KD = D // P
H = 8
DK = D // H
DFF = 128
NT = -(-N // P)
TILES = NT + 1
LAST = N - (NT - 1) * P
ROWS = TILES * P
GROUP = 16
GROUPS = -(-(E + NT * (P - 1)) // P // GROUP) + (1 if (E + NT * (P - 1)) // P % GROUP == 0 else 0)
CHUNKS = GROUPS * GROUP
HALVES = GROUPS // 2
NAT = -(-E // (P * 56)) * 56
SPARE = 2
PITCH = CHUNKS + SPARE
PARTS = NAT // 56
RING = 8
OH_RING = 4
EPS = 1e-5
FAR = 1e30
assert CHUNKS == 416 and TILES == GROUPS and GROUPS % 2 == 0 and NAT == 392


class Chain:

    def __init__(self, eng, sem):
        self.eng, self.sem, self.count, self.loop = eng, sem, 0, 0

    def then(self, ins):
        ins.then_inc(self.sem, 1)
        self.count += 1
        self.eng.wait_ge(self.sem, self.loop + self.count)

    def lag(self, ins):
        ins.then_inc(self.sem, 1)
        self.count += 1
        self.eng.wait_ge(self.sem, self.loop + self.count - 1)

    def settle(self):
        self.eng.wait_ge(self.sem, self.loop + self.count)

    def enter(self, i, steps):
        self.loop, self.steps, self.first = i * steps, steps, self.count

    def leave(self, times):
        assert self.count - self.first == self.steps, (self.count - self.first, self.steps)
        self.count = self.first + self.steps * times
        self.loop = 0


def regs(nc, eng, row, at, n, top):
    return nc.values_load_multi_w_load_instructions(
        row[0:1, bass.ds(at, n)], engines=(eng.engine,), min_val=0, max_val=top,
        skip_runtime_bounds_check_because="worked out on the chip within these bounds")[1]


def build(nc, x, edges, src_nat, dst_nat, w_nat, l0_ws, l0_bs, l0_wn, l0_g, l0_b, l0_alpha,
          l1_w, l1_b, l2_ws1, l2_wn1, l2_b1, l2_ws2, l2_wn2, l2_b2,
          wq, wk, wv, wo, ln1_g, ln1_b, ln2_g, ln2_b, w1, b1, w2, b2, out):
    with ExitStack() as ctx:
        def sb(name, shape, dt=F32):
            return ctx.enter_context(nc.sbuf_tensor(name, shape, dt))

        def sem(name):
            return ctx.enter_context(nc.semaphore(name))

        def dram(name, shape):
            return nc.dram_tensor(name, shape, F32, kind="Internal").ap()

        table = [dram(f"table{k}", [ROWS, D]) for k in range(5)]
        vtable = dram("vtable", [ROWS, D])
        by_src = dram("by_src", [P * PITCH, 4])
        nat_rec = dram("nat_rec", [P, NAT * 4])
        nat_pos = nc.dram_tensor("nat_pos", [P, NAT], I32, kind="Internal").ap()
        tile_s_dram = nc.dram_tensor("tile_s_dram", [P, CHUNKS], I32, kind="Internal").ap()

        X = sb("X", [P, TILES, D])
        ACC = sb("ACC", [P, TILES, D])
        R = sb("R", [P, TILES, D])
        G = sb("G", [P, RING, D])
        WA = sb("WA", [P, KD, D])
        WB = sb("WB", [P, KD, D])
        OHX = sb("OHX", [P, OH_RING + 2, P])
        iota = sb("iota", [P, P])
        ident = sb("ident", [P, P])
        VEC = sb("VEC", [P, 2, D])
        XT = sb("XT", [P, KD, P])
        XS = sb("XS", [P, D])
        rec = sb("rec", [P, CHUNKS, 2], I32)
        tile_d = sb("tile_d", [P, CHUNKS], I32)
        row2 = sb("row2", [P, CHUNKS], I32)
        stage_idx = sb("stage_idx", [P, 2, GROUP], I32)
        inv = sb("inv", [P, TILES])
        small = sb("small", [P, 48])
        chunk0_i = sb("chunk0_i", [P, 32], I32)
        alpha = small[:, 30:31]
        ones = small[:, 31:32]
        eps = small[:, 28:29]
        stat = [small[:, 0:12], small[:, 12:24]]
        recf = rec[:, :, :].bitcast(F32)

        accf = ACC[:, :, :].rearrange("p t d -> p (t d)")
        rf = R[:, :, :].rearrange("p t d -> p (t d)")
        count = rf[:, 13000:13032]
        XN = [G[:, 0, :], G[:, 1, :]]
        XTW = [G[:, 2 + i, :].rearrange("p (k n) -> p k n", k=KD) for i in range(2)]
        Y = [G[:, 4, :], G[:, 5, :]]
        T1 = [G[:, 6, :], XS[:, :]]
        T2 = [G[:, 7, :], XT[:, :, :].rearrange("p k n -> p (k n)")]
        OH = [OHX[:, i, :] for i in range(OH_RING)]
        OHT = [OHX[:, OH_RING + i, :] for i in range(2)]
        ohxf = OHX[:, :, :].rearrange("p a b -> p (a b)")
        st_rec = [ohxf[:, 280 * i:280 * i + 224].rearrange("p (c f) -> p c f", f=4) for i in range(2)]
        st_pos = [ohxf[:, 280 * i + 224:280 * i + 280].bitcast(I32) for i in range(2)]

        bank = [ctx.enter_context(nc.psum_tensor(f"bank{i}", [P, D], F32)) for i in range(8)]
        psA = bank[0:2]
        psR = [bank[0], bank[1], bank[4], bank[5]]
        psT, psS = bank[2], bank[3]
        psTP = bank[2:4]
        psY = bank[4:6]
        psD, psQ = bank[6], bank[7]

        s_const = sem("s_const")
        s_x = sem("s_x")
        s_nat = sem("s_nat")
        s_cnt = sem("s_cnt")
        s_tot = sem("s_tot")
        s_rows = sem("s_rows")
        s_prep = sem("s_prep")
        s_prep_out = sem("s_prep_out")
        s_rec = [sem("s_rec0"), sem("s_rec1")]
        s_scat_in = [sem("s_scat_in0"), sem("s_scat_in1")]
        s_scat = [sem("s_scat0"), sem("s_scat1")]
        s_srcrec = sem("s_srcrec")
        s_srcidx = sem("s_srcidx")
        s_w = {k: sem(f"w_{k}") for k in
               ("wn0", "ws0", "w1", "wn2a", "ws2a", "wn2b", "ws2b", "wk", "wq", "wv", "wo", "ffn")}
        s_v = {k: sem(f"v_{k}") for k in ("sum0", "norm0", "l1", "l2b", "last")}
        s_stage = sem("s_stage")
        g_landed = [sem(f"g_landed{i}") for i in range(RING)]
        g_free = sem("g_free")
        oh_ready = sem("oh_ready")
        acc_done = sem("acc_done")
        part_ready = sem("part_ready")
        part_copied = sem("part_copied")
        xs_ready = sem("xs_ready")
        tp_done = sem("tp_done")
        xt_ready = sem("xt_ready")
        self_done = sem("self_done")
        self_used = sem("self_used")
        xn_ready = sem("xn_ready")
        tp2_done = sem("tp2_done")
        xt2_ready = sem("xt2_ready")
        y_done = sem("y_done")
        y_copied = sem("y_copied")
        tab = [sem("tab0"), sem("tab1")]
        kept = sem("kept")
        var_ready = sem("var_ready")
        std_ready = sem("std_ready")
        dve_chain = sem("dve_chain")
        pool_chain = sem("pool_chain")
        d_done = sem("d_done")
        agg_done = sem("agg_done")
        v_staged = sem("v_staged")
        v_out = [sem("v_out0"), sem("v_out1")]
        a_tp = sem("a_tp")
        a_oht = sem("a_oht")
        a_q = sem("a_q")
        a_mul = sem("a_mul")
        s_tick, s_tick2 = sem("s_tick"), sem("s_tick2")
        m_in = sem("m_in")
        m_tp = sem("m_tp")
        m_cp = sem("m_cp")
        b_oh = sem("b_oh")
        b_mm = sem("b_mm")
        b_cp = sem("b_cp")
        p_oh = sem("p_oh")
        p_tp = sem("p_tp")
        p_oht = sem("p_oht")
        p_mm = sem("p_mm")
        p_sub = sem("p_sub")
        p_exp = sem("p_exp")
        c_mul = sem("c_mul")
        f_an = sem("f_an")
        f_tp = sem("f_tp")
        f_xt = sem("f_xt")
        f_mm = sem("f_mm")
        f_xp = sem("f_xp")
        f_f1 = sem("f_f1")
        f_relu = sem("f_relu")
        f_out = sem("f_out")
        s_out = sem("s_out")

        block = ctx.enter_context(nc.Block())

        SELF = {0: 0, 2: 1, 3: 2, 4: 3}

        def wrows(w):
            return w.rearrange("(k p) n -> p k n", p=P)

        def across(v):
            return v.rearrange("(a n) -> a n", a=1).broadcast_to([P, v.shape[0]])

        @block.sync
        def _(sp):
            sp.dma_start(rf[:, 0:NAT].bitcast(I32), dst_nat).then_inc(s_nat, 16)
            sp.dma_start(rf[:, NAT:2 * NAT].bitcast(I32), src_nat).then_inc(s_nat, 16)
            sp.dma_start(rf[:, 2 * NAT:3 * NAT], w_nat).then_inc(s_nat, 16)
            sp.dma_start(WA[:, :, :], wrows(l0_wn)).then_inc(s_w["wn0"], 16)
            sp.wait_ge(s_const, 1)
            for a in range(0, NT - 1, 4):
                sp.dma_start(X[:, a:a + 4, :],
                             x[a * P:(a + 4) * P, :].rearrange("(t p) d -> p t d", p=P)).then_inc(s_x, 16)
            sp.dma_start(X[0:LAST, NT - 1, :], x[(NT - 1) * P:N, :]).then_inc(s_x, 16)
            sp.dma_start(WB[:, :, :], wrows(l0_ws)).then_inc(s_w["ws0"], 16)
            sp.dma_start(VEC[:, 0, :], across(l0_bs)).then_inc(s_v["sum0"], 16)
            sp.dma_start(alpha, l0_alpha.broadcast_to([P, 1])).then_inc(s_v["sum0"], 16)

            sp.wait_ge(s_rows, 1)
            with sp.Fori(0, HALVES) as i:
                for half in range(2):
                    g = 2 * i + half
                    off = regs(nc, sp, row2, g * GROUP, GROUP, E)
                    for j in range(GROUP):
                        if j == 0:
                            sp.wait_ge(s_rec[half], i * 16 * GROUP)
                        sp.dma_start(rec[:, bass.ds(g * GROUP + j, 1), :],
                                     edges[bass.ds(off[j], P), :].unsqueeze(1)).then_inc(s_rec[half], 16)
            sp.wait_ge(s_prep, 1)
            sp.dma_start(by_src.rearrange("(p c) f -> p (c f)", p=P),
                         accf[:, 0:PITCH * 4]).then_inc(s_prep_out, 16)
            sp.dma_start(nat_rec, accf[:, PITCH * 4:PITCH * 4 + NAT * 4]).then_inc(s_prep_out, 16)
            sp.dma_start(nat_pos, accf[:, PITCH * 4 + NAT * 4:PITCH * 4 + NAT * 5].bitcast(I32))\
                .then_inc(s_prep_out, 16)
            sp.dma_start(tile_s_dram, accf[:, PITCH * 4 + NAT * 5:PITCH * 4 + NAT * 5 + CHUNKS].bitcast(I32))\
                .then_inc(s_prep_out, 16)
            sp.wait_ge(agg_done, 1)
            sp.dma_start(VEC[:, 0, :], across(l0_g)).then_inc(s_v["norm0"], 16)
            sp.dma_start(VEC[:, 1, :], across(l0_b)).then_inc(s_v["norm0"], 16)
            sp.dma_start(WA[:, :, :], wrows(l1_w)).then_inc(s_w["w1"], 16)
            sp.dma_start(row2[:, :], tile_s_dram).then_inc(s_srcrec, 16)
            for part in range(PARTS):
                h = part % 2
                if part >= 2:
                    sp.wait_ge(s_scat[h], 16 * 56 * (part // 2))
                sp.dma_start(st_rec[h], nat_rec[:, part * 224:(part + 1) * 224]
                             .rearrange("p (c f) -> p c f", f=4)).then_inc(s_scat_in[h], 16)
                sp.dma_start(st_pos[h], nat_pos[:, part * 56:(part + 1) * 56]).then_inc(s_scat_in[h], 16)
            for h in range(2):
                sp.wait_ge(s_scat[h], 16 * 56 * ((PARTS + 1 - h) // 2))
            sp.wait_ge(d_done, 1)
            sp.dma_start(rf[:, 0:CHUNKS * 4].rearrange("p (c f) -> p c f", f=4),
                         by_src.rearrange("(p c) f -> p c f", p=P)[:, 0:CHUNKS, :]).then_inc(s_srcrec, 16)
            sp.dma_start(VEC[:, 0, :], across(l1_b)).then_inc(s_v["l1"], 16)
            sp.dma_start(VEC[:, 1, :], across(l2_b1)).then_inc(s_v["l1"], 16)
            sp.wait_ge(y_done, 2 + 2 * TILES)
            sp.dma_start(WA[:, :, :], wrows(l2_wn1)).then_inc(s_w["wn2a"], 16)
            sp.dma_start(WB[:, :, :], wrows(l2_ws1)).then_inc(s_w["ws2a"], 16)
            sp.wait_ge(d_done, 2)
            sp.dma_start(VEC[:, 0, :], across(l2_b2)).then_inc(s_v["l2b"], 16)
            sp.wait_ge(y_done, 2 + 3 * TILES)
            sp.dma_start(WA[:, :, :], wrows(l2_wn2)).then_inc(s_w["wn2b"], 16)
            sp.wait_ge(self_done, 2 * TILES)
            sp.dma_start(WB[:, :, :], wrows(l2_ws2)).then_inc(s_w["ws2b"], 16)
            sp.wait_ge(y_done, 2 + 4 * TILES)
            sp.dma_start(WA[:, :, :], wrows(wk)).then_inc(s_w["wk"], 16)
            sp.wait_ge(self_done, 3 * TILES)
            sp.dma_start(WB[:, :, :], wrows(wq)).then_inc(s_w["wq"], 16)
            sp.wait_ge(y_done, 2 + 5 * TILES)
            sp.dma_start(WB[:, :, :], wrows(wv)).then_inc(s_w["wv"], 16)
            sp.dma_start(WA[:, :, :], wrows(wo)).then_inc(s_w["wo"], 16)
            with sp.Fori(0, HALVES) as i:
                for half in range(2):
                    t = 2 * i + half
                    sp.wait_ge(v_staged, t + 1)
                    sp.dma_start(vtable[bass.ds(t * P, P), :], VEC[:, half, :]).then_inc(v_out[half], 16)
            sp.wait_ge(self_done, 4 * TILES)
            sp.dma_start(WB[:, 0, :].rearrange("p (k n) -> p k n", k=KD), wrows(w1)).then_inc(s_w["ffn"], 16)
            sp.dma_start(WB[:, 1, :], w2).then_inc(s_w["ffn"], 16)
            sp.wait_ge(p_mm, 2 + CHUNKS)
            for n, v in enumerate((ln1_g, ln1_b, ln2_g, ln2_b, b2)):
                sp.dma_start(rf[:, 3328 + n * D:3328 + (n + 1) * D], across(v)).then_inc(s_v["last"], 16)
            sp.dma_start(small[:, 29:30], b1.rearrange("(n a) -> n a", a=1)).then_inc(s_v["last"], 16)
            with sp.Fori(0, NT - 1) as t:
                sp.wait_ge(f_out, t + 1)
                sp.dma_start(out[bass.ds(t * P, P), :].unsqueeze(1), X[:, bass.ds(t, 1), :]).then_inc(s_out, 16)
            sp.wait_ge(f_out, NT)
            sp.dma_start(out[(NT - 1) * P:N, :], X[0:LAST, NT - 1, :]).then_inc(s_out, 16)
            sp.wait_ge(s_out, 16 * NT)

        @block.gpsimd
        def _(pool):
            chain = Chain(pool, pool_chain)
            pool.memset(X[:, NT - 1:TILES, :], 0.0).then_inc(s_const, 1)
            chain.then(pool.memset(ident[:, :], 0.0))
            pool.affine_select(out=ident[:, :], in_=ident[:, :], compare_op=ALU.not_equal, fill=1.0,
                               base=0, pattern=[[-1, P]], channel_multiplier=1).then_inc(s_const, 1)
            pool.iota(iota[:, :], pattern=[[1, P]], base=0, channel_multiplier=0,
                      allow_small_or_imprecise_dtypes=True).then_inc(s_const, 1)
            pool.memset(eps, EPS)
            pool.memset(ones, 1.0).then_inc(s_const, 1)
            pool.memset(OHX[:, 0, :], 1.0).then_inc(s_const, 1)
            chain.then(pool.memset(OHX[:, 1, :], 0.0))
            pool.affine_select(out=OHX[:, 1, :], in_=OHX[:, 1, :], compare_op=ALU.is_ge, fill=1.0,
                               base=0, pattern=[[-1, P]], channel_multiplier=1).then_inc(s_const, 1)

            def gathers(q, rows, idx, ready):
                base = q * CHUNKS
                with pool.Fori(0, HALVES) as i:
                    for half in range(2):
                        g = 2 * i + half
                        if q == 0:
                            pool.wait_ge(s_rec[half], (i + 1) * 16 * GROUP)
                        pool.tensor_copy(stage_idx[:, half, :], idx(g)).then_inc(s_stage, 1)
                        pool.wait_ge(s_stage, q * GROUPS + g + 1)
                        for j in range(GROUP):
                            pool.wait_ge(g_free, base + g * GROUP + j + 1)
                            pool.sem_inc(s_tick, 1)
                            pool.indirect_dma_start(
                                out=G[:, j % RING, :], out_offset=None, in_=rows,
                                in_offset=bass.IndirectOffsetOnAxis(ap=stage_idx[:, half, j:j + 1], axis=0))\
                                .then_inc(g_landed[j % RING], 16)

            def table_ready(m):
                for half in range(2):
                    pool.wait_ge(tab[half], 16 * HALVES * (m + 1))
                if m:
                    pool.wait_ge(d_done, m)

            def by_dst(g):
                return rec[:, bass.ds(g * GROUP, GROUP), 0]

            table_ready(0)
            gathers(0, table[0], by_dst, None)
            pool.wait_ge(s_prep_out, 64)
            for part in range(PARTS):
                h = part % 2
                pool.wait_ge(s_scat_in[h], 32 * (part // 2 + 1))
                for c in range(56):
                    pool.indirect_dma_start(
                        out=by_src, out_offset=bass.IndirectOffsetOnAxis(ap=st_pos[h][:, c:c + 1], axis=0),
                        in_=st_rec[h][:, c, :], in_offset=None).then_inc(s_scat[h], 16)
            idx_s = rf[:, CHUNKS * 4:CHUNKS * 5].bitcast(I32)
            table_ready(1)
            pool.wait_ge(s_srcidx, 1)
            gathers(1, table[1], lambda g: idx_s[:, bass.ds(g * GROUP, GROUP)], None)
            table_ready(2)
            gathers(2, table[2], by_dst, None)
            table_ready(3)
            gathers(3, table[3], by_dst, None)
            table_ready(4)
            gathers(4, table[4], by_dst, None)
            for half in range(2):
                pool.wait_ge(v_out[half], 16 * HALVES)
            gathers(5, vtable, by_dst, None)

        @block.scalar
        def _(act):
            def roots(m, lns, i):
                for n in range(lns):
                    for h in range(2):
                        act.wait_ge(var_ready, LN_AT[m] + i * 2 * lns + 2 * n + h + 1)
                        act.activation(stat[h][:, 8:9], stat[h][:, 7:8], ACT.Sqrt, bias=eps).then_inc(std_ready, 1)

            def turned(m, i):
                for h in range(2):
                    tc = m * TILES + 2 * i + h
                    act.wait_ge(tp2_done, tc + 1)
                    act.wait_ge(y_done, tc + 1)
                    act.activation(XTW[h].rearrange("p k n -> p (k n)"), psTP[h][:, :], ACT.Copy)\
                        .then_inc(xt2_ready, 1)

            def products(m, i, queries):
                for h in range(2):
                    t = 2 * i + h
                    act.wait_ge(y_done, 2 + m * TILES + t + 1)
                    act.wait_ge(tab[h], (m * HALVES + i) * 16)
                    if queries:
                        act.activation(R[:, bass.ds(t, 1), :], psA[h][:, :].unsqueeze(1), ACT.Copy,
                                       scale=float(DK) ** -0.5)
                    act.activation(Y[h], psY[h][:, :], ACT.Copy).then_inc(y_copied, 1)
                for h in range(2):
                    t = 2 * i + h
                    act.wait_ge(y_copied, 2 + m * TILES + t + 1)
                    act.dma_start(table[m][bass.ds(t * P, P), :], Y[h]).then_inc(tab[h], 16)

            def dense(m, lns, keep=None, queries=False):
                def step(i, before):
                    if m == 0:
                        for h in range(2):
                            tc = 2 * i + h
                            act.wait_ge(xt2_ready, tc + 1)
                            act.activation(XN[h].unsqueeze(1), X[:, bass.ds(tc, 1), :], ACT.Copy)\
                                .then_inc(xn_ready, 1)
                    roots(m, lns, i)
                    turned(m, i)
                    if before is not None:
                        products(m, before, queries)
                    if keep is not None:
                        for h in range(2):
                            act.wait_ge(xn_ready, m * TILES + 2 * i + h + 1)
                            act.activation(keep[:, bass.ds(2 * i + h, 1), :], XN[h].unsqueeze(1), ACT.Copy)\
                                .then_inc(kept, 1)

                if m == 0:
                    act.wait_ge(s_x, 16 * 7)
                step(0, None)
                with act.Fori(1, HALVES) as i:
                    step(i, i - 1)
                products(m, HALVES - 1, queries)

            def beside(q, source, values=False):
                k = SELF[q]
                with act.Fori(0, HALVES) as i:
                    for half in range(2):
                        t = 2 * i + half
                        s = k * TILES + t
                        act.wait_ge(tp_done, s)
                        act.activation(XS[:, :].unsqueeze(1), source[:, bass.ds(t, 1), :], ACT.Copy)\
                            .then_inc(xs_ready, 1)
                        if q == 4:
                            scores(i, half, range(0, 8))
                        if q == 0:
                            parts(t, 0)
                        act.wait_ge(tp_done, s + 1)
                        act.wait_ge(self_done, s)
                        act.activation(XT[:, :, :].rearrange("p k n -> p (k n)"), psT[:, :], ACT.Copy)\
                            .then_inc(xt_ready, 1)
                        if q == 4:
                            scores(i, half, range(8, GROUP))
                            act.wait_ge(self_done, s + 1)
                            act.wait_ge(v_out[half], i * 16)
                            act.activation(VEC[:, half, :], psS[:, :], ACT.Copy).then_inc(v_staged, 1)
                        if q == 0:
                            parts(t, 1)

            def parts(g, b):
                act.wait_ge(part_ready, 2 * g + b + 1)
                act.activation(VEC[:, 1, bass.ds(g * GROUP + 8 * b, 8)], bank[6 + b][:, 0:8], ACT.Copy)\
                    .then_inc(part_copied, 1)

            def scores(i, half, chunks):
                for j in chunks:
                    a = (2 * i + half) * GROUP + j
                    act.wait_ge(a_tp, OH_RING + a + 1)
                    act.wait_ge(a_q, a + 1)
                    act.activation(OHT[j % 2], psY[j % 2][:, 0:P], ACT.Copy).then_inc(a_oht, 1)

            LN_AT = [0, 0, 2 * TILES, 3 * TILES, 3 * TILES]
            dense(0, 0)
            beside(0, X)
            dense(1, 2, keep=X)
            dense(2, 1, keep=X)
            beside(2, X)
            dense(3, 0, keep=R)
            beside(3, R)
            dense(4, 1, keep=X, queries=True)
            beside(4, X)

            kt, et = rf[:, 6656:9984], rf[:, 3328:6656]
            batches = [(a, min(4, GROUPS - a)) for a in range(0, GROUPS, 4)]
            n = 0
            for dst in (kt, et):
                for a, m in batches:
                    act.wait_ge(m_tp, n + 1)
                    act.activation(dst[:, a * P:(a + m) * P], bank[n % 2][:, 0:m * P], ACT.Copy).then_inc(m_cp, 1)
                    n += 1
            em9 = accf[:, 6656:6656 + CHUNKS * 9].rearrange("p (c f) -> p c f", f=9)
            last = accf[:, 10400:10400 + CHUNKS]
            for what in range(2):
                for a, m in batches:
                    act.wait_ge(m_tp, n + 1)
                    src = bank[n % 2][:, 0:m * P].rearrange("p (c h) -> p c h", h=H)
                    if what == 0:
                        dst = last[:, a * GROUP:(a + m) * GROUP].unsqueeze(2)
                        act.activation(dst, src[:, :, 0:1], ACT.Copy).then_inc(m_cp, 1)
                    else:
                        act.activation(em9[:, a * GROUP:(a + m) * GROUP, 0:H], src, ACT.Copy).then_inc(m_cp, 1)
                    n += 1
            mb9 = accf[:, 0:CHUNKS * 9].rearrange("p (c f) -> p c f", f=9)
            with act.Fori(0, HALVES) as i:
                for half in range(2):
                    g = 2 * i + half
                    act.wait_ge(b_mm, OH_RING + (g + 1) * GROUP)
                    act.activation(mb9[:, bass.ds(g * GROUP, GROUP), :],
                                   psY[half][:, 0:GROUP * 9].rearrange("p (c f) -> p c f", f=9), ACT.Copy)\
                        .then_inc(b_cp, 1)
            ep = rf[:, 0:CHUNKS * H]
            with act.Fori(0, HALVES) as i:
                for half in range(2):
                    g = 2 * i + half
                    for j in range(GROUP):
                        c = g * GROUP + j
                        act.wait_ge(p_tp, OH_RING + c + 1)
                        act.wait_ge(p_mm, c + 1)
                        act.activation(OHT[j % 2], psA[j % 2][:, 0:P], ACT.Copy).then_inc(p_oht, 1)
                    act.wait_ge(p_sub, 2 + g + 1)
                    part = ep[:, bass.ds(g * GROUP * H, GROUP * H)]
                    act.activation(part, part, ACT.Exp).then_inc(p_exp, 1)

            with act.Fori(0, NT) as t:
                act.wait_ge(f_tp, 2 * t + 1)
                act.activation(XTW[0].rearrange("p k n -> p (k n)"), psT[:, :], ACT.Copy).then_inc(f_xt, 1)
                act.wait_ge(var_ready, 4 * TILES + 3 * t + 1)
                act.activation(stat[0][:, 8:9], stat[0][:, 7:8], ACT.Sqrt, bias=eps).then_inc(std_ready, 1)
                act.wait_ge(f_tp, 2 * t + 2)
                act.activation(XTW[1].rearrange("p k n -> p (k n)"), psT[:, :], ACT.Copy).then_inc(f_xt, 1)
                act.wait_ge(f_f1, t + 1)
                act.activation(OHX[:, 0, :], psD[:, 0:P], ACT.Relu, bias=small[:, 29:30]).then_inc(f_relu, 1)
                for n in range(2):
                    act.wait_ge(var_ready, 4 * TILES + 3 * t + 2 + n)
                    act.activation(stat[0][:, 8:9], stat[0][:, 7:8], ACT.Sqrt, bias=eps).then_inc(std_ready, 1)

        @block.tensor
        def _(pe):
            pe.sem_inc(g_free, RING)
            pe.sem_inc(y_done, 2)
            pe.sem_inc(a_q, 2)
            pe.sem_inc(a_tp, OH_RING)
            pe.sem_inc(b_mm, OH_RING)
            pe.sem_inc(p_tp, OH_RING)
            pe.sem_inc(p_mm, 2)
            pe.sem_inc(xt2_ready, 2)
            pe.sem_inc(y_copied, 2)
            pe.sem_inc(acc_done, 4)
            pe.sem_inc(a_oht, 2)
            pe.sem_inc(a_mul, 2)
            pe.sem_inc(b_cp, 2)
            pe.sem_inc(p_oht, 2)
            pe.sem_inc(p_sub, 2)
            pe.wait_ge(s_const, 6)

            def dense(m, *weights, queries=False):
                for w in weights:
                    pe.wait_ge(s_w[w], 16)
                with pe.Fori(0, HALVES) as i:
                    for h in range(2):
                        tc = m * TILES + 2 * i + h
                        pe.wait_ge(xn_ready, tc + 1)
                        pe.wait_ge(xt2_ready, tc + 1)
                        for k in range(KD):
                            last = pe.transpose(psTP[h][:, k * P:(k + 1) * P],
                                                XN[h][:, k * P:(k + 1) * P], ident[:, :])
                        last.then_inc(tp2_done, 1)
                    for h in range(2):
                        tc = m * TILES + 2 * i + h
                        pe.wait_ge(xt2_ready, 2 + tc + 1)
                        pe.wait_ge(y_copied, tc + 1)
                        if queries:
                            for k in range(KD):
                                pe.matmul(psA[h][:, :], XTW[h][:, k, :], WB[:, k, :],
                                          start=(k == 0), stop=(k == KD - 1))
                        for k in range(KD):
                            last = pe.matmul(psY[h][:, :], XTW[h][:, k, :], WA[:, k, :],
                                             start=(k == 0), stop=(k == KD - 1))
                        last.then_inc(y_done, 1)

            def beside_turn(s):
                pe.wait_ge(xs_ready, s + 1)
                pe.wait_ge(xt_ready, s)
                for k in range(KD):
                    last = pe.transpose(psT[:, k * P:(k + 1) * P], XS[:, k * P:(k + 1) * P], ident[:, :])
                last.then_inc(tp_done, 1)

            def beside_product(s):
                pe.wait_ge(xt_ready, s + 1)
                pe.wait_ge(self_used, s)
                for k in range(KD):
                    last = pe.matmul(psS[:, :], XT[:, k, :], WB[:, k, :], start=(k == 0), stop=(k == KD - 1))
                last.then_inc(self_done, 1)

            def sums(q, weights=None):
                if weights:
                    pe.wait_ge(s_w[weights], 16)
                with pe.Fori(0, HALVES) as i:
                    for half in range(2):
                        g = 2 * i + half
                        for j in range(GROUP):
                            c = g * GROUP + j
                            n = q * CHUNKS + c
                            pe.wait_ge(oh_ready, n + 1 - (CHUNKS if q == 5 else 0))
                            pe.wait_ge(acc_done, n + 1 - (CHUNKS if q == 5 else 0))
                            if q == 0:
                                if j % 8 == 0:
                                    pe.wait_ge(part_copied, 2 * g + j // 8 - 1 if j else 2 * g)
                                mm = pe.matmul(bank[6 + j // 8][:, j % 8:j % 8 + 1], OH[j % OH_RING], ones,
                                               start=True, stop=True)
                                if j % 8 == 7:
                                    mm.then_inc(part_ready, 1)
                            if q == 5:
                                pe.wait_ge(acc_done, n + 3 - CHUNKS)
                                pe.wait_ge(c_mul, c + 1)
                                pe.matmul(bank[6 + j % 2][:, 0:H], OH[j % OH_RING],
                                          rf[:, bass.ds(c * H, H)], start=True, stop=True)
                            else:
                                pe.wait_ge(g_landed[j % RING],
                                           16 * (q * CHUNKS // RING + g * (GROUP // RING) + j // RING + 1))
                            pe.matmul(psR[j % 4][:, :], OH[j % OH_RING], G[:, j % RING, :],
                                      start=True, stop=True).then_inc(g_free, 1)
                            if q in SELF and j == 3:
                                beside_turn(SELF[q] * TILES + g)
                            if q in SELF and j == 11:
                                beside_product(SELF[q] * TILES + g)

            pe.wait_ge(s_cnt, 1)
            pe.matmul(psD[:, 0:NT], OHX[:, 0, :], count[:, 0:NT], start=True, stop=True).then_inc(s_tot, 1)
            dense(0, "wn0")
            pe.wait_ge(s_cnt, 2)
            pe.matmul(psD[:, 0:NT], OHX[:, 0, :], count[:, 0:NT], start=True, stop=True)
            pe.matmul(psD[:, 32:32 + NT], OHX[:, 1, :], count[:, 0:NT], start=True, stop=True).then_inc(s_tot, 1)
            sums(0, "ws0")
            dense(1, "w1")
            sums(1)
            dense(2, "wn2a")
            sums(2, "ws2a")
            dense(3, "wn2b")
            sums(3, "ws2b")
            dense(4, "wk", "wq", queries=True)
            pe.wait_ge(s_w["wv"], 16)
            with pe.Fori(0, HALVES) as i:
                for half in range(2):
                    g = 2 * i + half
                    tiles = regs(nc, pe, tile_d, g * GROUP, GROUP, TILES - 1)

                    def turn(j):
                        a = g * GROUP + j
                        pe.wait_ge(oh_ready, 4 * CHUNKS + a + 1)
                        pe.wait_ge(a_oht, a + 1)
                        pe.transpose(psY[j % 2][:, 0:P], OH[j % OH_RING], ident[:, :]).then_inc(a_tp, 1)

                    turn(0)
                    for j in range(GROUP):
                        a = g * GROUP + j
                        if j + 1 < GROUP:
                            turn(j + 1)
                        pe.wait_ge(a_oht, 2 + a + 1)
                        pe.wait_ge(a_mul, a + 1)
                        pe.matmul(psA[j % 2][:, :].unsqueeze(1), OHT[j % 2], R[:, bass.ds(tiles[j], 1), :],
                                  start=True, stop=True).then_inc(a_q, 1)
                        if j == 3:
                            beside_turn(3 * TILES + g)
                        if j == 11:
                            pe.wait_ge(v_staged, g)
                            pe.wait_ge(xt_ready, 3 * TILES + g + 1)
                            for k in range(KD):
                                mm = pe.matmul(psS[:, :], XT[:, k, :], WB[:, k, :],
                                               start=(k == 0), stop=(k == KD - 1))
                            mm.then_inc(self_done, 1)

            batches = [(a, min(4, GROUPS - a)) for a in range(0, GROUPS, 4)]
            key8, ep = accf[:, 3328:6656], rf[:, 0:3328]
            run = rf[:, 6656:9984]
            n = 0
            for step, src in enumerate((key8, ep, key8, run)):
                pe.wait_ge(m_in, (1, 2, 3, 4)[step])
                for a, m in batches:
                    if n >= 2:
                        pe.wait_ge(m_cp, n - 1)
                    for b in range(m):
                        last = pe.transpose(bank[n % 2][:, b * P:(b + 1) * P],
                                            src[:, (a + b) * P:(a + b + 1) * P], ident[:, :])
                    last.then_inc(m_tp, 1)
                    n += 1
            em9 = accf[:, 6656:6656 + CHUNKS * 9]
            pe.wait_ge(m_cp, 4 * len(batches))
            with pe.Fori(0, HALVES) as i:
                for half in range(2):
                    g = 2 * i + half
                    for j in range(GROUP):
                        c = g * GROUP + j
                        pe.wait_ge(b_oh, c + 1)
                        if j == 0:
                            pe.wait_ge(b_cp, g + 1)
                        pe.matmul(psY[half][:, j * 9:(j + 1) * 9], OH[j % OH_RING], em9[:, bass.ds(c * 9, 9)],
                                  start=True, stop=True).then_inc(b_mm, 1)
            mx = rf[:, 3328:6656]
            pe.wait_ge(m_in, 5)
            with pe.Fori(0, HALVES) as i:
                for half in range(2):
                    g = 2 * i + half
                    for j in range(GROUP):
                        c = g * GROUP + j
                        pe.wait_ge(p_oh, c + 1)
                        pe.wait_ge(p_oht, c + 1)
                        pe.transpose(psA[j % 2][:, 0:P], OH[j % OH_RING], ident[:, :]).then_inc(p_tp, 1)
                        pe.wait_ge(p_oht, 2 + c + 1)
                        if j == 0:
                            pe.wait_ge(p_sub, g + 1)
                        pe.matmul(psY[half][:, j * H:(j + 1) * H], OHT[j % 2], mx[:, bass.ds(c * H, H)],
                                  start=True, stop=True).then_inc(p_mm, 1)
            pe.wait_ge(p_exp, GROUPS)
            sums(5)
            pe.wait_ge(s_w["wo"], 16)
            pe.wait_ge(s_w["ffn"], 32)
            with pe.Fori(0, NT) as t:
                pe.wait_ge(f_an, t + 1)
                for k in range(KD):
                    last = pe.transpose(psT[:, k * P:(k + 1) * P], XN[0][:, k * P:(k + 1) * P], ident[:, :])
                last.then_inc(f_tp, 1)
                pe.wait_ge(f_xt, 2 * t + 1)
                for k in range(KD):
                    last = pe.matmul(psY[0][:, :], XTW[0][:, k, :], WA[:, k, :], start=(k == 0), stop=(k == KD - 1))
                last.then_inc(f_mm, 1)
                pe.wait_ge(f_xp, t + 1)
                for k in range(KD):
                    last = pe.transpose(psT[:, k * P:(k + 1) * P], XN[1][:, k * P:(k + 1) * P], ident[:, :])
                last.then_inc(f_tp, 1)
                pe.wait_ge(f_xt, 2 * t + 2)
                for k in range(KD):
                    last = pe.matmul(psD[:, 0:P], WB[:, 0, k * P:(k + 1) * P], XTW[1][:, k, :],
                                     start=(k == 0), stop=(k == KD - 1))
                last.then_inc(f_f1, 1)
                pe.wait_ge(f_relu, t + 1)
                pe.matmul(psY[1][:, :], OHX[:, 0, :], WB[:, 1, :], start=True, stop=True).then_inc(f_mm, 1)

        @block.vector
        def _(dve):
            chain = Chain(dve, dve_chain)
            then = chain.then
            lns = [0]

            dst_i, src_i = rf[:, 0:NAT].bitcast(I32), rf[:, NAT:2 * NAT].bitcast(I32)
            w_f = rf[:, 2 * NAT:3 * NAT]
            tmp_at = [3 * NAT]

            def tmp(n):
                tmp_at[0] += n
                assert tmp_at[0] <= 13000
                return rf[:, tmp_at[0] - n:tmp_at[0]]

            dst_f, lo_f, hi_f, pos = (tmp(NAT) for _ in range(4))
            lo_i, hi_i, pos_lo, pos_hi = (tmp(NAT).bitcast(I32) for _ in range(4))
            zeros = tmp(NAT)
            mask = tmp(NAT)
            cidx = tmp(CHUNKS)
            tile_f, off_f, hop = tmp(CHUNKS), tmp(CHUNKS), tmp(CHUNKS)
            start, cnt, full_f, chunk0, first, step_ = (tmp(32) for _ in range(6))
            full_i = tmp(32).bitcast(I32)
            place = tmp(32)
            t128 = VEC[:, 1, 0:CHUNKS]
            pre = accf[:, 0:NT * NAT].rearrange("p (t c) -> p t c", t=NT)

            def chunks_of():
                then(dve.tensor_scalar(full_f[:, 0:NT], cnt[:, 0:NT], float(P - 1), None, ALU.add))
                then(dve.tensor_copy(full_i[:, 0:NT], full_f[:, 0:NT]))
                then(dve.tensor_scalar(full_i[:, 0:NT], full_i[:, 0:NT], 7, None, ALU.logical_shift_right))
                then(dve.tensor_copy(full_f[:, 0:NT], full_i[:, 0:NT]))
                then(dve.tensor_tensor_scan(chunk0[:, 1:NT + 1], full_f[:, 0:NT], zeros[:, 0:NT], 0.0,
                                            ALU.add, ALU.add))

            then(dve.memset(zeros, 0.0))
            then(dve.memset(chunk0[:, 0:1], 0.0))
            then(dve.memset(start[:, 0:1], 0.0))
            dve.wait_ge(s_const, 6)
            for a in range(0, CHUNKS, P):
                m = min(P, CHUNKS - a)
                dve.tensor_scalar(cidx[:, a:a + m], iota[:, 0:m], float(a), None, ALU.add)
            dve.wait_ge(s_nat, 48)
            then(dve.tensor_copy(dst_f, dst_i))
            for t in range(NT):
                last = dve.tensor_scalar(pre[:, t, :], dst_f, float(P * (t + 1)), None, ALU.is_lt)
            then(last)
            dve.tensor_reduce(count[:, 0:NT], pre, AX.X, ALU.add).then_inc(s_cnt, 1)
            dve.wait_ge(s_tot, 1)
            then(dve.tensor_copy(start[:, 1:NT + 1], psD[:, 0:NT]))
            then(dve.tensor_tensor(cnt[:, 0:NT], start[:, 1:NT + 1], start[:, 0:NT], ALU.subtract))
            chunks_of()
            then(dve.scalar_tensor_tensor(first[:, 0:NT + 1], chunk0[:, 0:NT + 1], -float(P),
                                          start[:, 0:NT + 1], ALU.mult, ALU.add))
            then(dve.tensor_tensor(step_[:, 0:NT], first[:, 1:NT + 1], first[:, 0:NT], ALU.subtract))
            dve.tensor_scalar(off_f, cidx, float(P), None, ALU.mult)
            then(dve.memset(tile_f, 0.0))
            for t in range(NT):
                dve.tensor_scalar(hop, cidx, chunk0[:, t + 1:t + 2], step_[:, t:t + 1], ALU.is_ge, ALU.mult)
                then(dve.scalar_tensor_tensor(tile_f, cidx, chunk0[:, t + 1:t + 2], tile_f, ALU.is_ge, ALU.add))
                then(dve.tensor_tensor(off_f, off_f, hop, ALU.add))
            then(dve.tensor_scalar(off_f, off_f, float(E), None, ALU.min))
            dve.tensor_copy(tile_d[:, :], tile_f)
            dve.tensor_scalar(t128, tile_f, float(P), None, ALU.mult)
            then(dve.tensor_copy(row2[:, :], off_f))
            dve.sem_inc(s_rows, 1)
            then(dve.tensor_scalar(full_f[:, 0:TILES], chunk0[:, 0:TILES], float(CHUNKS - 1), None, ALU.min))
            then(dve.tensor_copy(chunk0_i[:, 0:TILES], full_f[:, 0:TILES]))

            dve.tensor_scalar(hi_i, src_i, 7, None, ALU.logical_shift_right)
            then(dve.tensor_scalar(lo_i, src_i, P - 1, None, ALU.bitwise_and))
            dve.tensor_copy(hi_f, hi_i)
            then(dve.tensor_copy(lo_f, lo_i))
            for b in range(NT):
                then(dve.tensor_scalar(mask, hi_f, float(b), None, ALU.is_equal))
                then(dve.tensor_tensor_scan(pre[:, b, :], mask, zeros, 0.0, ALU.add, ALU.add))
            dve.tensor_copy(count[:, 0:NT].unsqueeze(2), pre[:, :, NAT - 1:NAT]).then_inc(s_cnt, 1)
            dve.wait_ge(s_tot, 2)
            dve.tensor_copy(cnt[:, 0:NT], psD[:, 0:NT])
            then(dve.tensor_copy(place[:, 0:NT], psD[:, 32:32 + NT]))
            chunks_of()
            then(dve.scalar_tensor_tensor(place[:, 0:NT], chunk0[:, 0:NT], float(P), place[:, 0:NT],
                                          ALU.mult, ALU.add))
            then(dve.tensor_scalar(place[:, 0:NT], place[:, 0:NT], -1.0, None, ALU.add))
            then(dve.memset(tile_f, 0.0))
            for t in range(NT):
                then(dve.scalar_tensor_tensor(tile_f, cidx, chunk0[:, t + 1:t + 2], tile_f, ALU.is_ge, ALU.add))
            then(dve.tensor_tensor(pre, pre, place[:, 0:NT].unsqueeze(2).broadcast_to([P, NT, NAT]), ALU.add))
            for b in range(NT):
                last = dve.scalar_tensor_tensor(pre[:, b, :], hi_f, float(b), pre[:, b, :], ALU.is_equal, ALU.mult)
            then(last)
            then(dve.tensor_reduce(pos, pre.rearrange("p t c -> p c t"), AX.X, ALU.add))
            pads = P * NAT - E
            then(dve.tensor_scalar(mask, cidx[:, 0:NAT], float(CHUNKS * P - (NAT - pads)), None, ALU.add))
            then(dve.scalar_tensor_tensor(mask, hi_f, float(NT), mask, ALU.is_equal, ALU.mult))
            then(dve.tensor_tensor(pos, pos, mask, ALU.add))
            then(dve.tensor_copy(lo_i, pos))
            dve.tensor_scalar(pos_lo, lo_i, P - 1, None, ALU.bitwise_and)
            then(dve.tensor_scalar(pos_hi, lo_i, 7, None, ALU.logical_shift_right))
            dve.tensor_copy(mask, pos_lo)
            then(dve.tensor_copy(pos, pos_hi))
            then(dve.scalar_tensor_tensor(pos, mask, float(PITCH), pos, ALU.mult, ALU.add))
            blank = accf[:, 0:PITCH * 4].rearrange("p (c f) -> p c f", f=4)
            nrec = accf[:, PITCH * 4:PITCH * 4 + NAT * 4].rearrange("p (c f) -> p c f", f=4)
            then(dve.memset(blank, 0.0))
            dve.memset(blank[:, :, 0:1], -1.0)
            dve.memset(blank[:, :, 1:2], float(NT * P))
            dve.tensor_copy(nrec[:, :, 0:1], lo_f.unsqueeze(2))
            dve.tensor_copy(nrec[:, :, 1:2], dst_f.unsqueeze(2))
            dve.tensor_copy(nrec[:, :, 2:3], w_f.unsqueeze(2))
            dve.memset(nrec[:, :, 3:4], 0.0)
            dve.tensor_copy(accf[:, PITCH * 4 + NAT * 4:PITCH * 4 + NAT * 5].bitcast(I32), pos)
            then(dve.tensor_copy(accf[:, PITCH * 4 + NAT * 5:PITCH * 4 + NAT * 5 + CHUNKS].bitcast(I32), tile_f))
            dve.sem_inc(s_prep, 1)
            dve.wait_ge(s_prep_out, 64)

            def onehot(q, g, j, key, weight=None):
                n = q * CHUNKS + g * GROUP + j
                c = g * GROUP + j
                if q == 4:
                    dve.wait_ge(a_tp, c + 1)
                elif j >= 0:
                    dve.wait_ge(g_free, RING - OH_RING + n + 1)
                args = (key(c), weight(c), ALU.is_equal, ALU.mult) if weight else (key(c), None, ALU.is_equal)
                dve.tensor_scalar(OH[j % OH_RING], iota[:, :], *args).then_inc(oh_ready, 1)

            def sums(q, key, weight=None, bias=None, row=None):
                past = CHUNKS if q == 5 else 0
                then(dve.memset(accf, 0.0))
                if q == 5:
                    then(dve.memset(zsum, 0.0))
                steps = (1 if q == 0 else 0)
                with dve.Fori(0, HALVES) as i:
                    chain.enter(i, 2 * steps)
                    for half in range(2):
                        g = 2 * i + half
                        tiles = regs(nc, dve, row, g * GROUP, GROUP, TILES - 1)
                        if q == 0:
                            dve.wait_ge(s_rec[half], (i + 1) * 16 * GROUP)
                            at = bass.ds(g * GROUP, GROUP)
                            then(dve.tensor_tensor(recf[:, at, 1], rec[:, at, 1], t128[:, at], ALU.subtract))
                        def weighted(j):
                            c = g * GROUP + j
                            dve.wait_ge(g_landed[j % RING],
                                        16 * (q * CHUNKS // RING + g * (GROUP // RING) + j // RING + 1))
                            slot = G[:, j % RING, :].rearrange("p (h k) -> p h k", h=H)
                            dve.tensor_tensor(slot, slot, rf[:, bass.ds(c * H, H)].unsqueeze(2)
                                              .broadcast_to([P, H, DK]), ALU.mult).then_inc(c_mul, 1)

                        for j in range(3):
                            onehot(q, g, j, key, weight)
                        if q == 5:
                            weighted(0)
                        for j in range(GROUP):
                            n = q * CHUNKS + g * GROUP + j
                            if j + 3 < GROUP:
                                onehot(q, g, j + 3, key, weight)
                            if q == 5 and j + 1 < GROUP:
                                weighted(j + 1)
                            dve.wait_ge(g_free, RING + n + 1)
                            dve.wait_ge(acc_done, 4 + n - past)
                            if q == 5:
                                slot = zsum[:, bass.ds(tiles[j], 1), :]
                                dve.tensor_tensor(slot, slot, bank[6 + j % 2][:, 0:H].unsqueeze(1),
                                                  ALU.add)
                            slot = ACC[:, bass.ds(tiles[j], 1), :]
                            dve.tensor_tensor(slot, slot, psR[j % 4][:, :].unsqueeze(1), ALU.add)\
                                .then_inc(acc_done, 1)
                        if q in SELF:
                            s = SELF[q] * TILES + g
                            dve.wait_ge(self_done, s + 1)
                            dve.tensor_tensor(R[:, bass.ds(g, 1), :], psS[:, :].unsqueeze(1),
                                              bias.unsqueeze(1), ALU.add).then_inc(self_used, 1)
                    chain.leave(HALVES)
                dve.wait_ge(acc_done, 4 + (q + 1) * CHUNKS - past)
                if q in SELF:
                    dve.wait_ge(self_used, (SELF[q] + 1) * TILES)
                if q == 0:
                    degrees()
                dve.sem_inc(agg_done, 1)

            def degrees():
                dve.wait_ge(part_copied, 2 * GROUPS)
                same, total = G[:, 6, 0:CHUNKS], G[:, 7, 0:CHUNKS]
                dve.memset(same[:, CHUNKS - 1:CHUNKS], 0.0)
                then(dve.tensor_tensor(same[:, 0:CHUNKS - 1], tile_d[:, 1:CHUNKS], tile_d[:, 0:CHUNKS - 1],
                                       ALU.is_equal))
                then(dve.tensor_tensor_scan(total[:, ::-1], same[:, ::-1], t128[:, ::-1], 0.0, ALU.mult, ALU.add))
                firsts = regs(nc, dve, chunk0_i, 0, TILES, CHUNKS - 1)
                for t in range(TILES):
                    last = dve.tensor_copy(inv[:, t:t + 1], total[:, bass.ds(firsts[t], 1)])
                then(last)
                then(dve.tensor_scalar(inv[:, :], inv[:, :], 1.0, None, ALU.max))
                then(dve.reciprocal(inv[:, :], inv[:, :]))

            def norm(at, src, dst):
                then(dve.bn_stats(stat[0][:, 0:6], src))
                dve.sem_inc(s_tick2, 1)
                dve.bn_aggr(stat[0][:, 6:8], stat[0][:, 0:6]).then_inc(var_ready, 1)
                dve.wait_ge(std_ready, at)
                then(dve.reciprocal(stat[0][:, 9:10], stat[0][:, 8:9]))
                return dve.tensor_scalar(dst, src, stat[0][:, 6:7], stat[0][:, 9:10], ALU.subtract, ALU.mult)

            lag = chain.lag

            def stats(at):
                for h in range(2):
                    lag(dve.bn_stats(stat[h][:, 0:6], T1[h]))
                chain.settle()
                for h in range(2):
                    dve.sem_inc(s_tick2, 1)
                    dve.bn_aggr(stat[h][:, 6:8], stat[h][:, 0:6]).then_inc(var_ready, 1)
                for h in range(2):
                    dve.wait_ge(std_ready, at + h + 1)
                    lag(dve.reciprocal(stat[h][:, 9:10], stat[h][:, 8:9]))

            def normed(h, dst):
                return dve.tensor_scalar(dst, T1[h], stat[h][:, 6:7], stat[h][:, 9:10], ALU.subtract, ALU.mult)

            def dense(m, steps, per, vectors, body):
                if vectors:
                    dve.wait_ge(s_v[vectors], 32)
                with dve.Fori(0, HALVES) as i:
                    chain.enter(i, steps)
                    body(2 * i, lns[0] + i * 2 * per, m)
                    dve.wait_ge(xn_ready, m * TILES + 2 * i + 2)
                    chain.leave(HALVES)
                lns[0] += per * TILES
                dve.wait_ge(y_copied, 2 + (m + 1) * TILES)
                dve.wait_ge(kept, m * TILES)
                dve.sem_inc(d_done, 1)

            def free(h, m, t):
                dve.wait_ge(xt2_ready, m * TILES + t + h + 1)
                dve.wait_ge(kept, (m - 1) * TILES + t)

            def tile_of(buf, t):
                return buf[:, bass.ds(t, 1), :]

            t1 = [T1[h].unsqueeze(1) for h in range(2)]
            by_dst = lambda c: recf[:, bass.ds(c, 1), 1]

            dve.wait_ge(s_v["sum0"], 32)
            sums(0, by_dst, bias=VEC[:, 0, :], row=tile_d)

            def mean_and_self(t):
                for h in range(2):
                    lag(dve.scalar_tensor_tensor(t1[h], tile_of(ACC, t + h), inv[:, bass.ds(t + h, 1)],
                                                 tile_of(R, t + h), ALU.mult, ALU.add))

            def layer0(t, at, m):
                mean_and_self(t)
                stats(at)
                for h in range(2):
                    lag(normed(h, T2[h]))
                for h in range(2):
                    lag(dve.tensor_tensor(T2[h], T2[h], VEC[:, 0, :], ALU.mult))
                for h in range(2):
                    lag(dve.tensor_tensor(T1[h], T2[h], VEC[:, 1, :], ALU.add))
                for h in range(2):
                    lag(dve.tensor_scalar(T2[h], T1[h], 0.0, alpha, ALU.min, ALU.mult))
                for h in range(2):
                    lag(dve.scalar_tensor_tensor(T1[h], T1[h], 0.0, T2[h], ALU.max, ALU.add))
                for h in range(2):
                    lag(dve.scalar_tensor_tensor(t1[h], tile_of(X, t + h), 2.0, t1[h], ALU.mult, ALU.add))
                stats(at + 2)
                for h in range(2):
                    free(h, m, t)
                    chain.settle()
                    normed(h, XN[h]).then_inc(xn_ready, 1)

            dense(1, 22, 2, "norm0", layer0)

            dve.wait_ge(s_srcrec, 32)
            src_rec = rf[:, 0:CHUNKS * 4].rearrange("p (c f) -> p c f", f=4)
            then(dve.tensor_copy(rf[:, CHUNKS * 4:CHUNKS * 5].bitcast(I32).unsqueeze(2), src_rec[:, :, 1:2]))
            dve.sem_inc(s_srcidx, 1)
            sums(1, lambda c: src_rec[:, bass.ds(c, 1), 0], weight=lambda c: src_rec[:, bass.ds(c, 1), 2],
                 row=row2)

            def layer1(t, at, m):
                for h in range(2):
                    lag(dve.tensor_tensor(t1[h], tile_of(ACC, t + h), VEC[:, 0, :].unsqueeze(1), ALU.add))
                for h in range(2):
                    lag(dve.tensor_tensor(t1[h], tile_of(X, t + h), t1[h], ALU.add))
                stats(at)
                for h in range(2):
                    free(h, m, t)
                    chain.settle()
                    normed(h, XN[h]).then_inc(xn_ready, 1)

            dense(2, 8, 1, "l1", layer1)

            sums(2, by_dst, bias=VEC[:, 1, :], row=tile_d)

            def layer2a(t, at, m):
                mean_and_self(t)
                for h in range(2):
                    free(h, m, t)
                    chain.settle()
                    dve.tensor_scalar(XN[h], T1[h], 0.0, None, ALU.max).then_inc(xn_ready, 1)

            dense(3, 2, 0, None, layer2a)
            dve.wait_ge(s_v["l2b"], 16)
            sums(3, by_dst, bias=VEC[:, 0, :], row=tile_d)

            def layer2b(t, at, m):
                mean_and_self(t)
                for h in range(2):
                    lag(dve.scalar_tensor_tensor(t1[h], t1[h], 0.0, tile_of(X, t + h), ALU.max, ALU.add))
                stats(at)
                for h in range(2):
                    free(h, m, t)
                    chain.settle()
                    normed(h, XN[h]).then_inc(xn_ready, 1)

            dense(4, 8, 1, None, layer2b)

            raw = accf[:, 0:CHUNKS * H].rearrange("p (c h) -> p c h", h=H)
            with dve.Fori(0, HALVES) as i:
                for half in range(2):
                    g = 2 * i + half
                    for j in range(3):
                        onehot(4, g, j, by_dst)
                    for j in range(GROUP):
                        a = g * GROUP + j
                        dve.wait_ge(g_landed[j % RING],
                                    16 * (4 * CHUNKS // RING + g * (GROUP // RING) + j // RING + 1))
                        dve.wait_ge(a_q, 2 + a + 1)
                        dve.tensor_tensor(G[:, j % RING, :], G[:, j % RING, :], psA[j % 2][:, :], ALU.mult)\
                            .then_inc(a_mul, 1)
                        if j + 3 < GROUP:
                            onehot(4, g, j + 3, by_dst)
                        dve.wait_ge(a_mul, 2 + a + 1)
                        dve.tensor_reduce(raw[:, bass.ds(a, 1), :].rearrange("p a h -> p (a h)"),
                                          G[:, j % RING, :].rearrange("p (h k) -> p h k", h=H), AX.X, ALU.add)\
                            .then_inc(g_free, 1)
            dve.wait_ge(g_free, RING + 5 * CHUNKS)

            key8 = accf[:, 3328:6656].rearrange("p (c h) -> p c h", h=H)
            em9 = accf[:, 6656:6656 + CHUNKS * 9].rearrange("p (c f) -> p c f", f=9)
            last_key = accf[:, 10400:10400 + CHUNKS]
            far = accf[:, 10816:10816 + CHUNKS + 1]
            okay = accf[:, 11240:11240 + CHUNKS]
            ep = rf[:, 0:3328].rearrange("p (c h) -> p c h", h=H)
            keys = recf[:, :, 1:2]
            then(dve.tensor_copy(key8, keys.broadcast_to([P, CHUNKS, H])))
            dve.sem_inc(m_in, 1)
            then(dve.tensor_scalar(okay.unsqueeze(2), keys, 0.0, None, ALU.is_ge))
            then(dve.scalar_tensor_tensor(okay.unsqueeze(2), keys, float(P), okay.unsqueeze(2), ALU.is_lt, ALU.mult))
            then(dve.tensor_scalar(okay, okay, 1.0, FAR, ALU.subtract, ALU.mult))
            dve.wait_ge(a_q, 2 + CHUNKS)
            then(dve.tensor_tensor(ep, raw, okay.unsqueeze(2).broadcast_to([P, CHUNKS, H]), ALU.add))
            dve.sem_inc(m_in, 1)
            nb = len(range(0, GROUPS, 4))
            dve.wait_ge(m_cp, nb)
            kt = rf[:, 6656:9984].rearrange("p (g s) -> p g s", s=P)
            et = rf[:, 3328:6656]
            gate = rf[:, 9984:13312].rearrange("p (g s) -> p g s", s=P)
            lk = accf[:, 3328:6656].rearrange("p (g s) -> p g s", s=P)
            dve.memset(gate[:, :, 0:1], 0.0)
            then(dve.tensor_tensor(gate[:, :, 1:P], kt[:, :, 1:P], kt[:, :, 0:P - 1], ALU.is_equal))
            dve.memset(lk[:, :, P - 1:P], 1.0)
            then(dve.tensor_scalar(lk[:, :, 0:P - 1], gate[:, :, 1:P], -1.0, 1.0, ALU.mult, ALU.add))
            then(dve.scalar_tensor_tensor(lk, kt, 1.0, lk, ALU.add, ALU.mult))
            then(dve.tensor_scalar(lk, lk, -1.0, None, ALU.add))
            dve.sem_inc(m_in, 1)
            then(dve.tensor_scalar(gate, gate, 1.0, FAR, ALU.subtract, ALU.mult))
            dve.wait_ge(m_cp, 2 * nb)
            then(dve.tensor_tensor_scan(rf[:, 6656:9984], rf[:, 9984:13312], et, -FAR, ALU.add, ALU.max))
            then(dve.memset(em9[:, :, H:H + 1], 1.0))
            dve.sem_inc(m_in, 1)
            dve.wait_ge(m_cp, 4 * nb)
            with dve.Fori(0, HALVES) as i:
                for half in range(2):
                    for j in range(GROUP):
                        c = (2 * i + half) * GROUP + j
                        dve.wait_ge(b_mm, c + 1)
                        dve.tensor_scalar(OH[j % OH_RING], iota[:, :], last_key[:, bass.ds(c, 1)], None,
                                          ALU.is_equal).then_inc(b_oh, 1)
            dve.wait_ge(b_cp, 2 + GROUPS)
            mb9 = accf[:, 0:CHUNKS * 9].rearrange("p (c f) -> p c f", f=9)
            mx = rf[:, 3328:6656].rearrange("p (c h) -> p c h", h=H)
            my = accf[:, 6656:9984].rearrange("p (c h) -> p c h", h=H)
            then(dve.tensor_scalar(mb9[:, :, H:H + 1], mb9[:, :, H:H + 1], 1.0, FAR, ALU.subtract, ALU.mult))
            dve.tensor_tensor(mx, mb9[:, :, 0:H], mb9[:, :, H:H + 1].broadcast_to([P, CHUNKS, H]), ALU.add)
            dve.memset(far[:, 0:1], 0.0)
            dve.memset(far[:, CHUNKS:CHUNKS + 1], 0.0)
            then(dve.tensor_tensor(far[:, 1:CHUNKS], tile_d[:, 1:CHUNKS], tile_d[:, 0:CHUNKS - 1], ALU.is_equal))
            then(dve.tensor_scalar(far, far, 1.0, FAR, ALU.subtract, ALU.mult))
            for h in range(H):
                last = dve.tensor_tensor_scan(my[:, :, h], far[:, 0:CHUNKS], mx[:, :, h], -FAR, ALU.add, ALU.max)
            then(last)
            for h in range(H):
                last = dve.tensor_tensor_scan(mx[:, ::-1, h], far[:, CHUNKS:0:-1], my[:, ::-1, h], -FAR,
                                              ALU.add, ALU.max)
            then(last)
            dve.sem_inc(m_in, 1)
            with dve.Fori(0, HALVES) as i:
                for half in range(2):
                    g = 2 * i + half
                    for j in range(GROUP):
                        c = g * GROUP + j
                        dve.wait_ge(p_tp, c + 1)
                        dve.tensor_scalar(OH[j % OH_RING], iota[:, :], by_dst(c), None, ALU.is_equal)\
                            .then_inc(p_oh, 1)
                    dve.wait_ge(p_mm, 2 + (g + 1) * GROUP)
                    part = rf[:, bass.ds(g * GROUP * H, GROUP * H)]
                    dve.tensor_tensor(part, part, psY[half][:, 0:GROUP * H], ALU.subtract).then_inc(p_sub, 1)
            dve.wait_ge(p_exp, GROUPS)
            zsum = rf[:, 9984:9984 + TILES * H].rearrange("p (t h) -> p t h", h=H)
            zf = rf[:, 9984:9984 + TILES * H]
            sums(5, by_dst, row=tile_d)
            then(dve.tensor_scalar(zf, zf, 1e-30, None, ALU.max))
            then(dve.reciprocal(zf, zf))
            dve.wait_ge(s_v["last"], 96)
            vec = [rf[:, 3328 + n * D:3328 + (n + 1) * D] for n in range(5)]
            steps = 17
            with dve.Fori(0, NT) as t:
                chain.enter(t, steps)
                dve.tensor_tensor(XN[0].rearrange("p (h k) -> p h k", h=H),
                                  ACC[:, bass.ds(t, 1), :].rearrange("p a (h k) -> p (a h) k", h=H),
                                  rf[:, bass.ds(t * H + 9984, H)].unsqueeze(2).broadcast_to([P, H, DK]), ALU.mult)\
                    .then_inc(f_an, 1)
                dve.wait_ge(f_mm, 2 * t + 1)
                then(dve.tensor_tensor(t1[0], psY[0][:, :].unsqueeze(1), tile_of(X, t), ALU.add))
                then(norm(lns[0] + 3 * t + 1, T1[0], T2[0]))
                then(dve.tensor_tensor(T2[0], T2[0], vec[0], ALU.mult))
                then(dve.tensor_tensor(XN[1], T2[0], vec[1], ALU.add))
                dve.sem_inc(f_xp, 1)
                dve.wait_ge(f_mm, 2 * t + 2)
                then(dve.tensor_tensor(T1[0], psY[1][:, :], XN[1], ALU.add))
                then(dve.tensor_tensor(T1[0], T1[0], vec[4], ALU.add))
                then(norm(lns[0] + 3 * t + 2, T1[0], T2[0]))
                then(dve.tensor_tensor(T2[0], T2[0], vec[2], ALU.mult))
                then(dve.tensor_tensor(T2[0], T2[0], vec[3], ALU.add))
                then(dve.tensor_tensor(t1[0], T2[0].unsqueeze(1), tile_of(X, t), ALU.add))
                then(norm(lns[0] + 3 * t + 3, t1[0], tile_of(X, t)))
                dve.sem_inc(f_out, 1)
                chain.leave(NT)


def kernel(**inputs):
    import numpy as _np
    import concourse.bacc as _bacc
    from concourse import mybir as _mybir
    from concourse.bass_utils import run_bass_kernel_spmd as _run

    get = {k: _np.asarray(v) for k, v in inputs.items()}
    src, dst, w = get["src"], get["dst"], get["edge_weight"]
    none = _np.int32(NT * P)
    pad = P * NAT - E
    edges = _np.stack([_np.concatenate([src, _np.full(P, none, src.dtype)]),
                       _np.concatenate([dst, _np.full(P, none, dst.dtype)])], axis=1)
    arrays = {
        "x": get["x"],
        "edges": edges,
        "src_nat": _np.concatenate([src, _np.full(pad, none, src.dtype)]).reshape(P, NAT),
        "dst_nat": _np.concatenate([dst, _np.full(pad, none, dst.dtype)]).reshape(P, NAT),
        "w_nat": _np.concatenate([w, _np.zeros(pad, w.dtype)]).reshape(P, NAT),
    }
    names = {
        "l0_ws": "L0_gnn_W_self", "l0_bs": "L0_gnn_b_self", "l0_wn": "L0_gnn_W_neigh",
        "l0_g": "L0_gnn_gamma", "l0_b": "L0_gnn_beta", "l0_alpha": "L0_gnn_alpha",
        "l1_w": "L1_gnn_weight", "l1_b": "L1_gnn_bias",
        "l2_ws1": "L2_gnn_W_self1", "l2_wn1": "L2_gnn_W_neigh1", "l2_b1": "L2_gnn_b1",
        "l2_ws2": "L2_gnn_W_self2", "l2_wn2": "L2_gnn_W_neigh2", "l2_b2": "L2_gnn_b2",
        "wq": "L3_gnn_Wq", "wk": "L3_gnn_Wk", "wv": "L3_gnn_Wv", "wo": "L3_gnn_Wo",
        "ln1_g": "L3_gnn_ln1_g", "ln1_b": "L3_gnn_ln1_b", "ln2_g": "L3_gnn_ln2_g", "ln2_b": "L3_gnn_ln2_b",
        "w1": "L3_gnn_W1", "b1": "L3_gnn_b1", "w2": "L3_gnn_W2", "b2": "L3_gnn_b2",
    }
    for short, name in names.items():
        arrays[short] = get[name].reshape(1, 1) if short == "l0_alpha" else get[name]
    nc = _bacc.Bacc("TRN2", target_bir_lowering=False, num_devices=1)
    maps, args = {}, {}
    for name, a in arrays.items():
        a = _np.ascontiguousarray(a)
        maps[f"in_{name}"] = a
        args[name] = nc.dram_tensor(f"in_{name}", a.shape, _mybir.dt.from_np(a.dtype), kind="ExternalInput").ap()
    args["out"] = nc.dram_tensor("out_dram", (N, D), F32, kind="ExternalOutput").ap()
    build(nc, **args)
    r = _run(nc, [maps], core_ids=[0])
    return r.results[0]["out_dram"]
```

```python
from contextlib import ExitStack

import numpy as np
import concourse.bass as bass
from concourse import mybir

ALU = mybir.AluOpType
ACT = mybir.ActivationFunctionType
AX = mybir.AxisListType
F32 = mybir.dt.float32
I32 = mybir.dt.int32

P = 128
N = 3125
E = 50000
D = 512
KD = D // P
H = 8
DK = D // H
DFF = 128
NT = -(-N // P)
TILES = NT + 1
LAST = N - (NT - 1) * P
ROWS = TILES * P
GROUP = 16
GROUPS = -(-(E + NT * (P - 1)) // P // GROUP) + (1 if (E + NT * (P - 1)) // P % GROUP == 0 else 0)
CHUNKS = GROUPS * GROUP
HALVES = GROUPS // 2
NAT = -(-E // (P * 56)) * 56
SPARE = 2
PITCH = CHUNKS + SPARE
SCAT = 8
RING = 8
OH_RING = 4
HV = 5
EPS = 1e-5
FAR = 1e30
assert CHUNKS == 416 and TILES == GROUPS and GROUPS % 2 == 0 and NAT == 392


class Chain:

    def __init__(self, eng, sem):
        self.eng, self.sem, self.count, self.loop = eng, sem, 0, 0

    def then(self, ins):
        ins.then_inc(self.sem, 1)
        self.count += 1
        self.eng.wait_ge(self.sem, self.loop + self.count)

    def lag(self, ins):
        ins.then_inc(self.sem, 1)
        self.count += 1
        self.eng.wait_ge(self.sem, self.loop + self.count - 1)

    def settle(self):
        self.eng.wait_ge(self.sem, self.loop + self.count)

    def enter(self, i, steps):
        self.loop, self.steps, self.first = i * steps, steps, self.count

    def leave(self, times):
        assert self.count - self.first == self.steps, (self.count - self.first, self.steps)
        self.count = self.first + self.steps * times
        self.loop = 0


def over_groups(eng, body):
    with eng.Fori(0, HALVES - 1) as i:
        body(i, False)
    body(HALVES - 1, True)


def regs(nc, eng, row, at, n, top):
    return nc.values_load_multi_w_load_instructions(
        row[0:1, bass.ds(at, n)], engines=(eng.engine,), min_val=0, max_val=top,
        skip_runtime_bounds_check_because="worked out on the chip within these bounds")[1]


def build(nc, x, edges, src_nat, dst_nat, w_nat, l0_ws, l0_bs, l0_wn, l0_g, l0_b, l0_alpha,
          l1_w, l1_b, l2_ws1, l2_wn1, l2_b1, l2_ws2, l2_wn2, l2_b2,
          wq, wk, wv, wo, ln1_g, ln1_b, ln2_g, ln2_b, w1, b1, w2, b2, out):
    with ExitStack() as ctx:
        def sb(name, shape, dt=F32):
            return ctx.enter_context(nc.sbuf_tensor(name, shape, dt))

        def sem(name):
            return ctx.enter_context(nc.semaphore(name))

        def dram(name, shape):
            return nc.dram_tensor(name, shape, F32, kind="Internal").ap()

        table = [dram(f"table{k}", [ROWS, D]) for k in range(5)]
        vtable = dram("vtable", [ROWS, D])
        by_src = dram("by_src", [P * PITCH, 4])
        tile_s_dram = nc.dram_tensor("tile_s_dram", [P, CHUNKS], I32, kind="Internal").ap()

        X = sb("X", [P, TILES, D])
        ACC = sb("ACC", [P, TILES, D])
        R = sb("R", [P, TILES, D])
        G = sb("G", [P, RING, D])
        WA = sb("WA", [P, KD, D])
        WB = sb("WB", [P, KD, D])
        OHX = sb("OHX", [P, OH_RING + 2, P])
        iota = sb("iota", [P, P])
        ident = sb("ident", [P, P])
        VEC = sb("VEC", [P, 2, D])
        XT = sb("XT", [P, KD, P])
        XS = sb("XS", [P, D])
        rec = sb("rec", [P, CHUNKS, 2], I32)
        tile_d = sb("tile_d", [P, CHUNKS], I32)
        row2 = sb("row2", [P, CHUNKS], I32)
        stage_idx = sb("stage_idx", [P, 2, GROUP], I32)
        inv = sb("inv", [P, TILES])
        small = sb("small", [P, 48])
        chunk0_i = sb("chunk0_i", [P, 32], I32)
        sc_rec = sb("sc_rec", [P, 2, SCAT, 4])
        sc_pos = sb("sc_pos", [P, 2, SCAT], I32)
        alpha = small[:, 30:31]
        ones = small[:, 31:32]
        eps = small[:, 28:29]
        stat = [small[:, 0:12], small[:, 12:24]]
        recf = rec[:, :, :].bitcast(F32)

        accf = ACC[:, :, :].rearrange("p t d -> p (t d)")
        rf = R[:, :, :].rearrange("p t d -> p (t d)")
        count = rf[:, 13000:13032]
        XN = [G[:, 0, :], G[:, 1, :]]
        XTW = [G[:, 2 + i, :].rearrange("p (k n) -> p k n", k=KD) for i in range(2)]
        Y = [G[:, 4, :], G[:, 5, :]]
        T1 = [G[:, 6, :], XS[:, :]]
        T2 = [G[:, 7, :], XT[:, :, :].rearrange("p k n -> p (k n)")]
        OH = [OHX[:, i, :] for i in range(OH_RING)]
        OHT = [OHX[:, OH_RING + i, :] for i in range(2)]
        waf = WA[:, :, :].rearrange("p k n -> p (k n)")
        nrec = waf[:, 0:NAT * 4].rearrange("p (c f) -> p c f", f=4)
        npos = waf[:, NAT * 4:NAT * 5].bitcast(I32)
        blank = accf[:, NT * NAT:NT * NAT + PITCH * 4]
        tiles_s = accf[:, NT * NAT + PITCH * 4:NT * NAT + PITCH * 4 + CHUNKS].bitcast(I32)

        t128 = VEC[:, 1, 0:CHUNKS]
        vec = [rf[:, 3328 + n * D:3328 + (n + 1) * D] for n in range(5)]
        AN, XTA, T1A, T2A = ([G[:, 2 * n + h, :] for h in range(2)] for n in range(4))
        XP, XTB, XB, TB = ([rf[:, 5888 + (2 * n + h) * D:5888 + (2 * n + h + 1) * D] for h in range(2)]
                           for n in range(4))
        XTA, XTB = ([v.rearrange("p (k n) -> p k n", k=KD) for v in b] for b in (XTA, XTB))
        HID = [OHX[:, h, :] for h in range(2)]
        zparts = rf[:, 6656:9984]

        bank = [ctx.enter_context(nc.psum_tensor(f"bank{i}", [P, D], F32)) for i in range(8)]
        psA = bank[0:2]
        psR = [bank[0], bank[1], bank[4], bank[5]]
        psT, psS = bank[2], bank[3]
        psTP = bank[2:4]
        psY = bank[4:6]
        psD, psQ = bank[6], bank[7]

        s_const = sem("s_const")
        s_x = sem("s_x")
        s_nat = sem("s_nat")
        s_cnt = sem("s_cnt")
        s_tot = sem("s_tot")
        s_rows = sem("s_rows")
        s_prep = sem("s_prep")
        s_blank = sem("s_blank")
        s_blank_out = sem("s_blank_out")
        s_tile_out = sem("s_tile_out")
        s_rec = [sem("s_rec0"), sem("s_rec1")]
        s_scat_in = sem("s_scat_in")
        s_float = sem("s_float")
        s_key = sem("s_key")
        s_scat = [sem("s_scat0"), sem("s_scat1")]
        s_srcrec = sem("s_srcrec")
        s_srcidx = sem("s_srcidx")
        s_w = {k: sem(f"w_{k}") for k in
               ("wn0", "ws0", "w1", "wn2a", "ws2a", "wn2b", "ws2b", "wk", "wq", "wv", "wo", "ffn")}
        s_v = {k: sem(f"v_{k}") for k in ("sum0", "norm0", "l1", "l2b", "last")}
        s_stage = sem("s_stage")
        g_landed = [sem(f"g_landed{i}") for i in range(RING)]
        g_free = sem("g_free")
        oh_ready = sem("oh_ready")
        acc_done = sem("acc_done")
        part_ready = sem("part_ready")
        part_copied = sem("part_copied")
        acc_read = sem("acc_read")
        cleared = sem("cleared")
        xs_ready = sem("xs_ready")
        tp_done = sem("tp_done")
        xt_ready = sem("xt_ready")
        self_done = sem("self_done")
        self_used = sem("self_used")
        xn_ready = sem("xn_ready")
        tp2_done = sem("tp2_done")
        xt2_ready = sem("xt2_ready")
        y_done = sem("y_done")
        y_copied = sem("y_copied")
        tab = [sem("tab0"), sem("tab1")]
        kept = sem("kept")
        var_ready = sem("var_ready")
        std_ready = sem("std_ready")
        dve_chain = sem("dve_chain")
        pool_chain = sem("pool_chain")
        d_done = sem("d_done")
        agg_done = sem("agg_done")
        v_staged = sem("v_staged")
        v_out = [sem("v_out0"), sem("v_out1")]
        a_tp = sem("a_tp")
        a_oht = sem("a_oht")
        a_q = sem("a_q")
        a_mul = sem("a_mul")
        s_tick, s_tick2 = sem("s_tick"), sem("s_tick2")
        m_in = sem("m_in")
        m_tp = sem("m_tp")
        m_cp = sem("m_cp")
        b_oh = sem("b_oh")
        b_mm = sem("b_mm")
        b_cp = sem("b_cp")
        p_oh = sem("p_oh")
        p_tp = sem("p_tp")
        p_oht = sem("p_oht")
        p_mm = sem("p_mm")
        p_sub = sem("p_sub")
        p_exp = sem("p_exp")
        c_mul = sem("c_mul")
        c_mul2 = sem("c_mul2")
        fa_in = sem("fa_in")
        fa_turned = sem("fa_turned")
        fa_copied = sem("fa_copied")
        fa_out = sem("fa_out")
        fa_normed = sem("fa_normed")
        fa_scaled = sem("fa_scaled")
        fa_beside = sem("fa_beside")
        fb_turned = sem("fb_turned")
        fb_copied = sem("fb_copied")
        fb_hidden = sem("fb_hidden")
        fb_relu = sem("fb_relu")
        fb_out = sem("fb_out")
        fb_normed = sem("fb_normed")
        fb_scaled = sem("fb_scaled")
        f_out = sem("f_out")
        s_out = sem("s_out")

        block = ctx.enter_context(nc.Block())

        SELF = {0: 0, 2: 1, 3: 2, 4: 3}

        def wrows(w):
            return w.rearrange("(k p) n -> p k n", p=P)

        def across(v):
            return v.rearrange("(a n) -> a n", a=1).broadcast_to([P, v.shape[0]])

        @block.sync
        def _(sp):
            sp.dma_start(rf[:, 0:NAT].bitcast(I32), dst_nat).then_inc(s_nat, 16)
            sp.dma_start(rf[:, NAT:2 * NAT].bitcast(I32), src_nat).then_inc(s_nat, 16)
            sp.dma_start(rf[:, 2 * NAT:3 * NAT], w_nat).then_inc(s_nat, 16)
            sp.dma_start(WA[:, :, :], wrows(l0_wn)).then_inc(s_w["wn0"], 16)
            sp.wait_ge(s_const, 1)
            sp.wait_ge(s_blank, 1)
            sp.dma_start(by_src.rearrange("(p c) f -> p (c f)", p=P), blank).then_inc(s_blank_out, 16)
            for a in range(0, NT - 1, 4):
                sp.dma_start(X[:, a:a + 4, :],
                             x[a * P:(a + 4) * P, :].rearrange("(t p) d -> p t d", p=P)).then_inc(s_x, 16)
            sp.dma_start(X[0:LAST, NT - 1, :], x[(NT - 1) * P:N, :]).then_inc(s_x, 16)
            sp.dma_start(WB[:, :, :], wrows(l0_ws)).then_inc(s_w["ws0"], 16)
            sp.dma_start(VEC[:, 0, :], across(l0_bs)).then_inc(s_v["sum0"], 16)
            sp.dma_start(alpha, l0_alpha.broadcast_to([P, 1])).then_inc(s_v["sum0"], 16)

            sp.wait_ge(s_rows, 1)
            with sp.Fori(0, HALVES) as i:
                for half in range(2):
                    g = 2 * i + half
                    off = regs(nc, sp, row2, g * GROUP, GROUP, E)
                    for j in range(GROUP):
                        if j == 0:
                            sp.wait_ge(s_rec[half], i * 16 * GROUP)
                        sp.dma_start(rec[:, bass.ds(g * GROUP + j, 1), :],
                                     edges[bass.ds(off[j], P), :].unsqueeze(1)).then_inc(s_rec[half], 16)
            sp.wait_ge(agg_done, 1)
            sp.dma_start(VEC[:, 0, :], across(l0_g)).then_inc(s_v["norm0"], 16)
            sp.dma_start(VEC[:, 1, :], across(l0_b)).then_inc(s_v["norm0"], 16)
            sp.dma_start(WB[:, :, :], wrows(l1_w)).then_inc(s_w["w1"], 16)
            sp.wait_ge(s_tile_out, 16)
            sp.dma_start(row2[:, :], tile_s_dram).then_inc(s_srcrec, 16)
            for h in range(2):
                sp.wait_ge(s_scat[h], 16 * NAT // 2)
            sp.wait_ge(d_done, 1)
            sp.dma_start(rf[:, 0:CHUNKS * 4].rearrange("p (c f) -> p c f", f=4),
                         by_src.rearrange("(p c) f -> p c f", p=P)[:, 0:CHUNKS, :]).then_inc(s_srcrec, 16)
            sp.dma_start(VEC[:, 0, :], across(l1_b)).then_inc(s_v["l1"], 16)
            sp.dma_start(VEC[:, 1, :], across(l2_b1)).then_inc(s_v["l1"], 16)
            sp.dma_start(WA[:, :, :], wrows(l2_wn1)).then_inc(s_w["wn2a"], 16)
            sp.wait_ge(y_done, 2 + 2 * TILES)
            sp.dma_start(WB[:, :, :], wrows(l2_ws1)).then_inc(s_w["ws2a"], 16)
            sp.wait_ge(d_done, 2)
            sp.dma_start(VEC[:, 0, :], across(l2_b2)).then_inc(s_v["l2b"], 16)
            sp.wait_ge(y_done, 2 + 3 * TILES)
            sp.dma_start(WA[:, :, :], wrows(l2_wn2)).then_inc(s_w["wn2b"], 16)
            sp.wait_ge(self_done, 2 * TILES)
            sp.dma_start(WB[:, :, :], wrows(l2_ws2)).then_inc(s_w["ws2b"], 16)
            sp.wait_ge(y_done, 2 + 4 * TILES)
            sp.dma_start(WA[:, :, :], wrows(wk)).then_inc(s_w["wk"], 16)
            sp.wait_ge(self_done, 3 * TILES)
            sp.dma_start(WB[:, :, :], wrows(wq)).then_inc(s_w["wq"], 16)
            sp.wait_ge(y_done, 2 + 5 * TILES)
            sp.dma_start(WB[:, :, :], wrows(wv)).then_inc(s_w["wv"], 16)
            sp.dma_start(WA[:, :, :], wrows(wo)).then_inc(s_w["wo"], 16)
            with sp.Fori(0, HALVES) as i:
                for half in range(2):
                    t = 2 * i + half
                    sp.wait_ge(v_staged, t + 1)
                    sp.dma_start(vtable[bass.ds(t * P, P), :], VEC[:, half, :]).then_inc(v_out[half], 16)
            sp.wait_ge(self_done, 4 * TILES)
            sp.dma_start(WB[:, 0, :].rearrange("p (k n) -> p k n", k=KD), wrows(w1)).then_inc(s_w["ffn"], 16)
            sp.dma_start(WB[:, 1, :], w2).then_inc(s_w["ffn"], 16)
            sp.wait_ge(p_mm, 4 + CHUNKS // 4)
            for n, v in enumerate((ln1_g, ln1_b, ln2_g, ln2_b, b2)):
                sp.dma_start(rf[:, 3328 + n * D:3328 + (n + 1) * D], across(v)).then_inc(s_v["last"], 16)
            sp.dma_start(small[:, 29:30], b1.rearrange("(n a) -> n a", a=1)).then_inc(s_v["last"], 16)
            with sp.Fori(0, NT - 1) as t:
                sp.wait_ge(f_out, t + 1)
                sp.dma_start(out[bass.ds(t * P, P), :].unsqueeze(1), X[:, bass.ds(t, 1), :]).then_inc(s_out, 16)
            sp.wait_ge(f_out, NT)
            sp.dma_start(out[(NT - 1) * P:N, :], X[0:LAST, NT - 1, :]).then_inc(s_out, 16)
            sp.wait_ge(s_out, 16 * NT)

        @block.gpsimd
        def _(pool):
            chain = Chain(pool, pool_chain)
            pool.memset(X[:, NT - 1:TILES, :], 0.0).then_inc(s_const, 1)
            empty = blank.rearrange("p (c f) -> p c f", f=4)
            chain.then(pool.memset(empty, 0.0))
            pool.memset(empty[:, :, 0:1], -1.0)
            chain.then(pool.memset(empty[:, :, 1:2], float(NT * P)))
            pool.sem_inc(s_blank, 1)
            chain.then(pool.memset(ident[:, :], 0.0))
            pool.affine_select(out=ident[:, :], in_=ident[:, :], compare_op=ALU.not_equal, fill=1.0,
                               base=0, pattern=[[-1, P]], channel_multiplier=1).then_inc(s_const, 1)
            pool.iota(iota[:, :], pattern=[[1, P]], base=0, channel_multiplier=0,
                      allow_small_or_imprecise_dtypes=True).then_inc(s_const, 1)
            pool.memset(eps, EPS)
            pool.memset(ones, 1.0).then_inc(s_const, 1)
            pool.memset(OHX[:, 0, :], 1.0).then_inc(s_const, 1)
            chain.then(pool.memset(OHX[:, 1, :], 0.0))
            pool.affine_select(out=OHX[:, 1, :], in_=OHX[:, 1, :], compare_op=ALU.is_ge, fill=1.0,
                               base=0, pattern=[[-1, P]], channel_multiplier=1).then_inc(s_const, 1)

            def gathers(q, rows, idx):
                base = q * CHUNKS
                with pool.Fori(0, HALVES) as i:
                    for half in range(2):
                        g = 2 * i + half
                        if q == 0:
                            pool.wait_ge(s_rec[half], (i + 1) * 16 * GROUP)
                            at = bass.ds(g * GROUP, GROUP)
                            pool.tensor_copy(recf[:, at, 1], rec[:, at, 1]).then_inc(s_float, 1)
                            pool.wait_ge(s_float, g + 1)
                            pool.tensor_tensor(recf[:, at, 1], recf[:, at, 1], t128[:, at], ALU.subtract)\
                                .then_inc(s_key, 1)
                            pool.wait_ge(s_scat[half], i * 16 * SCAT)
                            pool.tensor_copy(sc_rec[:, half, :, :], nrec[:, bass.ds(g * SCAT, SCAT), :])\
                                .then_inc(s_scat_in, 1)
                            pool.tensor_copy(sc_pos[:, half, :], npos[:, bass.ds(g * SCAT, SCAT)])\
                                .then_inc(s_scat_in, 1)
                        pool.tensor_copy(stage_idx[:, half, :], idx(g)).then_inc(s_stage, 1)
                        pool.wait_ge(s_stage, q * GROUPS + g + 1)
                        for j in range(GROUP):
                            pool.wait_ge(g_free, base + g * GROUP + j + 1)
                            pool.sem_inc(s_tick, 1)
                            pool.indirect_dma_start(
                                out=G[:, j % RING, :], out_offset=None, in_=rows,
                                in_offset=bass.IndirectOffsetOnAxis(ap=stage_idx[:, half, j:j + 1], axis=0))\
                                .then_inc(g_landed[j % RING], 16)
                            if q == 0 and j % 2:
                                if j == 1:
                                    pool.wait_ge(s_scat_in, 2 * g + 2)
                                    pool.sem_inc(s_tick, 1)
                                scatter(sc_rec[:, half, j // 2, :], sc_pos[:, half, j // 2:j // 2 + 1], half)

            def scatter(record, place, half):
                pool.indirect_dma_start(out=by_src, out_offset=bass.IndirectOffsetOnAxis(ap=place, axis=0),
                                        in_=record, in_offset=None).then_inc(s_scat[half], 16)

            def table_ready(m):
                for half in range(2):
                    pool.wait_ge(tab[half], 16 * HALVES * (m + 1))
                if m:
                    pool.wait_ge(d_done, m)

            def clear(m):
                for i in range(HALVES):
                    pool.wait_ge(acc_read, (m - 1) * HALVES + i + 1)
                    pool.memset(ACC[:, 2 * i:2 * i + 2, :], 0.0).then_inc(cleared, 1)

            def by_dst(g):
                return rec[:, bass.ds(g * GROUP, GROUP), 0]

            pool.wait_ge(s_prep, 1)
            pool.wait_ge(s_blank_out, 16)
            table_ready(0)
            gathers(0, table[0], by_dst)
            rest = range(SCAT * GROUPS, NAT)
            for n, c in enumerate(rest):
                scatter(nrec[:, c, :], npos[:, c:c + 1], c % 2)
                if (n + 1) % (len(rest) // HALVES) == 0 and (n + 1) // (len(rest) // HALVES) <= HALVES:
                    i = (n + 1) // (len(rest) // HALVES) - 1
                    pool.wait_ge(acc_read, i + 1)
                    pool.memset(ACC[:, 2 * i:2 * i + 2, :], 0.0).then_inc(cleared, 1)
            idx_s = rf[:, CHUNKS * 4:CHUNKS * 5].bitcast(I32)
            table_ready(1)
            pool.wait_ge(s_srcidx, 1)
            gathers(1, table[1], lambda g: idx_s[:, bass.ds(g * GROUP, GROUP)])
            clear(2)
            table_ready(2)
            gathers(2, table[2], by_dst)
            clear(3)
            table_ready(3)
            gathers(3, table[3], by_dst)
            table_ready(4)
            gathers(4, table[4], by_dst)
            pool.wait_ge(m_in, 5)
            for i in range(HALVES):
                pool.memset(ACC[:, 2 * i:2 * i + 2, :], 0.0).then_inc(cleared, 1)
            for half in range(2):
                pool.wait_ge(v_out[half], 16 * HALVES)
            pool.wait_ge(p_mm, 4 + CHUNKS // 4)
            gathers(5, vtable, by_dst)
            def rounds(a, b):
                if b is not None:
                    for h in range(2):
                        pool.wait_ge(fb_normed, 2 * b + h + 1)
                        chain.lag(pool.tensor_tensor(TB[h], TB[h], vec[2], ALU.mult))
                    chain.settle()
                    for h in range(2):
                        pool.tensor_tensor(TB[h], TB[h], vec[3], ALU.add).then_inc(fb_scaled, 1)
                if a is not None:
                    for h in range(2):
                        pool.wait_ge(fa_normed, 2 * a + h + 1)
                        chain.lag(pool.tensor_tensor(T2A[h], T2A[h], vec[0], ALU.mult))
                    chain.settle()
                    for h in range(2):
                        pool.tensor_tensor(XP[h], T2A[h], vec[1], ALU.add).then_inc(fa_scaled, 1)
                    for h in range(2):
                        pool.wait_ge(fa_scaled, 2 * a + h + 1)
                        pool.sem_inc(s_tick, 1)
                        pool.tensor_tensor(XB[h], XP[h], vec[4], ALU.add).then_inc(fa_beside, 1)

            pool.wait_ge(s_v["last"], 96)
            rounds(0, None)
            with pool.Fori(1, HALVES) as i:
                chain.enter(i - 1, 4)
                rounds(i, i - 1)
                chain.leave(HALVES - 1)
            rounds(None, HALVES - 1)

        @block.scalar
        def _(act):
            def roots(m, lns, i):
                for n in range(lns):
                    for h in range(2):
                        act.wait_ge(var_ready, LN_AT[m] + i * 2 * lns + 2 * n + h + 1)
                        act.activation(stat[h][:, 8:9], stat[h][:, 7:8], ACT.Sqrt, bias=eps).then_inc(std_ready, 1)

            def turned(m, i):
                for h in range(2):
                    tc = m * TILES + 2 * i + h
                    act.wait_ge(tp2_done, tc + 1)
                    act.wait_ge(y_done, tc + 1)
                    act.activation(XTW[h].rearrange("p k n -> p (k n)"), psTP[h][:, :], ACT.Copy)\
                        .then_inc(xt2_ready, 1)

            def products(m, i, queries):
                for h in range(2):
                    t = 2 * i + h
                    act.wait_ge(y_done, 2 + m * TILES + t + 1)
                    act.wait_ge(tab[h], (m * HALVES + i) * 16)
                    if queries:
                        act.activation(R[:, bass.ds(t, 1), :], psA[h][:, :].unsqueeze(1), ACT.Copy,
                                       scale=float(DK) ** -0.5)
                    act.activation(Y[h], psY[h][:, :], ACT.Copy).then_inc(y_copied, 1)
                for h in range(2):
                    t = 2 * i + h
                    act.wait_ge(y_copied, 2 + m * TILES + t + 1)
                    act.dma_start(table[m][bass.ds(t * P, P), :], Y[h]).then_inc(tab[h], 16)

            def dense(m, lns, keep=None, queries=False):
                def step(i, before):
                    if m == 0:
                        for h in range(2):
                            tc = 2 * i + h
                            act.wait_ge(xt2_ready, tc + 1)
                            act.activation(XN[h].unsqueeze(1), X[:, bass.ds(tc, 1), :], ACT.Copy)\
                                .then_inc(xn_ready, 1)
                    roots(m, lns, i)
                    turned(m, i)
                    if before is not None:
                        products(m, before, queries)
                    if keep is not None:
                        for h in range(2):
                            act.wait_ge(xn_ready, m * TILES + 2 * i + h + 1)
                            act.activation(keep[:, bass.ds(2 * i + h, 1), :], XN[h].unsqueeze(1), ACT.Copy)\
                                .then_inc(kept, 1)

                if m == 0:
                    act.wait_ge(s_x, 16 * 7)
                step(0, None)
                with act.Fori(1, HALVES) as i:
                    step(i, i - 1)
                products(m, HALVES - 1, queries)

            def beside(q, source, values=False):
                k = SELF[q]
                with act.Fori(0, HALVES) as i:
                    for half in range(2):
                        t = 2 * i + half
                        s = k * TILES + t
                        act.wait_ge(tp_done, s)
                        act.activation(XS[:, :].unsqueeze(1), source[:, bass.ds(t, 1), :], ACT.Copy)\
                            .then_inc(xs_ready, 1)
                        if q == 4:
                            scores(i, half, range(0, 8))
                        act.wait_ge(tp_done, s + 1)
                        act.wait_ge(self_done, s)
                        act.activation(XT[:, :, :].rearrange("p k n -> p (k n)"), psT[:, :], ACT.Copy)\
                            .then_inc(xt_ready, 1)
                        if q == 4:
                            scores(i, half, range(8, GROUP))
                            act.wait_ge(self_done, s + 1)
                            act.wait_ge(v_out[half], i * 16)
                            act.activation(VEC[:, half, :], psS[:, :], ACT.Copy).then_inc(v_staged, 1)
                        if q == 0:
                            act.wait_ge(part_ready, t + 1)
                            act.activation(VEC[:, 1, bass.ds(t * GROUP, GROUP)], bank[6 + half][:, 0:GROUP],
                                           ACT.Copy).then_inc(part_copied, 1)

            def scores(i, half, chunks):
                for j in chunks:
                    a = (2 * i + half) * GROUP + j
                    act.wait_ge(a_tp, OH_RING + a + 1)
                    act.wait_ge(a_q, a + 1)
                    act.activation(OHT[j % 2], psY[j % 2][:, 0:P], ACT.Copy).then_inc(a_oht, 1)

            LN_AT = [0, 0, 2 * TILES, 3 * TILES, 3 * TILES]
            dense(0, 0)
            act.wait_ge(s_prep, 1)
            act.dma_start(tile_s_dram, tiles_s).then_inc(s_tile_out, 16)
            beside(0, X)
            dense(1, 2, keep=X)
            dense(2, 1, keep=X)
            beside(2, X)
            dense(3, 0, keep=R)
            beside(3, R)
            dense(4, 1, keep=X, queries=True)
            beside(4, X)

            kt, et = rf[:, 6656:9984], rf[:, 3328:6656]
            batches = [(a, min(4, GROUPS - a)) for a in range(0, GROUPS, 4)]
            n = 0
            for dst in (kt, et):
                for a, m in batches:
                    act.wait_ge(m_tp, n + 1)
                    act.activation(dst[:, a * P:(a + m) * P], bank[n % 2][:, 0:m * P], ACT.Copy).then_inc(m_cp, 1)
                    n += 1
            em9 = accf[:, 6656:6656 + CHUNKS * 9].rearrange("p (c f) -> p c f", f=9)
            last = accf[:, 10400:10400 + CHUNKS]
            for what in range(2):
                for a, m in batches:
                    act.wait_ge(m_tp, n + 1)
                    src = bank[n % 2][:, 0:m * P].rearrange("p (c h) -> p c h", h=H)
                    if what == 0:
                        dst = last[:, a * GROUP:(a + m) * GROUP].unsqueeze(2)
                        act.activation(dst, src[:, :, 0:1], ACT.Copy).then_inc(m_cp, 1)
                    else:
                        act.activation(em9[:, a * GROUP:(a + m) * GROUP, 0:H], src, ACT.Copy).then_inc(m_cp, 1)
                    n += 1
            mb9 = accf[:, 0:CHUNKS * 9].rearrange("p (c f) -> p c f", f=9)
            with act.Fori(0, HALVES) as i:
                for half in range(2):
                    g = 2 * i + half
                    act.wait_ge(b_mm, RING + (g + 1) * 4)
                    act.activation(mb9[:, bass.ds(g * GROUP, GROUP), :],
                                   psY[half][:, 0:GROUP * 9].rearrange("p (c f) -> p c f", f=9), ACT.Copy)\
                        .then_inc(b_cp, 1)
            ep = rf[:, 0:CHUNKS * H]
            with act.Fori(0, HALVES) as i:
                for b in range(8):
                    n = i * 8 + b
                    act.wait_ge(p_tp, 4 + n + 1)
                    act.wait_ge(p_mm, n + 1)
                    act.activation(G[:, 4 + b % 4, :], bank[b % 2][:, :], ACT.Copy).then_inc(p_oht, 1)
                for half in range(2):
                    g = 2 * i + half
                    act.wait_ge(p_sub, 2 + g + 1)
                    part = ep[:, bass.ds(g * GROUP * H, GROUP * H)]
                    act.activation(part, part, ACT.Exp).then_inc(p_exp, 1)
            act.wait_ge(p_exp, GROUPS)

            def weighted(g, j):
                act.wait_ge(g_landed[j % RING],
                            16 * (5 * CHUNKS // RING + g * (GROUP // RING) + j // RING + 1))
                for h in range(HV, H):
                    slot = G[:, j % RING, h * DK:(h + 1) * DK]
                    last = act.activation(slot, slot, ACT.Copy, scale=rf[:, bass.ds((g * GROUP + j) * H + h, 1)])
                last.then_inc(c_mul2, 1)

            for j in range(4):
                weighted(0, j)

            def values(i, end):
                for half in range(2):
                    g = 2 * i + half
                    for j in range(4, GROUP + 4):
                        if not (end and half == 1 and j >= GROUP):
                            weighted(g, j)
                    act.wait_ge(part_ready, GROUPS + g + 1)
                    act.activation(zparts[:, bass.ds(g * GROUP * H, GROUP * H)], bank[6 + half][:, 0:GROUP * H],
                                   ACT.Copy).then_inc(part_copied, 1)

            over_groups(act, values)

            def root(n, h):
                act.wait_ge(var_ready, 4 * TILES + n + h + 1)
                act.activation(stat[h][:, 8:9], stat[h][:, 7:8], ACT.Sqrt, bias=eps).then_inc(std_ready, 1)

            def rounds(a, b, n):
                if a is not None:
                    for h in range(2):
                        act.wait_ge(fa_turned, 2 * a + h + 1)
                        act.activation(XTA[h].rearrange("p k n -> p (k n)"), psTP[h][:, :], ACT.Copy)\
                            .then_inc(fa_copied, 1)
                for part in ([b] if b is not None else []) + ([a] if a is not None else []) + \
                            ([b] if b is not None else []):
                    for h in range(2):
                        root(n, h)
                    n = n + 2
                if a is not None:
                    for h in range(2):
                        act.wait_ge(fb_turned, 2 * a + h + 1)
                        act.activation(XTB[h].rearrange("p k n -> p (k n)"), psA[h][:, :], ACT.Copy)\
                            .then_inc(fb_copied, 1)

            rounds(0, None, 0)
            with act.Fori(1, HALVES) as i:
                rounds(i, i - 1, 6 * i - 4)
            rounds(None, HALVES - 1, 6 * HALVES - 4)

        @block.tensor
        def _(pe):
            pe.sem_inc(g_free, RING)
            pe.sem_inc(y_done, 2)
            pe.sem_inc(a_q, 2)
            pe.sem_inc(a_tp, OH_RING)
            pe.sem_inc(b_mm, RING)
            pe.sem_inc(p_tp, 4)
            pe.sem_inc(p_mm, 4)
            pe.sem_inc(xt2_ready, 2)
            pe.sem_inc(y_copied, 2)
            pe.sem_inc(acc_done, 4)
            pe.sem_inc(a_oht, 2)
            pe.sem_inc(a_mul, 2)
            pe.sem_inc(b_cp, 2)
            pe.sem_inc(p_oht, 2)
            pe.sem_inc(p_sub, 2)
            pe.sem_inc(part_copied, 2)
            pe.wait_ge(s_const, 6)

            def dense(m, *weights, queries=False, W=WA, pairs=(0, HALVES)):
                for w in weights:
                    pe.wait_ge(s_w[w], 16)
                with pe.Fori(*pairs) as i:
                    for h in range(2):
                        tc = m * TILES + 2 * i + h
                        pe.wait_ge(xn_ready, tc + 1)
                        pe.wait_ge(xt2_ready, tc + 1)
                        for k in range(KD):
                            last = pe.transpose(psTP[h][:, k * P:(k + 1) * P],
                                                XN[h][:, k * P:(k + 1) * P], ident[:, :])
                        last.then_inc(tp2_done, 1)
                    for h in range(2):
                        tc = m * TILES + 2 * i + h
                        pe.wait_ge(xt2_ready, 2 + tc + 1)
                        pe.wait_ge(y_copied, tc + 1)
                        if queries:
                            for k in range(KD):
                                pe.matmul(psA[h][:, :], XTW[h][:, k, :], WB[:, k, :],
                                          start=(k == 0), stop=(k == KD - 1))
                        for k in range(KD):
                            last = pe.matmul(psY[h][:, :], XTW[h][:, k, :], W[:, k, :],
                                             start=(k == 0), stop=(k == KD - 1))
                        last.then_inc(y_done, 1)

            def beside_turn(s):
                pe.wait_ge(xs_ready, s + 1)
                pe.wait_ge(xt_ready, s)
                for k in range(KD):
                    last = pe.transpose(psT[:, k * P:(k + 1) * P], XS[:, k * P:(k + 1) * P], ident[:, :])
                last.then_inc(tp_done, 1)

            def beside_product(s):
                pe.wait_ge(xt_ready, s + 1)
                pe.wait_ge(self_used, s)
                for k in range(KD):
                    last = pe.matmul(psS[:, :], XT[:, k, :], WB[:, k, :], start=(k == 0), stop=(k == KD - 1))
                last.then_inc(self_done, 1)

            def sums(q, weights=None):
                if weights:
                    pe.wait_ge(s_w[weights], 16)
                past = CHUNKS if q == 5 else 0
                with pe.Fori(0, HALVES) as i:
                    for half in range(2):
                        g = 2 * i + half
                        if q == 0 or q == 5:
                            pe.wait_ge(part_copied, (GROUPS if q == 5 else 0) + g + 1)
                        for j in range(GROUP):
                            c = g * GROUP + j
                            n = q * CHUNKS + c
                            pe.wait_ge(oh_ready, n + 1)
                            if q == 0:
                                mm = pe.matmul(bank[6 + half][:, j:j + 1], OH[j % OH_RING], ones,
                                               start=True, stop=True)
                            if q == 5:
                                mm = pe.matmul(bank[6 + half][:, j * H:(j + 1) * H], OH[j % OH_RING],
                                               rf[:, bass.ds(c * H, H)], start=True, stop=True)
                                pe.wait_ge(c_mul, c + 1)
                                pe.wait_ge(c_mul2, c + 1)
                            else:
                                pe.wait_ge(g_landed[j % RING],
                                           16 * (q * CHUNKS // RING + g * (GROUP // RING) + j // RING + 1))
                            if (q == 0 or q == 5) and j == GROUP - 1:
                                mm.then_inc(part_ready, 1)
                            pe.wait_ge(acc_done, n + 1 - past)
                            pe.matmul(psR[j % 4][:, :], OH[j % OH_RING], G[:, j % RING, :],
                                      start=True, stop=True).then_inc(g_free, 1)
                            if q in SELF and j == 3:
                                beside_turn(SELF[q] * TILES + g)
                            if q in SELF and j == 11:
                                beside_product(SELF[q] * TILES + g)

            pe.wait_ge(s_cnt, 1)
            pe.matmul(psD[:, 0:NT], OHX[:, 0, :], count[:, 0:NT], start=True, stop=True).then_inc(s_tot, 1)
            dense(0, "wn0", pairs=(0, 8))
            pe.wait_ge(s_cnt, 2)
            pe.matmul(psD[:, 0:NT], OHX[:, 0, :], count[:, 0:NT], start=True, stop=True)
            pe.matmul(psD[:, 32:32 + NT], OHX[:, 1, :], count[:, 0:NT], start=True, stop=True).then_inc(s_tot, 1)
            dense(0, pairs=(8, HALVES))
            sums(0, "ws0")
            dense(1, "w1", W=WB)
            sums(1)
            dense(2, "wn2a")
            sums(2, "ws2a")
            dense(3, "wn2b")
            sums(3, "ws2b")
            dense(4, "wk", "wq", queries=True)
            pe.wait_ge(s_w["wv"], 16)
            def turn(g, j):
                a = g * GROUP + j
                pe.wait_ge(oh_ready, 4 * CHUNKS + a + 1)
                pe.wait_ge(a_oht, a + 1)
                pe.transpose(psY[j % 2][:, 0:P], OH[j % OH_RING], ident[:, :]).then_inc(a_tp, 1)

            def scores(i, end):
                for half in range(2):
                    g = 2 * i + half
                    tiles = regs(nc, pe, tile_d, g * GROUP, GROUP, TILES - 1)
                    for j in range(GROUP):
                        a = g * GROUP + j
                        if not (end and half == 1 and j + 1 == GROUP):
                            turn(g, j + 1)
                        pe.wait_ge(a_oht, 2 + a + 1)
                        pe.wait_ge(a_mul, a + 1)
                        pe.matmul(psA[j % 2][:, :].unsqueeze(1), OHT[j % 2], R[:, bass.ds(tiles[j], 1), :],
                                  start=True, stop=True).then_inc(a_q, 1)
                        if j == 3:
                            beside_turn(3 * TILES + g)
                        if j == 11:
                            pe.wait_ge(v_staged, g)
                            pe.wait_ge(xt_ready, 3 * TILES + g + 1)
                            for k in range(KD):
                                mm = pe.matmul(psS[:, :], XT[:, k, :], WB[:, k, :],
                                               start=(k == 0), stop=(k == KD - 1))
                            mm.then_inc(self_done, 1)

            turn(0, 0)
            over_groups(pe, scores)

            batches = [(a, min(4, GROUPS - a)) for a in range(0, GROUPS, 4)]
            key8, ep = accf[:, 3328:6656], rf[:, 0:3328]
            run = rf[:, 6656:9984]
            n = 0
            for step, src in enumerate((key8, ep, key8, run)):
                pe.wait_ge(m_in, (1, 2, 3, 4)[step])
                for a, m in batches:
                    if n >= 2:
                        pe.wait_ge(m_cp, n - 1)
                    for b in range(m):
                        last = pe.transpose(bank[n % 2][:, b * P:(b + 1) * P],
                                            src[:, (a + b) * P:(a + b + 1) * P], ident[:, :])
                    last.then_inc(m_tp, 1)
                    n += 1
            em9 = accf[:, 6656:6656 + CHUNKS * 9]
            pe.wait_ge(m_cp, 4 * len(batches))
            with pe.Fori(0, HALVES) as i:
                for b in range(8):
                    n = i * 8 + b
                    pe.wait_ge(b_oh, n + 1)
                    if b % 4 == 0:
                        pe.wait_ge(b_cp, 2 * i + b // 4 + 1)
                    for k in range(4):
                        j = b % 4 * 4 + k
                        mm = pe.matmul(psY[b // 4][:, j * 9:(j + 1) * 9], G[:, b, k * P:(k + 1) * P],
                                       em9[:, bass.ds((n * 4 + k) * 9, 9)], start=True, stop=True)
                    mm.then_inc(b_mm, 1)
            mx = rf[:, 3328:6656]
            pe.wait_ge(m_in, 5)

            def turn4(i, b):
                pe.wait_ge(p_oh, i * 8 + b + 1)
                pe.wait_ge(p_oht, i * 8 + b + 1)
                for k in range(4):
                    last = pe.transpose(bank[b % 2][:, k * P:(k + 1) * P], G[:, b % 4, k * P:(k + 1) * P],
                                        ident[:, :])
                last.then_inc(p_tp, 1)

            with pe.Fori(0, HALVES) as i:
                turn4(i, 0)
                for b in range(8):
                    n = i * 8 + b
                    if b < 7:
                        turn4(i, b + 1)
                    pe.wait_ge(p_oht, 2 + n + 1)
                    if b % 4 == 0:
                        pe.wait_ge(p_sub, 2 * i + b // 4 + 1)
                    for k in range(4):
                        j = b % 4 * 4 + k
                        mm = pe.matmul(psY[b // 4][:, j * H:(j + 1) * H], G[:, 4 + b % 4, k * P:(k + 1) * P],
                                       mx[:, bass.ds((n * 4 + k) * H, H)], start=True, stop=True)
                    mm.then_inc(p_mm, 1)

            pe.wait_ge(p_exp, GROUPS)
            sums(5)
            pe.wait_ge(s_w["wo"], 16)
            pe.wait_ge(s_w["ffn"], 32)

            def rounds(a, b):
                if a is not None:
                    for h in range(2):
                        pe.wait_ge(fa_in, 2 * a + h + 1)
                        for k in range(KD):
                            last = pe.transpose(psTP[h][:, k * P:(k + 1) * P], AN[h][:, k * P:(k + 1) * P],
                                                ident[:, :])
                        last.then_inc(fa_turned, 1)
                if b is not None:
                    for h in range(2):
                        pe.wait_ge(fb_relu, 2 * b + h + 1)
                        pe.matmul(psA[h][:, :], HID[h], WB[:, 1, :], start=True, stop=True).then_inc(fb_out, 1)
                if a is not None:
                    for h in range(2):
                        pe.wait_ge(fa_copied, 2 * a + h + 1)
                        for k in range(KD):
                            last = pe.matmul(psY[h][:, :], XTA[h][:, k, :], WA[:, k, :],
                                             start=(k == 0), stop=(k == KD - 1))
                        last.then_inc(fa_out, 1)
                    for h in range(2):
                        pe.wait_ge(fa_scaled, 2 * a + h + 1)
                        for k in range(KD):
                            last = pe.transpose(psA[h][:, k * P:(k + 1) * P], XP[h][:, k * P:(k + 1) * P],
                                                ident[:, :])
                        last.then_inc(fb_turned, 1)
                    for h in range(2):
                        pe.wait_ge(fb_copied, 2 * a + h + 1)
                        for k in range(KD):
                            last = pe.matmul(bank[6 + h][:, 0:P], WB[:, 0, k * P:(k + 1) * P], XTB[h][:, k, :],
                                             start=(k == 0), stop=(k == KD - 1))
                        last.then_inc(fb_hidden, 1)

            rounds(0, None)
            with pe.Fori(1, HALVES) as i:
                rounds(i, i - 1)
            rounds(None, HALVES - 1)

        @block.vector
        def _(dve):
            chain = Chain(dve, dve_chain)
            then = chain.then
            lns = [0]

            dst_i, src_i = rf[:, 0:NAT].bitcast(I32), rf[:, NAT:2 * NAT].bitcast(I32)
            w_f = rf[:, 2 * NAT:3 * NAT]
            tmp_at = [3 * NAT]

            def tmp(n):
                tmp_at[0] += n
                assert tmp_at[0] <= 13000
                return rf[:, tmp_at[0] - n:tmp_at[0]]

            dst_f, lo_f, hi_f, pos = (tmp(NAT) for _ in range(4))
            lo_i, hi_i, pos_lo, pos_hi = (tmp(NAT).bitcast(I32) for _ in range(4))
            zeros = tmp(NAT)
            mask = tmp(NAT)
            cidx = tmp(CHUNKS)
            tile_f, off_f, hop = tmp(CHUNKS), tmp(CHUNKS), tmp(CHUNKS)
            start, cnt, full_f, chunk0, first, step_ = (tmp(32) for _ in range(6))
            full_i = tmp(32).bitcast(I32)
            place = tmp(32)
            pre = accf[:, 0:NT * NAT].rearrange("p (t c) -> p t c", t=NT)

            def chunks_of():
                then(dve.tensor_scalar(full_f[:, 0:NT], cnt[:, 0:NT], float(P - 1), None, ALU.add))
                then(dve.tensor_copy(full_i[:, 0:NT], full_f[:, 0:NT]))
                then(dve.tensor_scalar(full_i[:, 0:NT], full_i[:, 0:NT], 7, None, ALU.logical_shift_right))
                then(dve.tensor_copy(full_f[:, 0:NT], full_i[:, 0:NT]))
                then(dve.tensor_tensor_scan(chunk0[:, 1:NT + 1], full_f[:, 0:NT], zeros[:, 0:NT], 0.0,
                                            ALU.add, ALU.add))

            then(dve.memset(zeros, 0.0))
            then(dve.memset(chunk0[:, 0:1], 0.0))
            then(dve.memset(start[:, 0:1], 0.0))
            dve.wait_ge(s_const, 6)
            for a in range(0, CHUNKS, P):
                m = min(P, CHUNKS - a)
                dve.tensor_scalar(cidx[:, a:a + m], iota[:, 0:m], float(a), None, ALU.add)
            dve.wait_ge(s_nat, 48)
            then(dve.tensor_copy(dst_f, dst_i))
            for t in range(NT):
                last = dve.tensor_scalar(pre[:, t, :], dst_f, float(P * (t + 1)), None, ALU.is_lt)
            then(last)
            dve.tensor_reduce(count[:, 0:NT], pre, AX.X, ALU.add).then_inc(s_cnt, 1)
            dve.wait_ge(s_tot, 1)
            then(dve.tensor_copy(start[:, 1:NT + 1], psD[:, 0:NT]))
            then(dve.tensor_tensor(cnt[:, 0:NT], start[:, 1:NT + 1], start[:, 0:NT], ALU.subtract))
            chunks_of()
            then(dve.scalar_tensor_tensor(first[:, 0:NT + 1], chunk0[:, 0:NT + 1], -float(P),
                                          start[:, 0:NT + 1], ALU.mult, ALU.add))
            then(dve.tensor_tensor(step_[:, 0:NT], first[:, 1:NT + 1], first[:, 0:NT], ALU.subtract))
            dve.tensor_scalar(off_f, cidx, float(P), None, ALU.mult)
            then(dve.memset(tile_f, 0.0))
            for t in range(NT):
                dve.tensor_scalar(hop, cidx, chunk0[:, t + 1:t + 2], step_[:, t:t + 1], ALU.is_ge, ALU.mult)
                then(dve.scalar_tensor_tensor(tile_f, cidx, chunk0[:, t + 1:t + 2], tile_f, ALU.is_ge, ALU.add))
                then(dve.tensor_tensor(off_f, off_f, hop, ALU.add))
            then(dve.tensor_scalar(off_f, off_f, float(E), None, ALU.min))
            dve.tensor_copy(tile_d[:, :], tile_f)
            dve.tensor_scalar(t128, tile_f, float(P), None, ALU.mult)
            then(dve.tensor_copy(row2[:, :], off_f))
            dve.sem_inc(s_rows, 1)
            then(dve.tensor_scalar(full_f[:, 0:TILES], chunk0[:, 0:TILES], float(CHUNKS - 1), None, ALU.min))
            then(dve.tensor_copy(chunk0_i[:, 0:TILES], full_f[:, 0:TILES]))

            dve.tensor_scalar(hi_i, src_i, 7, None, ALU.logical_shift_right)
            then(dve.tensor_scalar(lo_i, src_i, P - 1, None, ALU.bitwise_and))
            dve.tensor_copy(hi_f, hi_i)
            then(dve.tensor_copy(lo_f, lo_i))
            for b in range(NT):
                then(dve.tensor_scalar(mask, hi_f, float(b), None, ALU.is_equal))
                then(dve.tensor_tensor_scan(pre[:, b, :], mask, zeros, 0.0, ALU.add, ALU.add))
            dve.tensor_copy(count[:, 0:NT].unsqueeze(2), pre[:, :, NAT - 1:NAT]).then_inc(s_cnt, 1)
            dve.wait_ge(s_tot, 2)
            dve.tensor_copy(cnt[:, 0:NT], psD[:, 0:NT])
            then(dve.tensor_copy(place[:, 0:NT], psD[:, 32:32 + NT]))
            chunks_of()
            then(dve.scalar_tensor_tensor(place[:, 0:NT], chunk0[:, 0:NT], float(P), place[:, 0:NT],
                                          ALU.mult, ALU.add))
            then(dve.tensor_scalar(place[:, 0:NT], place[:, 0:NT], -1.0, None, ALU.add))
            then(dve.memset(tile_f, 0.0))
            for t in range(NT):
                then(dve.scalar_tensor_tensor(tile_f, cidx, chunk0[:, t + 1:t + 2], tile_f, ALU.is_ge, ALU.add))
            then(dve.tensor_tensor(pre, pre, place[:, 0:NT].unsqueeze(2).broadcast_to([P, NT, NAT]), ALU.add))
            for b in range(NT):
                last = dve.scalar_tensor_tensor(pre[:, b, :], hi_f, float(b), pre[:, b, :], ALU.is_equal, ALU.mult)
            then(last)
            then(dve.tensor_reduce(pos, pre.rearrange("p t c -> p c t"), AX.X, ALU.add))
            pads = P * NAT - E
            then(dve.tensor_scalar(mask, cidx[:, 0:NAT], float(CHUNKS * P - (NAT - pads)), None, ALU.add))
            then(dve.scalar_tensor_tensor(mask, hi_f, float(NT), mask, ALU.is_equal, ALU.mult))
            then(dve.tensor_tensor(pos, pos, mask, ALU.add))
            then(dve.tensor_copy(lo_i, pos))
            dve.tensor_scalar(pos_lo, lo_i, P - 1, None, ALU.bitwise_and)
            then(dve.tensor_scalar(pos_hi, lo_i, 7, None, ALU.logical_shift_right))
            dve.tensor_copy(mask, pos_lo)
            then(dve.tensor_copy(pos, pos_hi))
            then(dve.scalar_tensor_tensor(pos, mask, float(PITCH), pos, ALU.mult, ALU.add))
            then(dve.tensor_copy(tiles_s, tile_f))
            dve.wait_ge(y_done, 2 + TILES)
            dve.tensor_copy(nrec[:, :, 0:1], lo_f.unsqueeze(2))
            dve.tensor_copy(nrec[:, :, 1:2], dst_f.unsqueeze(2))
            dve.tensor_copy(nrec[:, :, 2:3], w_f.unsqueeze(2))
            dve.memset(nrec[:, :, 3:4], 0.0)
            then(dve.tensor_copy(npos, pos))
            dve.sem_inc(s_prep, 1)

            def onehot(q, g, j, key, weight=None):
                n = q * CHUNKS + g * GROUP + j
                c = g * GROUP + j
                if q == 4:
                    dve.wait_ge(a_tp, c + 1)
                else:
                    dve.wait_ge(g_free, RING - OH_RING + n + 1)
                if q == 0 and j % GROUP == 0:
                    dve.wait_ge(s_key, g + j // GROUP + 1)
                args = (key(c), weight(c), ALU.is_equal, ALU.mult) if weight else (key(c), None, ALU.is_equal)
                dve.tensor_scalar(OH[j % OH_RING], iota[:, :], *args).then_inc(oh_ready, 1)

            def weighted(g, j):
                dve.wait_ge(g_landed[j % RING],
                            16 * (5 * CHUNKS // RING + g * (GROUP // RING) + j // RING + 1))
                slot = G[:, j % RING, 0:HV * DK].rearrange("p (h k) -> p h k", h=HV)
                dve.tensor_tensor(slot, slot, rf[:, bass.ds((g * GROUP + j) * H, HV)].unsqueeze(2)
                                  .broadcast_to([P, HV, DK]), ALU.mult).then_inc(c_mul, 1)

            def sums(q, key, weight=None, bias=None, row=None):
                past = CHUNKS if q == 5 else 0
                if q == 0:
                    dve.wait_ge(s_blank_out, 16)
                    dve.wait_ge(s_tile_out, 16)
                    then(dve.memset(accf, 0.0))
                else:
                    dve.wait_ge(cleared, HALVES * (q if q < 4 else 4))
                for j in range(3):
                    onehot(q, 0, j, key, weight)
                if q == 5:
                    for j in range(2):
                        weighted(0, j)

                def groups(i, end):
                    for half in range(2):
                        g = 2 * i + half
                        tiles = regs(nc, dve, row, g * GROUP, GROUP, TILES - 1)
                        ahead = lambda j: not (end and half == 1 and j >= GROUP)
                        for j in range(GROUP):
                            n = q * CHUNKS + g * GROUP + j
                            if ahead(j + 3):
                                onehot(q, g, j + 3, key, weight)
                            if q == 5 and ahead(j + 2):
                                weighted(g, j + 2)
                            dve.wait_ge(g_free, RING + n + 1)
                            dve.wait_ge(acc_done, 4 + n - past)
                            slot = ACC[:, bass.ds(tiles[j], 1), :]
                            dve.tensor_tensor(slot, slot, psR[j % 4][:, :].unsqueeze(1), ALU.add)\
                                .then_inc(acc_done, 1)
                            if q in SELF and j == 14:
                                s = SELF[q] * TILES + g
                                dve.wait_ge(self_done, s + 1)
                                dve.tensor_tensor(R[:, bass.ds(g, 1), :], psS[:, :].unsqueeze(1),
                                                  bias.unsqueeze(1), ALU.add).then_inc(self_used, 1)

                over_groups(dve, groups)
                dve.wait_ge(acc_done, 4 + (q + 1) * CHUNKS - past)
                if q in SELF:
                    dve.wait_ge(self_used, (SELF[q] + 1) * TILES)
                if q == 0:
                    degrees()
                dve.sem_inc(agg_done, 1)

            def degrees():
                dve.wait_ge(part_copied, 2 + GROUPS)
                same, total = G[:, 6, 0:CHUNKS], G[:, 7, 0:CHUNKS]
                dve.memset(same[:, CHUNKS - 1:CHUNKS], 0.0)
                then(dve.tensor_tensor(same[:, 0:CHUNKS - 1], tile_d[:, 1:CHUNKS], tile_d[:, 0:CHUNKS - 1],
                                       ALU.is_equal))
                then(dve.tensor_tensor_scan(total[:, ::-1], same[:, ::-1], t128[:, ::-1], 0.0, ALU.mult, ALU.add))
                firsts = regs(nc, dve, chunk0_i, 0, TILES, CHUNKS - 1)
                for t in range(TILES):
                    last = dve.tensor_copy(inv[:, t:t + 1], total[:, bass.ds(firsts[t], 1)])
                then(last)
                then(dve.tensor_scalar(inv[:, :], inv[:, :], 1.0, None, ALU.max))
                then(dve.reciprocal(inv[:, :], inv[:, :]))

            lag = chain.lag

            def stats(at, of=T1):
                for h in range(2):
                    lag(dve.bn_stats(stat[h][:, 0:6], of[h]))
                chain.settle()
                for h in range(2):
                    dve.sem_inc(s_tick2, 1)
                    dve.bn_aggr(stat[h][:, 6:8], stat[h][:, 0:6]).then_inc(var_ready, 1)
                for h in range(2):
                    dve.wait_ge(std_ready, at + h + 1)
                    lag(dve.reciprocal(stat[h][:, 9:10], stat[h][:, 8:9]))

            def normed(h, dst, of=T1):
                return dve.tensor_scalar(dst, of[h], stat[h][:, 6:7], stat[h][:, 9:10], ALU.subtract, ALU.mult)

            def dense(m, steps, per, vectors, body):
                if vectors:
                    dve.wait_ge(s_v[vectors], 32)
                with dve.Fori(0, HALVES) as i:
                    chain.enter(i, steps)
                    body(2 * i, lns[0] + i * 2 * per, m)
                    dve.wait_ge(xn_ready, m * TILES + 2 * i + 2)
                    chain.leave(HALVES)
                lns[0] += per * TILES
                dve.wait_ge(y_copied, 2 + (m + 1) * TILES)
                dve.wait_ge(kept, m * TILES)
                dve.sem_inc(d_done, 1)

            def free(h, m, t):
                dve.wait_ge(xt2_ready, m * TILES + t + h + 1)
                dve.wait_ge(kept, (m - 1) * TILES + t)

            def tile_of(buf, t):
                return buf[:, bass.ds(t, 1), :]

            t1 = [T1[h].unsqueeze(1) for h in range(2)]
            by_dst = lambda c: recf[:, bass.ds(c, 1), 1]

            dve.wait_ge(s_v["sum0"], 32)
            sums(0, by_dst, bias=VEC[:, 0, :], row=tile_d)

            def mean_and_self(t):
                for h in range(2):
                    lag(dve.scalar_tensor_tensor(t1[h], tile_of(ACC, t + h), inv[:, bass.ds(t + h, 1)],
                                                 tile_of(R, t + h), ALU.mult, ALU.add))

            def layer0(t, at, m):
                mean_and_self(t)
                stats(at)
                dve.sem_inc(acc_read, 1)
                for h in range(2):
                    lag(normed(h, T2[h]))
                for h in range(2):
                    lag(dve.tensor_tensor(T2[h], T2[h], VEC[:, 0, :], ALU.mult))
                for h in range(2):
                    lag(dve.tensor_tensor(T1[h], T2[h], VEC[:, 1, :], ALU.add))
                for h in range(2):
                    lag(dve.tensor_scalar(T2[h], T1[h], 0.0, alpha, ALU.min, ALU.mult))
                for h in range(2):
                    lag(dve.scalar_tensor_tensor(T1[h], T1[h], 0.0, T2[h], ALU.max, ALU.add))
                for h in range(2):
                    lag(dve.scalar_tensor_tensor(t1[h], tile_of(X, t + h), 2.0, t1[h], ALU.mult, ALU.add))
                stats(at + 2)
                for h in range(2):
                    free(h, m, t)
                    chain.settle()
                    normed(h, XN[h]).then_inc(xn_ready, 1)

            dense(1, 22, 2, "norm0", layer0)

            dve.wait_ge(s_srcrec, 32)
            src_rec = rf[:, 0:CHUNKS * 4].rearrange("p (c f) -> p c f", f=4)
            then(dve.tensor_copy(rf[:, CHUNKS * 4:CHUNKS * 5].bitcast(I32).unsqueeze(2), src_rec[:, :, 1:2]))
            dve.sem_inc(s_srcidx, 1)
            sums(1, lambda c: src_rec[:, bass.ds(c, 1), 0], weight=lambda c: src_rec[:, bass.ds(c, 1), 2],
                 row=row2)

            def layer1(t, at, m):
                for h in range(2):
                    lag(dve.tensor_tensor(t1[h], tile_of(ACC, t + h), VEC[:, 0, :].unsqueeze(1), ALU.add))
                for h in range(2):
                    lag(dve.tensor_tensor(t1[h], tile_of(X, t + h), t1[h], ALU.add))
                stats(at)
                dve.sem_inc(acc_read, 1)
                for h in range(2):
                    free(h, m, t)
                    chain.settle()
                    normed(h, XN[h]).then_inc(xn_ready, 1)

            dense(2, 8, 1, "l1", layer1)

            sums(2, by_dst, bias=VEC[:, 1, :], row=tile_d)

            def layer2a(t, at, m):
                mean_and_self(t)
                for h in range(2):
                    free(h, m, t)
                    chain.settle()
                    dve.tensor_scalar(XN[h], T1[h], 0.0, None, ALU.max).then_inc(xn_ready, 1)
                dve.sem_inc(acc_read, 1)

            dense(3, 2, 0, None, layer2a)
            dve.wait_ge(s_v["l2b"], 16)
            sums(3, by_dst, bias=VEC[:, 0, :], row=tile_d)

            def layer2b(t, at, m):
                mean_and_self(t)
                for h in range(2):
                    lag(dve.scalar_tensor_tensor(t1[h], t1[h], 0.0, tile_of(X, t + h), ALU.max, ALU.add))
                stats(at)
                for h in range(2):
                    free(h, m, t)
                    chain.settle()
                    normed(h, XN[h]).then_inc(xn_ready, 1)

            dense(4, 8, 1, None, layer2b)

            raw = accf[:, 0:CHUNKS * H].rearrange("p (c h) -> p c h", h=H)
            for j in range(3):
                onehot(4, 0, j, by_dst)

            def scores(i, end):
                for half in range(2):
                    g = 2 * i + half
                    for j in range(GROUP):
                        a = g * GROUP + j
                        if not (end and half == 1 and j + 3 >= GROUP):
                            onehot(4, g, j + 3, by_dst)
                        dve.wait_ge(g_landed[j % RING],
                                    16 * (4 * CHUNKS // RING + g * (GROUP // RING) + j // RING + 1))
                        dve.wait_ge(a_q, 2 + a + 1)
                        dve.tensor_tensor(G[:, j % RING, :], G[:, j % RING, :], psA[j % 2][:, :], ALU.mult)\
                            .then_inc(a_mul, 1)
                        dve.wait_ge(a_mul, 2 + a + 1)
                        dve.tensor_reduce(raw[:, bass.ds(a, 1), :].rearrange("p a h -> p (a h)"),
                                          G[:, j % RING, :].rearrange("p (h k) -> p h k", h=H), AX.X, ALU.add)\
                            .then_inc(g_free, 1)

            over_groups(dve, scores)
            dve.wait_ge(g_free, RING + 5 * CHUNKS)

            key8 = accf[:, 3328:6656].rearrange("p (c h) -> p c h", h=H)
            em9 = accf[:, 6656:6656 + CHUNKS * 9].rearrange("p (c f) -> p c f", f=9)
            last_key = accf[:, 10400:10400 + CHUNKS]
            far = accf[:, 10816:10816 + CHUNKS + 1]
            okay = accf[:, 11240:11240 + CHUNKS]
            ep = rf[:, 0:3328].rearrange("p (c h) -> p c h", h=H)
            keys = recf[:, :, 1:2]
            then(dve.tensor_copy(key8, keys.broadcast_to([P, CHUNKS, H])))
            dve.sem_inc(m_in, 1)
            then(dve.tensor_scalar(okay.unsqueeze(2), keys, 0.0, None, ALU.is_ge))
            then(dve.scalar_tensor_tensor(okay.unsqueeze(2), keys, float(P), okay.unsqueeze(2), ALU.is_lt, ALU.mult))
            then(dve.tensor_scalar(okay, okay, 1.0, FAR, ALU.subtract, ALU.mult))
            dve.wait_ge(a_q, 2 + CHUNKS)
            then(dve.tensor_tensor(ep, raw, okay.unsqueeze(2).broadcast_to([P, CHUNKS, H]), ALU.add))
            dve.sem_inc(m_in, 1)
            nb = len(range(0, GROUPS, 4))
            dve.wait_ge(m_cp, nb)
            kt = rf[:, 6656:9984].rearrange("p (g s) -> p g s", s=P)
            et = rf[:, 3328:6656]
            gate = rf[:, 9984:13312].rearrange("p (g s) -> p g s", s=P)
            lk = accf[:, 3328:6656].rearrange("p (g s) -> p g s", s=P)
            dve.memset(gate[:, :, 0:1], 0.0)
            then(dve.tensor_tensor(gate[:, :, 1:P], kt[:, :, 1:P], kt[:, :, 0:P - 1], ALU.is_equal))
            dve.memset(lk[:, :, P - 1:P], 1.0)
            then(dve.tensor_scalar(lk[:, :, 0:P - 1], gate[:, :, 1:P], -1.0, 1.0, ALU.mult, ALU.add))
            then(dve.scalar_tensor_tensor(lk, kt, 1.0, lk, ALU.add, ALU.mult))
            then(dve.tensor_scalar(lk, lk, -1.0, None, ALU.add))
            dve.sem_inc(m_in, 1)
            then(dve.tensor_scalar(gate, gate, 1.0, FAR, ALU.subtract, ALU.mult))
            dve.wait_ge(m_cp, 2 * nb)
            then(dve.tensor_tensor_scan(rf[:, 6656:9984], rf[:, 9984:13312], et, -FAR, ALU.add, ALU.max))
            then(dve.memset(em9[:, :, H:H + 1], 1.0))
            dve.sem_inc(m_in, 1)
            dve.wait_ge(m_cp, 4 * nb)

            def onehot4(slot, key, c):
                return dve.tensor_tensor(G[:, slot, :].rearrange("p (c k) -> p c k", c=4),
                                         iota[:, :].unsqueeze(1).broadcast_to([P, 4, P]),
                                         key[:, bass.ds(c, 4)].unsqueeze(2).broadcast_to([P, 4, P]), ALU.is_equal)

            with dve.Fori(0, HALVES) as i:
                for b in range(8):
                    n = i * 8 + b
                    dve.wait_ge(b_mm, n + 1)
                    onehot4(b, last_key, n * 4).then_inc(b_oh, 1)
            dve.wait_ge(b_cp, 2 + GROUPS)
            mb9 = accf[:, 0:CHUNKS * 9].rearrange("p (c f) -> p c f", f=9)
            mx = rf[:, 3328:6656].rearrange("p (c h) -> p c h", h=H)
            my = accf[:, 6656:9984].rearrange("p (c h) -> p c h", h=H)
            then(dve.tensor_scalar(mb9[:, :, H:H + 1], mb9[:, :, H:H + 1], 1.0, FAR, ALU.subtract, ALU.mult))
            dve.tensor_tensor(mx, mb9[:, :, 0:H], mb9[:, :, H:H + 1].broadcast_to([P, CHUNKS, H]), ALU.add)
            dve.memset(far[:, 0:1], 0.0)
            dve.memset(far[:, CHUNKS:CHUNKS + 1], 0.0)
            then(dve.tensor_tensor(far[:, 1:CHUNKS], tile_d[:, 1:CHUNKS], tile_d[:, 0:CHUNKS - 1], ALU.is_equal))
            then(dve.tensor_scalar(far, far, 1.0, FAR, ALU.subtract, ALU.mult))
            for h in range(H):
                last = dve.tensor_tensor_scan(my[:, :, h], far[:, 0:CHUNKS], mx[:, :, h], -FAR, ALU.add, ALU.max)
            then(last)
            for h in range(H):
                last = dve.tensor_tensor_scan(mx[:, ::-1, h], far[:, CHUNKS:0:-1], my[:, ::-1, h], -FAR,
                                              ALU.add, ALU.max)
            then(last)
            dve.sem_inc(m_in, 1)
            with dve.Fori(0, HALVES) as i:
                for b in range(8):
                    n = i * 8 + b
                    dve.wait_ge(p_tp, n + 1)
                    onehot4(b % 4, recf[:, :, 1], n * 4).then_inc(p_oh, 1)
                for half in range(2):
                    g = 2 * i + half
                    dve.wait_ge(p_mm, 4 + (g + 1) * 4)
                    part = rf[:, bass.ds(g * GROUP * H, GROUP * H)]
                    dve.tensor_tensor(part, part, psY[half][:, 0:GROUP * H], ALU.subtract).then_inc(p_sub, 1)
            dve.wait_ge(p_exp, GROUPS)
            sums(5, by_dst, row=tile_d)
            z = rf[:, 9984:9984 + TILES * H].rearrange("p (t h) -> p t h", h=H)
            zf = rf[:, 9984:9984 + TILES * H]
            zp = zparts.rearrange("p (c h) -> p c h", h=H)
            total = rf[:, 0:CHUNKS * H].rearrange("p (c h) -> p c h", h=H)
            same = XS[:, 0:CHUNKS]
            dve.wait_ge(part_copied, 2 + 2 * GROUPS)
            dve.memset(same[:, CHUNKS - 1:CHUNKS], 0.0)
            then(dve.tensor_tensor(same[:, 0:CHUNKS - 1], tile_d[:, 1:CHUNKS], tile_d[:, 0:CHUNKS - 1], ALU.is_equal))
            for h in range(H):
                last = dve.tensor_tensor_scan(total[:, ::-1, h], same[:, ::-1], zp[:, ::-1, h], 0.0,
                                              ALU.mult, ALU.add)
            then(last)
            firsts = regs(nc, dve, chunk0_i, 0, TILES, CHUNKS - 1)
            for t in range(TILES):
                last = dve.tensor_copy(z[:, t:t + 1, :], total[:, bass.ds(firsts[t], 1), :])
            then(last)
            then(dve.tensor_scalar(zf, zf, 1e-30, None, ALU.max))
            then(dve.reciprocal(zf, zf))
            dve.wait_ge(s_v["last"], 96)

            def rounds(a, b, n):
                n = lns[0] + n
                if a is not None:
                    for h in range(2):
                        t = 2 * a + h
                        dve.tensor_tensor(AN[h].rearrange("p (h k) -> p h k", h=H),
                                          ACC[:, bass.ds(t, 1), :].rearrange("p a (h k) -> p (a h) k", h=H),
                                          rf[:, bass.ds(t * H + 9984, H)].unsqueeze(2).broadcast_to([P, H, DK]),
                                          ALU.mult).then_inc(fa_in, 1)
                if b is not None:
                    for h in range(2):
                        dve.wait_ge(fb_hidden, 2 * b + h + 1)
                        dve.tensor_scalar(HID[h], bank[6 + h][:, 0:P], small[:, 29:30], 0.0, ALU.add, ALU.max)\
                            .then_inc(fb_relu, 1)
                    for h in range(2):
                        dve.wait_ge(fb_out, 2 * b + h + 1)
                        dve.wait_ge(fa_beside, 2 * b + h + 1)
                        lag(dve.tensor_tensor(TB[h], psA[h][:, :], XB[h], ALU.add))
                    stats(n, TB)
                    chain.settle()
                    for h in range(2):
                        normed(h, TB[h], TB).then_inc(fb_normed, 1)
                    n = n + 2
                if a is not None:
                    for h in range(2):
                        dve.wait_ge(fa_out, 2 * a + h + 1)
                        lag(dve.tensor_tensor(T1A[h].unsqueeze(1), psY[h][:, :].unsqueeze(1),
                                              tile_of(X, 2 * a + h), ALU.add))
                    if b is not None:
                        dve.wait_ge(fb_normed, 2 * b + 2)
                    stats(n, T1A)
                    chain.settle()
                    for h in range(2):
                        normed(h, T2A[h], T1A).then_inc(fa_normed, 1)
                    n = n + 2
                if b is not None:
                    for h in range(2):
                        dve.wait_ge(fb_scaled, 2 * b + h + 1)
                        lag(dve.tensor_tensor(TB[h].unsqueeze(1), TB[h].unsqueeze(1), tile_of(X, 2 * b + h), ALU.add))
                    if a is not None:
                        dve.wait_ge(fa_normed, 2 * a + 2)
                    stats(n, TB)
                    chain.settle()
                    for h in range(2):
                        normed(h, tile_of(X, 2 * b + h), [v.unsqueeze(1) for v in TB]).then_inc(f_out, 1)

            rounds(0, None, 0)
            steps = 2 * (3 + 3 + 3)
            with dve.Fori(1, HALVES) as i:
                chain.enter(i - 1, steps)
                rounds(i, i - 1, 6 * i - 4)
                chain.leave(HALVES - 1)
            rounds(None, HALVES - 1, 6 * HALVES - 4)


def kernel(**inputs):
    import numpy as _np
    import concourse.bacc as _bacc
    from concourse import mybir as _mybir
    from concourse.bass_utils import run_bass_kernel_spmd as _run

    get = {k: _np.asarray(v) for k, v in inputs.items()}
    src, dst, w = get["src"], get["dst"], get["edge_weight"]
    none = _np.int32(NT * P)
    pad = P * NAT - E
    edges = _np.stack([_np.concatenate([src, _np.full(P, none, src.dtype)]),
                       _np.concatenate([dst, _np.full(P, none, dst.dtype)])], axis=1)
    arrays = {
        "x": get["x"],
        "edges": edges,
        "src_nat": _np.concatenate([src, _np.full(pad, none, src.dtype)]).reshape(P, NAT),
        "dst_nat": _np.concatenate([dst, _np.full(pad, none, dst.dtype)]).reshape(P, NAT),
        "w_nat": _np.concatenate([w, _np.zeros(pad, w.dtype)]).reshape(P, NAT),
    }
    names = {
        "l0_ws": "L0_gnn_W_self", "l0_bs": "L0_gnn_b_self", "l0_wn": "L0_gnn_W_neigh",
        "l0_g": "L0_gnn_gamma", "l0_b": "L0_gnn_beta", "l0_alpha": "L0_gnn_alpha",
        "l1_w": "L1_gnn_weight", "l1_b": "L1_gnn_bias",
        "l2_ws1": "L2_gnn_W_self1", "l2_wn1": "L2_gnn_W_neigh1", "l2_b1": "L2_gnn_b1",
        "l2_ws2": "L2_gnn_W_self2", "l2_wn2": "L2_gnn_W_neigh2", "l2_b2": "L2_gnn_b2",
        "wq": "L3_gnn_Wq", "wk": "L3_gnn_Wk", "wv": "L3_gnn_Wv", "wo": "L3_gnn_Wo",
        "ln1_g": "L3_gnn_ln1_g", "ln1_b": "L3_gnn_ln1_b", "ln2_g": "L3_gnn_ln2_g", "ln2_b": "L3_gnn_ln2_b",
        "w1": "L3_gnn_W1", "b1": "L3_gnn_b1", "w2": "L3_gnn_W2", "b2": "L3_gnn_b2",
    }
    for short, name in names.items():
        arrays[short] = get[name].reshape(1, 1) if short == "l0_alpha" else get[name]
    nc = _bacc.Bacc("TRN2", target_bir_lowering=False, num_devices=1)
    maps, args = {}, {}
    for name, a in arrays.items():
        a = _np.ascontiguousarray(a)
        maps[f"in_{name}"] = a
        args[name] = nc.dram_tensor(f"in_{name}", a.shape, _mybir.dt.from_np(a.dtype), kind="ExternalInput").ap()
    args["out"] = nc.dram_tensor("out_dram", (N, D), F32, kind="ExternalOutput").ap()
    build(nc, **args)
    r = _run(nc, [maps], core_ids=[0])
    return r.results[0]["out_dram"]
```

```python
from contextlib import ExitStack

import numpy as np
import concourse.bass as bass
from concourse import mybir

ALU = mybir.AluOpType
ACT = mybir.ActivationFunctionType
AX = mybir.AxisListType
F32 = mybir.dt.float32
I32 = mybir.dt.int32

P = 128
N = 3125
E = 50000
D = 512
KD = D // P
H = 8
DK = D // H
DFF = 128
NT = -(-N // P)
TILES = NT + 1
LAST = N - (NT - 1) * P
ROWS = TILES * P
GROUP = 16
GROUPS = -(-(E + NT * (P - 1)) // P // GROUP) + (1 if (E + NT * (P - 1)) // P % GROUP == 0 else 0)
CHUNKS = GROUPS * GROUP
HALVES = GROUPS // 2
NAT = -(-E // (P * 56)) * 56
SPARE = 2
PITCH = CHUNKS + SPARE
SCAT = 8
RING = 8
OH_RING = 4
BATCHES = -(-GROUPS // 4)
HS, HV = 5, 4
EPS = 1e-5
FAR = 1e30
assert CHUNKS == 416 and TILES == GROUPS and GROUPS % 2 == 0 and NAT == 392


class Chain:

    def __init__(self, eng, sem):
        self.eng, self.sem, self.count, self.loop = eng, sem, 0, 0

    def then(self, ins):
        ins.then_inc(self.sem, 1)
        self.count += 1
        self.eng.wait_ge(self.sem, self.loop + self.count)

    def lag(self, ins):
        ins.then_inc(self.sem, 1)
        self.count += 1
        self.eng.wait_ge(self.sem, self.loop + self.count - 1)

    def settle(self):
        self.eng.wait_ge(self.sem, self.loop + self.count)

    def enter(self, i, steps):
        self.loop, self.steps, self.first = i * steps, steps, self.count

    def leave(self, times):
        assert self.count - self.first == self.steps, (self.count - self.first, self.steps)
        self.count = self.first + self.steps * times
        self.loop = 0


def later(i):
    return not isinstance(i, int) or i > 0


def over_groups(eng, body, peel=False):
    if peel:
        body(0, False)
    with eng.Fori(1 if peel else 0, HALVES - 1) as i:
        body(i, False)
    body(HALVES - 1, True)


def regs(nc, eng, row, at, n, top):
    return nc.values_load_multi_w_load_instructions(
        row[0:1, bass.ds(at, n)], engines=(eng.engine,), min_val=0, max_val=top,
        skip_runtime_bounds_check_because="worked out on the chip within these bounds")[1]


def build(nc, x, edges, src_nat, dst_nat, w_nat, l0_ws, l0_bs, l0_wn, l0_g, l0_b, l0_alpha,
          l1_w, l1_b, l2_ws1, l2_wn1, l2_b1, l2_ws2, l2_wn2, l2_b2,
          wq, wk, wv, wo, ln1_g, ln1_b, ln2_g, ln2_b, w1, b1, w2, b2, out):
    with ExitStack() as ctx:
        def sb(name, shape, dt=F32):
            return ctx.enter_context(nc.sbuf_tensor(name, shape, dt))

        def sem(name):
            return ctx.enter_context(nc.semaphore(name))

        def dram(name, shape):
            return nc.dram_tensor(name, shape, F32, kind="Internal").ap()

        table = [dram(f"table{k}", [ROWS, D]) for k in range(5)]
        vtable = dram("vtable", [ROWS, D])
        by_src = dram("by_src", [P * PITCH, 4])
        tile_s_dram = nc.dram_tensor("tile_s_dram", [P, CHUNKS], I32, kind="Internal").ap()

        X = sb("X", [P, TILES, D])
        ACC = sb("ACC", [P, TILES, D])
        R = sb("R", [P, TILES, D])
        G = sb("G", [P, RING, D])
        WA = sb("WA", [P, KD, D])
        WB = sb("WB", [P, KD, D])
        OHX = sb("OHX", [P, OH_RING, P])
        iota = sb("iota", [P, P])
        ident = sb("ident", [P, P])
        VEC = sb("VEC", [P, 2, D])
        XT = sb("XT", [P, KD, P])
        XS = sb("XS", [P, D])
        rec = sb("rec", [P, CHUNKS, 2], I32)
        tile_d = sb("tile_d", [P, CHUNKS], I32)
        row2 = sb("row2", [P, CHUNKS], I32)
        stage_idx = sb("stage_idx", [P, 2, GROUP], I32)
        inv = sb("inv", [P, TILES])
        small = sb("small", [P, 48])
        chunk0_i = sb("chunk0_i", [P, 32], I32)
        sc_rec = sb("sc_rec", [P, 2, SCAT, 4])
        sc_pos = sb("sc_pos", [P, 2, SCAT], I32)
        alpha = small[:, 30:31]
        ones = small[:, 31:32]
        eps = small[:, 28:29]
        stat = [small[:, 0:12], small[:, 12:24]]
        recf = rec[:, :, :].bitcast(F32)

        accf = ACC[:, :, :].rearrange("p t d -> p (t d)")
        rf = R[:, :, :].rearrange("p t d -> p (t d)")
        count = rf[:, 13000:13032]
        XN = [G[:, 0, :], G[:, 1, :]]
        XTW = [G[:, 2 + i, :].rearrange("p (k n) -> p k n", k=KD) for i in range(2)]
        Y = [G[:, 4, :], G[:, 5, :]]
        T1 = [G[:, 6, :], XS[:, :]]
        T2 = [G[:, 7, :], XT[:, :, :].rearrange("p k n -> p (k n)")]
        OH = [OHX[:, i, :] for i in range(OH_RING)]
        OHT = [WA[:, 0, i * P:(i + 1) * P] for i in range(4)]
        waf = WA[:, :, :].rearrange("p k n -> p (k n)")
        nrec = waf[:, 0:NAT * 4].rearrange("p (c f) -> p c f", f=4)
        npos = waf[:, NAT * 4:NAT * 5].bitcast(I32)
        blank = accf[:, NT * NAT:NT * NAT + PITCH * 4]
        tiles_s = accf[:, NT * NAT + PITCH * 4:NT * NAT + PITCH * 4 + CHUNKS].bitcast(I32)

        t128 = VEC[:, 1, 0:CHUNKS]
        vec = [rf[:, 3328 + n * D:3328 + (n + 1) * D] for n in range(5)]
        AN, XTA, T1A, T2A = ([G[:, 2 * n + h, :] for h in range(2)] for n in range(4))
        XP, XTB, XB, TB = ([rf[:, 5888 + (2 * n + h) * D:5888 + (2 * n + h + 1) * D] for h in range(2)]
                           for n in range(4))
        XTA, XTB = ([v.rearrange("p (k n) -> p k n", k=KD) for v in b] for b in (XTA, XTB))
        HID = [OHX[:, h, :] for h in range(2)]
        kt, et = rf[:, 6656:9984], rf[:, 3328:6656]
        scratch = rf[:, 9984:13312]
        batches = [(a, min(4, GROUPS - a)) for a in range(0, GROUPS, 4)]
        key8, ep = accf[:, 3336:6664], accf[:, 6664:9992]

        def scan_order(v):
            return v.rearrange("p (j g h) -> p j g h", g=GROUPS, h=H)

        def turn_order(v):
            return v.rearrange("p (g j h) -> p j g h", g=GROUPS, h=H)

        cols = small[:, 32:37]
        carry = small[:, 38:40]
        carried = G[0:1, 3, 0:2 * P]
        zparts = rf[:, 6656:9984]

        bank = [ctx.enter_context(nc.psum_tensor(f"bank{i}", [P, D], F32)) for i in range(8)]
        psA = bank[0:2]
        psR = [bank[0], bank[1], bank[4], bank[5]]
        psT, psS = bank[2], bank[3]
        psTP = bank[2:4]
        psY = bank[4:6]
        psD = bank[6]
        psK = [bank[0], bank[1], bank[6], bank[7]]

        s_const = sem("s_const")
        s_x = sem("s_x")
        s_nat = sem("s_nat")
        s_cnt = sem("s_cnt")
        s_tot = sem("s_tot")
        s_rows = sem("s_rows")
        s_prep = sem("s_prep")
        s_blank = sem("s_blank")
        s_blank_out = sem("s_blank_out")
        s_tile_out = sem("s_tile_out")
        s_rec = [sem("s_rec0"), sem("s_rec1")]
        s_scat_in = sem("s_scat_in")
        s_float = sem("s_float")
        s_key = sem("s_key")
        s_scat = [sem("s_scat0"), sem("s_scat1")]
        s_srcrec = sem("s_srcrec")
        s_srcidx = sem("s_srcidx")
        s_w = {k: sem(f"w_{k}") for k in
               ("wn0", "ws0", "w1", "wn2a", "ws2a", "wn2b", "ws2b", "wk", "wq", "wv", "wo", "ffn")}
        s_v = {k: sem(f"v_{k}") for k in ("sum0", "norm0", "l1", "l2b", "last")}
        s_stage = sem("s_stage")
        g_landed = [sem(f"g_landed{i}") for i in range(RING)]
        g_free = sem("g_free")
        oh_ready = sem("oh_ready")
        acc_done = sem("acc_done")
        part_ready = sem("part_ready")
        part_copied = sem("part_copied")
        acc_read = sem("acc_read")
        cleared = sem("cleared")
        xs_ready = sem("xs_ready")
        tp_done = sem("tp_done")
        xt_ready = sem("xt_ready")
        self_done = sem("self_done")
        self_used = sem("self_used")
        xn_ready = sem("xn_ready")
        tp2_done = sem("tp2_done")
        xt2_ready = sem("xt2_ready")
        y_done = sem("y_done")
        y_copied = sem("y_copied")
        tab = [sem("tab0"), sem("tab1")]
        kept = sem("kept")
        var_ready = sem("var_ready")
        std_ready = sem("std_ready")
        dve_chain = sem("dve_chain")
        pool_chain = sem("pool_chain")
        d_done = sem("d_done")
        agg_done = sem("agg_done")
        v_staged = sem("v_staged")
        v_out = [sem("v_out0"), sem("v_out1")]
        a_tp = sem("a_tp")
        a_oht = sem("a_oht")
        a_q = sem("a_q")
        a_mul = sem("a_mul")
        a_sum = sem("a_sum")
        s_tick, s_tick2 = sem("s_tick"), sem("s_tick2")
        m_in = sem("m_in")
        m_tp = sem("m_tp")
        m_cp = sem("m_cp")
        m_rows = sem("m_rows")
        c_mul = sem("c_mul")
        c_mul2 = sem("c_mul2")
        fa_in = sem("fa_in")
        fa_turned = sem("fa_turned")
        fa_copied = sem("fa_copied")
        fa_out = sem("fa_out")
        fa_scaled = sem("fa_scaled")
        fa_beside = sem("fa_beside")
        fb_turned = sem("fb_turned")
        fb_copied = sem("fb_copied")
        fb_hidden = sem("fb_hidden")
        fb_relu = sem("fb_relu")
        fb_out = sem("fb_out")
        fb_normed = sem("fb_normed")
        fb_scaled = sem("fb_scaled")
        f_out = sem("f_out")
        s_out = sem("s_out")

        block = ctx.enter_context(nc.Block())

        SELF = {0: 0, 2: 1, 3: 2, 4: 3}

        def wrows(w):
            return w.rearrange("(k p) n -> p k n", p=P)

        def across(v):
            return v.rearrange("(a n) -> a n", a=1).broadcast_to([P, v.shape[0]])

        @block.sync
        def _(sp):
            sp.dma_start(rf[:, 0:NAT].bitcast(I32), dst_nat).then_inc(s_nat, 16)
            sp.dma_start(rf[:, NAT:2 * NAT].bitcast(I32), src_nat).then_inc(s_nat, 16)
            sp.dma_start(rf[:, 2 * NAT:3 * NAT], w_nat).then_inc(s_nat, 16)
            sp.dma_start(WA[:, :, :], wrows(l0_wn)).then_inc(s_w["wn0"], 16)
            sp.wait_ge(s_const, 1)
            sp.wait_ge(s_blank, 1)
            sp.dma_start(by_src.rearrange("(p c) f -> p (c f)", p=P), blank).then_inc(s_blank_out, 16)
            for a in range(0, NT - 1, 4):
                sp.dma_start(X[:, a:a + 4, :],
                             x[a * P:(a + 4) * P, :].rearrange("(t p) d -> p t d", p=P)).then_inc(s_x, 16)
            sp.dma_start(X[0:LAST, NT - 1, :], x[(NT - 1) * P:N, :]).then_inc(s_x, 16)
            sp.dma_start(WB[:, :, :], wrows(l0_ws)).then_inc(s_w["ws0"], 16)
            sp.dma_start(VEC[:, 0, :], across(l0_bs)).then_inc(s_v["sum0"], 16)
            sp.dma_start(alpha, l0_alpha.broadcast_to([P, 1])).then_inc(s_v["sum0"], 16)

            sp.wait_ge(s_rows, 1)
            def records(i, end):
                for half in range(2):
                    g = 2 * i + half
                    off = regs(nc, sp, row2, g * GROUP, GROUP, E)
                    for j in range(GROUP):
                        if j == 0 and later(i):
                            sp.wait_ge(s_rec[half], i * 16 * GROUP)
                        sp.dma_start(rec[:, bass.ds(g * GROUP + j, 1), :],
                                     edges[bass.ds(off[j], P), :].unsqueeze(1)).then_inc(s_rec[half], 16)

            over_groups(sp, records, peel=True)
            sp.wait_ge(agg_done, 1)
            sp.dma_start(VEC[:, 0, :], across(l0_g)).then_inc(s_v["norm0"], 16)
            sp.dma_start(VEC[:, 1, :], across(l0_b)).then_inc(s_v["norm0"], 16)
            sp.dma_start(WB[:, :, :], wrows(l1_w)).then_inc(s_w["w1"], 16)
            sp.wait_ge(s_tile_out, 16)
            sp.dma_start(row2[:, :], tile_s_dram).then_inc(s_srcrec, 16)
            for h in range(2):
                sp.wait_ge(s_scat[h], 16 * NAT // 2)
            sp.wait_ge(d_done, 1)
            sp.dma_start(rf[:, 0:CHUNKS * 4].rearrange("p (c f) -> p c f", f=4),
                         by_src.rearrange("(p c) f -> p c f", p=P)[:, 0:CHUNKS, :]).then_inc(s_srcrec, 16)
            sp.dma_start(VEC[:, 0, :], across(l1_b)).then_inc(s_v["l1"], 16)
            sp.dma_start(VEC[:, 1, :], across(l2_b1)).then_inc(s_v["l1"], 16)
            sp.dma_start(WA[:, :, :], wrows(l2_wn1)).then_inc(s_w["wn2a"], 16)
            sp.wait_ge(y_done, 2 + 2 * TILES)
            sp.dma_start(WB[:, :, :], wrows(l2_ws1)).then_inc(s_w["ws2a"], 16)
            sp.wait_ge(d_done, 2)
            sp.dma_start(VEC[:, 0, :], across(l2_b2)).then_inc(s_v["l2b"], 16)
            sp.wait_ge(y_done, 2 + 3 * TILES)
            sp.dma_start(WA[:, :, :], wrows(l2_wn2)).then_inc(s_w["wn2b"], 16)
            sp.wait_ge(self_done, 1 + 2 * TILES)
            sp.dma_start(WB[:, :, :], wrows(l2_ws2)).then_inc(s_w["ws2b"], 16)
            sp.wait_ge(y_done, 2 + 4 * TILES)
            sp.dma_start(WA[:, :, :], wrows(wk)).then_inc(s_w["wk"], 16)
            sp.wait_ge(self_done, 1 + 3 * TILES)
            sp.dma_start(WB[:, :, :], wrows(wq)).then_inc(s_w["wq"], 16)
            sp.wait_ge(y_done, 2 + 5 * TILES)
            sp.dma_start(WB[:, :, :], wrows(wv)).then_inc(s_w["wv"], 16)
            with sp.Fori(0, HALVES) as i:
                for half in range(2):
                    t = 2 * i + half
                    sp.wait_ge(v_staged, 1 + t + 1)
                    sp.dma_start(vtable[bass.ds(t * P, P), :], VEC[:, half, :]).then_inc(v_out[half], 16)
            sp.wait_ge(self_done, 1 + 4 * TILES)
            sp.dma_start(WB[:, 0, :].rearrange("p (k n) -> p k n", k=KD), wrows(w1)).then_inc(s_w["ffn"], 16)
            sp.dma_start(WB[:, 1, :], w2).then_inc(s_w["ffn"], 16)
            sp.wait_ge(a_q, 4 + CHUNKS)
            sp.dma_start(WA[:, :, :], wrows(wo)).then_inc(s_w["wo"], 16)
            sp.wait_ge(m_cp, 4 * BATCHES)
            for n, v in enumerate((ln1_g, ln1_b, ln2_g, ln2_b, b2)):
                sp.dma_start(rf[:, 3328 + n * D:3328 + (n + 1) * D], across(v)).then_inc(s_v["last"], 16)
            sp.dma_start(small[:, 29:30], b1.rearrange("(n a) -> n a", a=1)).then_inc(s_v["last"], 16)
            with sp.Fori(0, NT - 1) as t:
                sp.wait_ge(f_out, t + 1)
                sp.dma_start(out[bass.ds(t * P, P), :].unsqueeze(1), X[:, bass.ds(t, 1), :]).then_inc(s_out, 16)
            sp.wait_ge(f_out, NT)
            sp.dma_start(out[(NT - 1) * P:N, :], X[0:LAST, NT - 1, :]).then_inc(s_out, 16)
            sp.wait_ge(s_out, 16 * NT)

        @block.gpsimd
        def _(pool):
            chain = Chain(pool, pool_chain)
            pool.memset(X[:, NT - 1:TILES, :], 0.0).then_inc(s_const, 1)
            empty = blank.rearrange("p (c f) -> p c f", f=4)
            chain.then(pool.memset(empty, 0.0))
            pool.memset(empty[:, :, 0:1], -1.0)
            chain.then(pool.memset(empty[:, :, 1:2], float(NT * P)))
            pool.sem_inc(s_blank, 1)
            chain.then(pool.memset(ident[:, :], 0.0))
            pool.affine_select(out=ident[:, :], in_=ident[:, :], compare_op=ALU.not_equal, fill=1.0,
                               base=0, pattern=[[-1, P]], channel_multiplier=1).then_inc(s_const, 1)
            pool.iota(iota[:, :], pattern=[[1, P]], base=0, channel_multiplier=0,
                      allow_small_or_imprecise_dtypes=True).then_inc(s_const, 1)
            pool.memset(eps, EPS)
            pool.memset(ones, 1.0).then_inc(s_const, 1)
            pool.memset(OHX[:, 0, :], 1.0).then_inc(s_const, 1)
            chain.then(pool.memset(OHX[:, 1, :], 0.0))
            pool.affine_select(out=OHX[:, 1, :], in_=OHX[:, 1, :], compare_op=ALU.is_ge, fill=1.0,
                               base=0, pattern=[[-1, P]], channel_multiplier=1).then_inc(s_const, 1)

            def gathers(q, rows, idx):
                base = q * CHUNKS

                def groups(i, end):
                    for half in range(2):
                        g = 2 * i + half
                        if q == 0:
                            pool.wait_ge(s_rec[half], (i + 1) * 16 * GROUP)
                            at = bass.ds(g * GROUP, GROUP)
                            pool.tensor_copy(recf[:, at, 1], rec[:, at, 1]).then_inc(s_float, 1)
                            pool.wait_ge(s_float, g + 1)
                            pool.tensor_tensor(recf[:, at, 1], recf[:, at, 1], t128[:, at], ALU.subtract)\
                                .then_inc(s_key, 1)
                            if later(i):
                                pool.wait_ge(s_scat[half], i * 16 * SCAT)
                            pool.tensor_copy(sc_rec[:, half, :, :], nrec[:, bass.ds(g * SCAT, SCAT), :])\
                                .then_inc(s_scat_in, 1)
                            pool.tensor_copy(sc_pos[:, half, :], npos[:, bass.ds(g * SCAT, SCAT)])\
                                .then_inc(s_scat_in, 1)
                        pool.tensor_copy(stage_idx[:, half, :], idx(g)).then_inc(s_stage, 1)
                        pool.wait_ge(s_stage, q * GROUPS + g + 1)
                        for j in range(GROUP):
                            pool.wait_ge(g_free, base + g * GROUP + j + 1)
                            if q == 4:
                                pool.wait_ge(a_sum, g * GROUP + j + 1)
                            pool.sem_inc(s_tick, 1)
                            pool.indirect_dma_start(
                                out=G[:, j % RING, :], out_offset=None, in_=rows,
                                in_offset=bass.IndirectOffsetOnAxis(ap=stage_idx[:, half, j:j + 1], axis=0))\
                                .then_inc(g_landed[j % RING], 16)
                            if q == 0 and j % 2:
                                if j == 1:
                                    pool.wait_ge(s_scat_in, 2 * g + 2)
                                    pool.sem_inc(s_tick, 1)
                                scatter(sc_rec[:, half, j // 2, :], sc_pos[:, half, j // 2:j // 2 + 1], half)

                if q == 0:
                    over_groups(pool, groups, peel=True)
                else:
                    with pool.Fori(0, HALVES) as i:
                        groups(i, False)

            def scatter(record, place, half):
                pool.indirect_dma_start(out=by_src, out_offset=bass.IndirectOffsetOnAxis(ap=place, axis=0),
                                        in_=record, in_offset=None).then_inc(s_scat[half], 16)

            def table_ready(m):
                for half in range(2):
                    pool.wait_ge(tab[half], 16 * HALVES * (m + 1))
                if m:
                    pool.wait_ge(d_done, m)

            def clear(m):
                for i in range(HALVES):
                    pool.wait_ge(acc_read, (m - 1) * HALVES + i + 1)
                    pool.memset(ACC[:, 2 * i:2 * i + 2, :], 0.0).then_inc(cleared, 1)

            def by_dst(g):
                return rec[:, bass.ds(g * GROUP, GROUP), 0]

            pool.wait_ge(s_prep, 1)
            pool.wait_ge(s_blank_out, 16)
            table_ready(0)
            gathers(0, table[0], by_dst)
            rest = range(SCAT * GROUPS, NAT)
            for n, c in enumerate(rest):
                scatter(nrec[:, c, :], npos[:, c:c + 1], c % 2)
                if (n + 1) % (len(rest) // HALVES) == 0 and (n + 1) // (len(rest) // HALVES) <= HALVES:
                    i = (n + 1) // (len(rest) // HALVES) - 1
                    pool.wait_ge(acc_read, i + 1)
                    pool.memset(ACC[:, 2 * i:2 * i + 2, :], 0.0).then_inc(cleared, 1)
            idx_s = rf[:, CHUNKS * 4:CHUNKS * 5].bitcast(I32)
            table_ready(1)
            pool.wait_ge(s_srcidx, 1)
            gathers(1, table[1], lambda g: idx_s[:, bass.ds(g * GROUP, GROUP)])
            clear(2)
            table_ready(2)
            gathers(2, table[2], by_dst)
            clear(3)
            table_ready(3)
            gathers(3, table[3], by_dst)
            table_ready(4)
            gathers(4, table[4], by_dst)
            pool.wait_ge(m_in, 5)
            for i in range(HALVES):
                pool.memset(ACC[:, 2 * i:2 * i + 2, :], 0.0).then_inc(cleared, 1)
            for half in range(2):
                pool.wait_ge(v_out[half], 16 * HALVES)
            gathers(5, vtable, by_dst)
            def rounds(a, b):
                if b is not None:
                    for h in range(2):
                        pool.wait_ge(fb_normed, 2 * b + h + 1)
                        chain.lag(pool.tensor_tensor(TB[h], TB[h], vec[2], ALU.mult))
                    chain.settle()
                    for h in range(2):
                        pool.tensor_tensor(TB[h], TB[h], vec[3], ALU.add).then_inc(fb_scaled, 1)
                if a is not None:
                    for h in range(2):
                        pool.wait_ge(fa_scaled, 2 * a + h + 1)
                        pool.sem_inc(s_tick, 1)
                        pool.tensor_tensor(XB[h], XP[h], vec[4], ALU.add).then_inc(fa_beside, 1)

            pool.wait_ge(s_v["last"], 96)
            rounds(0, None)
            with pool.Fori(1, HALVES) as i:
                chain.enter(i - 1, 2)
                rounds(i, i - 1)
                chain.leave(HALVES - 1)
            rounds(None, HALVES - 1)

        @block.scalar
        def _(act):
            def roots(m, lns, i):
                for n in range(lns):
                    for h in range(2):
                        act.wait_ge(var_ready, LN_AT[m] + i * 2 * lns + 2 * n + h + 1)
                        act.activation(stat[h][:, 8:9], stat[h][:, 7:8], ACT.Sqrt, bias=eps).then_inc(std_ready, 1)

            def turned(m, i):
                for h in range(2):
                    tc = m * TILES + 2 * i + h
                    act.wait_ge(tp2_done, tc + 1)
                    act.wait_ge(y_done, tc + 1)
                    act.activation(XTW[h].rearrange("p k n -> p (k n)"), psTP[h][:, :], ACT.Copy)\
                        .then_inc(xt2_ready, 1)

            def products(m, i, queries):
                for h in range(2):
                    t = 2 * i + h
                    act.wait_ge(y_done, 2 + m * TILES + t + 1)
                    if m or later(i):
                        act.wait_ge(tab[h], (m * HALVES + i) * 16)
                    if queries:
                        act.activation(R[:, bass.ds(t, 1), :], psA[h][:, :].unsqueeze(1), ACT.Copy,
                                       scale=float(DK) ** -0.5)
                    act.activation(Y[h], psY[h][:, :], ACT.Copy).then_inc(y_copied, 1)
                for h in range(2):
                    t = 2 * i + h
                    act.wait_ge(y_copied, 2 + m * TILES + t + 1)
                    act.dma_start(table[m][bass.ds(t * P, P), :], Y[h]).then_inc(tab[h], 16)

            def dense(m, lns, keep=None, queries=False):
                def step(i, before):
                    if m == 0:
                        for h in range(2):
                            tc = 2 * i + h
                            act.wait_ge(xt2_ready, tc + 1)
                            act.activation(XN[h].unsqueeze(1), X[:, bass.ds(tc, 1), :], ACT.Copy)\
                                .then_inc(xn_ready, 1)
                    roots(m, lns, i)
                    turned(m, i)
                    if before is not None:
                        products(m, before, queries)
                    if keep is not None:
                        for h in range(2):
                            act.wait_ge(xn_ready, m * TILES + 2 * i + h + 1)
                            act.activation(keep[:, bass.ds(2 * i + h, 1), :], XN[h].unsqueeze(1), ACT.Copy)\
                                .then_inc(kept, 1)

                if m == 0:
                    act.wait_ge(s_x, 16 * 7)
                step(0, None)
                if m == 0:
                    step(1, 0)
                with act.Fori(2 if m == 0 else 1, HALVES) as i:
                    step(i, i - 1)
                products(m, HALVES - 1, queries)

            def beside(q, source, values=False):
                k = SELF[q]
                with act.Fori(0, HALVES) as i:
                    for half in range(2):
                        t = 2 * i + half
                        s = k * TILES + t
                        act.wait_ge(tp_done, 1 + s)
                        act.activation(XS[:, :].unsqueeze(1), source[:, bass.ds(t, 1), :], ACT.Copy)\
                            .then_inc(xs_ready, 1)
                        act.wait_ge(tp_done, 1 + s + 1)
                        act.wait_ge(self_done, 1 + s)
                        act.activation(XT[:, :, :].rearrange("p k n -> p (k n)"), psT[:, :], ACT.Copy)\
                            .then_inc(xt_ready, 1)
                        if q == 0:
                            act.wait_ge(part_ready, t + 1)
                            act.activation(VEC[:, 1, bass.ds(t * GROUP, GROUP)], bank[6 + half][:, 0:GROUP],
                                           ACT.Copy).then_inc(part_copied, 1)

            def turned_onehot(g, j):
                a = g * GROUP + j
                act.wait_ge(a_tp, OH_RING + a + 1)
                act.wait_ge(a_q, a + 1)
                act.activation(OHT[j % 4], psY[j % 2][:, 0:P], ACT.Copy).then_inc(a_oht, 1)

            def scores(i, end):
                for half in range(2):
                    g = 2 * i + half
                    s = SELF[4] * TILES + g
                    for j in range(GROUP):
                        a = g * GROUP + j
                        if not (end and half == 1 and j + 2 >= GROUP):
                            turned_onehot(g, j + 2)
                        act.wait_ge(a_mul, 4 + a + 1)
                        for h in range(HS, H):
                            part = G[:, j % RING, h * DK:(h + 1) * DK]
                            last = act.activation(part, part, ACT.Copy, accum_out=accf[:, bass.ds(a * H + h, 1)])
                        last.then_inc(a_sum, 1)
                        if j == 1:
                            act.wait_ge(tp_done, 1 + s)
                            act.activation(XS[:, :].unsqueeze(1), X[:, bass.ds(g, 1), :], ACT.Copy)\
                                .then_inc(xs_ready, 1)
                        if j == 6:
                            act.wait_ge(tp_done, 1 + s + 1)
                            act.wait_ge(self_done, 1 + s)
                            act.activation(XT[:, :, :].rearrange("p k n -> p (k n)"), psT[:, :], ACT.Copy)\
                                .then_inc(xt_ready, 1)
                        if j == 15:
                            act.wait_ge(self_done, 1 + s + 1)
                            if later(i):
                                act.wait_ge(v_out[half], i * 16)
                            act.activation(VEC[:, half, :], psS[:, :], ACT.Copy).then_inc(v_staged, 1)

            LN_AT = [0, 0, 2 * TILES, 3 * TILES, 3 * TILES]
            dense(0, 0)
            act.wait_ge(s_prep, 1)
            act.dma_start(tile_s_dram, tiles_s).then_inc(s_tile_out, 16)
            beside(0, X)
            dense(1, 2, keep=X)
            dense(2, 1, keep=X)
            beside(2, X)
            dense(3, 0, keep=R)
            beside(3, R)
            dense(4, 1, keep=X, queries=True)
            turned_onehot(0, 0)
            turned_onehot(0, 1)
            over_groups(act, scores, peel=True)

            n = 0
            for dst in (kt, et):
                for a, m in batches:
                    act.wait_ge(m_tp, n + 1)
                    act.activation(dst[:, a * P:(a + m) * P], bank[n % 2][:, 0:m * P], ACT.Copy).then_inc(m_cp, 1)
                    n += 1
            act.wait_ge(m_in, 6)
            for a, m in batches:
                act.activation(et[:, a * P:(a + m) * P], et[:, a * P:(a + m) * P], ACT.Exp).then_inc(m_cp, 1)
            for a, m in batches:
                act.wait_ge(m_tp, n + 1)
                act.activation(scan_order(rf[:, 0:CHUNKS * H])[:, :, a:a + m, :],
                               bank[n % 2][:, 0:m * P].rearrange("p (g j h) -> p j g h", g=m, h=H), ACT.Copy)\
                    .then_inc(m_cp, 1)
                n += 1
            act.wait_ge(m_cp, 4 * BATCHES)

            def weighted(g, j):
                act.wait_ge(g_landed[j % RING],
                            16 * (5 * CHUNKS // RING + g * (GROUP // RING) + j // RING + 1))
                for h in range(HV, H):
                    slot = G[:, j % RING, h * DK:(h + 1) * DK]
                    last = act.activation(slot, slot, ACT.Copy, scale=rf[:, bass.ds((g * GROUP + j) * H + h, 1)])
                last.then_inc(c_mul2, 1)

            for j in range(4):
                weighted(0, j)

            def values(i, end):
                for half in range(2):
                    g = 2 * i + half
                    for j in range(4, GROUP + 4):
                        if not (end and half == 1 and j >= GROUP):
                            weighted(g, j)
                    act.wait_ge(part_ready, GROUPS + g + 1)
                    act.activation(zparts[:, bass.ds(g * GROUP * H, GROUP * H)], bank[6 + half][:, 0:GROUP * H],
                                   ACT.Copy).then_inc(part_copied, 1)

            over_groups(act, values)

            def root(n, h):
                act.wait_ge(var_ready, 4 * TILES + n + h + 1)
                act.activation(stat[h][:, 8:9], stat[h][:, 7:8], ACT.Sqrt, bias=eps).then_inc(std_ready, 1)

            def rounds(a, b, following, n):
                if following is not None:
                    for h in range(2):
                        act.wait_ge(fa_turned, 2 * following + h + 1)
                        act.activation(XTA[h].rearrange("p k n -> p (k n)"), psTP[h][:, :], ACT.Copy)\
                            .then_inc(fa_copied, 1)
                for part in ([b] if b is not None else []) + ([a] if a is not None else []) + \
                            ([b] if b is not None else []):
                    for h in range(2):
                        root(n, h)
                    n = n + 2
                if a is not None:
                    for h in range(2):
                        act.wait_ge(fb_turned, 2 * a + h + 1)
                        act.activation(XTB[h].rearrange("p k n -> p (k n)"), psA[h][:, :], ACT.Copy)\
                            .then_inc(fb_copied, 1)

            rounds(None, None, 0, 0)
            rounds(0, None, 1, 0)
            with act.Fori(1, HALVES - 1) as i:
                rounds(i, i - 1, i + 1, 6 * i - 4)
            rounds(HALVES - 1, HALVES - 2, None, 6 * HALVES - 10)
            rounds(None, HALVES - 1, None, 6 * HALVES - 4)

        @block.tensor
        def _(pe):
            for one in (tp_done, self_done, xt_ready, self_used, v_staged, kept):
                pe.sem_inc(one, 1)
            pe.sem_inc(g_free, RING)
            pe.sem_inc(y_done, 2)
            pe.sem_inc(a_q, 4)
            pe.sem_inc(a_tp, OH_RING)
            pe.sem_inc(xt2_ready, 2)
            pe.sem_inc(y_copied, 2)
            pe.sem_inc(acc_done, 4)
            pe.sem_inc(a_oht, 2)
            pe.sem_inc(a_mul, 4)
            pe.sem_inc(a_sum, RING)
            pe.sem_inc(part_copied, 2)
            pe.wait_ge(s_const, 6)

            def dense(m, *weights, queries=False, W=WA, pairs=(0, HALVES)):
                for w in weights:
                    pe.wait_ge(s_w[w], 16)
                with pe.Fori(*pairs) as i:
                    for h in range(2):
                        tc = m * TILES + 2 * i + h
                        pe.wait_ge(xn_ready, tc + 1)
                        pe.wait_ge(xt2_ready, tc + 1)
                        for k in range(KD):
                            last = pe.transpose(psTP[h][:, k * P:(k + 1) * P],
                                                XN[h][:, k * P:(k + 1) * P], ident[:, :])
                        last.then_inc(tp2_done, 1)
                    for h in range(2):
                        tc = m * TILES + 2 * i + h
                        pe.wait_ge(xt2_ready, 2 + tc + 1)
                        pe.wait_ge(y_copied, tc + 1)
                        if queries:
                            for k in range(KD):
                                pe.matmul(psA[h][:, :], XTW[h][:, k, :], WB[:, k, :],
                                          start=(k == 0), stop=(k == KD - 1))
                        for k in range(KD):
                            last = pe.matmul(psY[h][:, :], XTW[h][:, k, :], W[:, k, :],
                                             start=(k == 0), stop=(k == KD - 1))
                        last.then_inc(y_done, 1)

            def beside_turn(s):
                pe.wait_ge(xs_ready, s + 1)
                pe.wait_ge(xt_ready, 1 + s)
                for k in range(KD):
                    last = pe.transpose(psT[:, k * P:(k + 1) * P], XS[:, k * P:(k + 1) * P], ident[:, :])
                last.then_inc(tp_done, 1)

            def beside_product(s):
                pe.wait_ge(xt_ready, 1 + s + 1)
                pe.wait_ge(self_used, 1 + s)
                for k in range(KD):
                    last = pe.matmul(psS[:, :], XT[:, k, :], WB[:, k, :], start=(k == 0), stop=(k == KD - 1))
                last.then_inc(self_done, 1)

            def sums(q, weights=None):
                if weights:
                    pe.wait_ge(s_w[weights], 16)
                past = CHUNKS if q == 5 else 0
                with pe.Fori(0, HALVES) as i:
                    for half in range(2):
                        g = 2 * i + half
                        if q == 0 or q == 5:
                            pe.wait_ge(part_copied, (GROUPS if q == 5 else 0) + g + 1)
                        for j in range(GROUP):
                            c = g * GROUP + j
                            n = q * CHUNKS + c
                            pe.wait_ge(oh_ready, n + 1)
                            if q == 0:
                                mm = pe.matmul(bank[6 + half][:, j:j + 1], OH[j % OH_RING], ones,
                                               start=True, stop=True)
                            if q == 5:
                                mm = pe.matmul(bank[6 + half][:, j * H:(j + 1) * H], OH[j % OH_RING],
                                               rf[:, bass.ds(c * H, H)], start=True, stop=True)
                                pe.wait_ge(c_mul, c + 1)
                                pe.wait_ge(c_mul2, c + 1)
                            else:
                                pe.wait_ge(g_landed[j % RING],
                                           16 * (q * CHUNKS // RING + g * (GROUP // RING) + j // RING + 1))
                            if (q == 0 or q == 5) and j == GROUP - 1:
                                mm.then_inc(part_ready, 1)
                            pe.wait_ge(acc_done, n + 1 - past)
                            pe.matmul(psR[j % 4][:, :], OH[j % OH_RING], G[:, j % RING, :],
                                      start=True, stop=True).then_inc(g_free, 1)
                            if q in SELF and j == 3:
                                beside_turn(SELF[q] * TILES + g)
                            if q in SELF and j == 11:
                                beside_product(SELF[q] * TILES + g)

            pe.wait_ge(s_cnt, 1)
            pe.matmul(psD[:, 0:NT], OHX[:, 0, :], count[:, 0:NT], start=True, stop=True).then_inc(s_tot, 1)
            dense(0, "wn0", pairs=(0, 8))
            pe.wait_ge(s_cnt, 2)
            pe.matmul(psD[:, 0:NT], OHX[:, 0, :], count[:, 0:NT], start=True, stop=True)
            pe.matmul(psD[:, 32:32 + NT], OHX[:, 1, :], count[:, 0:NT], start=True, stop=True).then_inc(s_tot, 1)
            dense(0, pairs=(8, HALVES))
            sums(0, "ws0")
            dense(1, "w1", W=WB)
            sums(1)
            dense(2, "wn2a")
            sums(2, "ws2a")
            dense(3, "wn2b")
            sums(3, "ws2b")
            dense(4, "wk", "wq", queries=True)
            pe.wait_ge(s_w["wv"], 16)
            def turn(g, j):
                a = g * GROUP + j
                pe.wait_ge(oh_ready, 4 * CHUNKS + a + 1)
                pe.wait_ge(a_oht, a + 1)
                pe.transpose(psY[j % 2][:, 0:P], OH[j % OH_RING], ident[:, :]).then_inc(a_tp, 1)

            def scores(i, end):
                for half in range(2):
                    g = 2 * i + half
                    tiles = regs(nc, pe, tile_d, g * GROUP, GROUP, TILES - 1)
                    for j in range(GROUP):
                        a = g * GROUP + j
                        if not (end and half == 1 and j + 2 >= GROUP):
                            turn(g, j + 2)
                        pe.wait_ge(a_oht, 2 + a + 1)
                        pe.wait_ge(a_mul, a + 1)
                        pe.matmul(psK[j % 4][:, :].unsqueeze(1), OHT[j % 4], R[:, bass.ds(tiles[j], 1), :],
                                  start=True, stop=True).then_inc(a_q, 1)
                        if j == 4:
                            beside_turn(3 * TILES + g)
                        if j == 8:
                            pe.wait_ge(v_staged, 1 + g)
                            pe.wait_ge(xt_ready, 1 + 3 * TILES + g + 1)
                        if j >= 8 and j % 2 == 0:
                            k = (j - 8) // 2
                            mm = pe.matmul(psS[:, :], XT[:, k, :], WB[:, k, :],
                                           start=(k == 0), stop=(k == KD - 1))
                            if k == KD - 1:
                                mm.then_inc(self_done, 1)

            turn(0, 0)
            turn(0, 1)
            over_groups(pe, scores)

            n = 0

            def turns(src, a, m):
                for b in range(m):
                    last = pe.transpose(bank[n % 2][:, b * P:(b + 1) * P], src[:, (a + b) * P:(a + b + 1) * P],
                                        ident[:, :])
                last.then_inc(m_tp, 1)

            pe.wait_ge(a_mul, 4 + CHUNKS)
            for step, src in enumerate((key8, ep)):
                pe.wait_ge(m_in, step + 1)
                for a, m in batches:
                    if n >= 2:
                        pe.wait_ge(m_cp, n - 1)
                    turns(src, a, m)
                    n += 1
            pe.wait_ge(m_in, 3)
            pe.wait_ge(m_cp, 2 * BATCHES)
            for k in range(4):
                pe.matmul(bank[0][0:1, k * P:(k + 1) * P], cols[:, k:k + 1], ident[:, :], start=True, stop=True)
            pe.matmul(bank[1][0:1, 0:P], cols[:, 4:5], ident[:, :], start=True, stop=True).then_inc(m_rows, 1)
            pe.wait_ge(m_in, 4)
            pe.matmul(psT[:, 0:1], carried[:, 0:P], ones[0:1, :], start=True, stop=True)
            pe.matmul(psT[:, 1:2], carried[:, P:2 * P], ones[0:1, :], start=True, stop=True).then_inc(m_rows, 1)
            for k, (a, m) in enumerate(batches):
                pe.wait_ge(m_cp, 2 * BATCHES + k + 1)
                if k >= 2:
                    pe.wait_ge(m_cp, 3 * BATCHES + k - 1)
                turns(et, a, m)
                n += 1
            pe.wait_ge(m_cp, 4 * BATCHES)
            sums(5)
            pe.wait_ge(s_w["wo"], 16)
            pe.wait_ge(s_w["ffn"], 32)

            def rounds(a, b, following):
                if following is not None:
                    for h in range(2):
                        pe.wait_ge(fa_in, 2 * following + h + 1)
                        for k in range(KD):
                            last = pe.transpose(psTP[h][:, k * P:(k + 1) * P], AN[h][:, k * P:(k + 1) * P],
                                                ident[:, :])
                        last.then_inc(fa_turned, 1)
                if b is not None:
                    for h in range(2):
                        pe.wait_ge(fb_relu, 2 * b + h + 1)
                        pe.matmul(psA[h][:, :], HID[h], WB[:, 1, :], start=True, stop=True).then_inc(fb_out, 1)
                if following is not None:
                    for h in range(2):
                        pe.wait_ge(fa_copied, 2 * following + h + 1)
                        for k in range(KD):
                            last = pe.matmul(psY[h][:, :], XTA[h][:, k, :], WA[:, k, :],
                                             start=(k == 0), stop=(k == KD - 1))
                        last.then_inc(fa_out, 1)
                if a is not None:
                    for h in range(2):
                        pe.wait_ge(fa_scaled, 2 * a + h + 1)
                        for k in range(KD):
                            last = pe.transpose(psA[h][:, k * P:(k + 1) * P], XP[h][:, k * P:(k + 1) * P],
                                                ident[:, :])
                        last.then_inc(fb_turned, 1)
                    for h in range(2):
                        pe.wait_ge(fb_copied, 2 * a + h + 1)
                        for k in range(KD):
                            last = pe.matmul(bank[6 + h][:, 0:P], WB[:, 0, k * P:(k + 1) * P], XTB[h][:, k, :],
                                             start=(k == 0), stop=(k == KD - 1))
                        last.then_inc(fb_hidden, 1)

            rounds(None, None, 0)
            rounds(0, None, 1)
            with pe.Fori(1, HALVES - 1) as i:
                rounds(i, i - 1, i + 1)
            rounds(HALVES - 1, HALVES - 2, None)
            rounds(None, HALVES - 1, None)

        @block.vector
        def _(dve):
            chain = Chain(dve, dve_chain)
            then = chain.then
            lns = [0]

            dst_i, src_i = rf[:, 0:NAT].bitcast(I32), rf[:, NAT:2 * NAT].bitcast(I32)
            w_f = rf[:, 2 * NAT:3 * NAT]
            tmp_at = [3 * NAT]

            def tmp(n):
                tmp_at[0] += n
                assert tmp_at[0] <= 13000
                return rf[:, tmp_at[0] - n:tmp_at[0]]

            dst_f, lo_f, hi_f, pos = (tmp(NAT) for _ in range(4))
            lo_i, hi_i, pos_lo, pos_hi = (tmp(NAT).bitcast(I32) for _ in range(4))
            zeros = tmp(NAT)
            mask = tmp(NAT)
            cidx = tmp(CHUNKS)
            tile_f, off_f, hop = tmp(CHUNKS), tmp(CHUNKS), tmp(CHUNKS)
            start, cnt, full_f, chunk0, first, step_ = (tmp(32) for _ in range(6))
            full_i = tmp(32).bitcast(I32)
            place = tmp(32)
            pre = accf[:, 0:NT * NAT].rearrange("p (t c) -> p t c", t=NT)

            def chunks_of():
                then(dve.tensor_scalar(full_f[:, 0:NT], cnt[:, 0:NT], float(P - 1), None, ALU.add))
                then(dve.tensor_copy(full_i[:, 0:NT], full_f[:, 0:NT]))
                then(dve.tensor_scalar(full_i[:, 0:NT], full_i[:, 0:NT], 7, None, ALU.logical_shift_right))
                then(dve.tensor_copy(full_f[:, 0:NT], full_i[:, 0:NT]))
                then(dve.tensor_tensor_scan(chunk0[:, 1:NT + 1], full_f[:, 0:NT], zeros[:, 0:NT], 0.0,
                                            ALU.add, ALU.add))

            then(dve.memset(zeros, 0.0))
            then(dve.memset(chunk0[:, 0:1], 0.0))
            then(dve.memset(start[:, 0:1], 0.0))
            dve.wait_ge(s_const, 6)
            for a in range(0, CHUNKS, P):
                m = min(P, CHUNKS - a)
                dve.tensor_scalar(cidx[:, a:a + m], iota[:, 0:m], float(a), None, ALU.add)
            dve.wait_ge(s_nat, 48)
            then(dve.tensor_copy(dst_f, dst_i))
            for t in range(NT):
                last = dve.tensor_scalar(pre[:, t, :], dst_f, float(P * (t + 1)), None, ALU.is_lt)
            then(last)
            dve.tensor_reduce(count[:, 0:NT], pre, AX.X, ALU.add).then_inc(s_cnt, 1)
            dve.wait_ge(s_tot, 1)
            then(dve.tensor_copy(start[:, 1:NT + 1], psD[:, 0:NT]))
            then(dve.tensor_tensor(cnt[:, 0:NT], start[:, 1:NT + 1], start[:, 0:NT], ALU.subtract))
            chunks_of()
            then(dve.scalar_tensor_tensor(first[:, 0:NT + 1], chunk0[:, 0:NT + 1], -float(P),
                                          start[:, 0:NT + 1], ALU.mult, ALU.add))
            then(dve.tensor_tensor(step_[:, 0:NT], first[:, 1:NT + 1], first[:, 0:NT], ALU.subtract))
            dve.tensor_scalar(off_f, cidx, float(P), None, ALU.mult)
            then(dve.memset(tile_f, 0.0))
            for t in range(NT):
                dve.tensor_scalar(hop, cidx, chunk0[:, t + 1:t + 2], step_[:, t:t + 1], ALU.is_ge, ALU.mult)
                then(dve.scalar_tensor_tensor(tile_f, cidx, chunk0[:, t + 1:t + 2], tile_f, ALU.is_ge, ALU.add))
                then(dve.tensor_tensor(off_f, off_f, hop, ALU.add))
            then(dve.tensor_scalar(off_f, off_f, float(E), None, ALU.min))
            dve.tensor_copy(tile_d[:, :], tile_f)
            dve.tensor_scalar(t128, tile_f, float(P), None, ALU.mult)
            then(dve.tensor_copy(row2[:, :], off_f))
            dve.sem_inc(s_rows, 1)
            then(dve.tensor_scalar(full_f[:, 0:TILES], chunk0[:, 0:TILES], float(CHUNKS - 1), None, ALU.min))
            then(dve.tensor_copy(chunk0_i[:, 0:TILES], full_f[:, 0:TILES]))

            dve.tensor_scalar(hi_i, src_i, 7, None, ALU.logical_shift_right)
            then(dve.tensor_scalar(lo_i, src_i, P - 1, None, ALU.bitwise_and))
            dve.tensor_copy(hi_f, hi_i)
            then(dve.tensor_copy(lo_f, lo_i))
            for b in range(NT):
                then(dve.tensor_scalar(mask, hi_f, float(b), None, ALU.is_equal))
                then(dve.tensor_tensor_scan(pre[:, b, :], mask, zeros, 0.0, ALU.add, ALU.add))
            dve.tensor_copy(count[:, 0:NT].unsqueeze(2), pre[:, :, NAT - 1:NAT]).then_inc(s_cnt, 1)
            dve.wait_ge(s_tot, 2)
            dve.tensor_copy(cnt[:, 0:NT], psD[:, 0:NT])
            then(dve.tensor_copy(place[:, 0:NT], psD[:, 32:32 + NT]))
            chunks_of()
            then(dve.scalar_tensor_tensor(place[:, 0:NT], chunk0[:, 0:NT], float(P), place[:, 0:NT],
                                          ALU.mult, ALU.add))
            then(dve.tensor_scalar(place[:, 0:NT], place[:, 0:NT], -1.0, None, ALU.add))
            then(dve.memset(tile_f, 0.0))
            for t in range(NT):
                then(dve.scalar_tensor_tensor(tile_f, cidx, chunk0[:, t + 1:t + 2], tile_f, ALU.is_ge, ALU.add))
            then(dve.tensor_tensor(pre, pre, place[:, 0:NT].unsqueeze(2).broadcast_to([P, NT, NAT]), ALU.add))
            for b in range(NT):
                last = dve.scalar_tensor_tensor(pre[:, b, :], hi_f, float(b), pre[:, b, :], ALU.is_equal, ALU.mult)
            then(last)
            then(dve.tensor_reduce(pos, pre.rearrange("p t c -> p c t"), AX.X, ALU.add))
            pads = P * NAT - E
            then(dve.tensor_scalar(mask, cidx[:, 0:NAT], float(CHUNKS * P - (NAT - pads)), None, ALU.add))
            then(dve.scalar_tensor_tensor(mask, hi_f, float(NT), mask, ALU.is_equal, ALU.mult))
            then(dve.tensor_tensor(pos, pos, mask, ALU.add))
            then(dve.tensor_copy(lo_i, pos))
            dve.tensor_scalar(pos_lo, lo_i, P - 1, None, ALU.bitwise_and)
            then(dve.tensor_scalar(pos_hi, lo_i, 7, None, ALU.logical_shift_right))
            dve.tensor_copy(mask, pos_lo)
            then(dve.tensor_copy(pos, pos_hi))
            then(dve.scalar_tensor_tensor(pos, mask, float(PITCH), pos, ALU.mult, ALU.add))
            then(dve.tensor_copy(tiles_s, tile_f))
            dve.wait_ge(y_done, 2 + TILES)
            dve.tensor_copy(nrec[:, :, 0:1], lo_f.unsqueeze(2))
            dve.tensor_copy(nrec[:, :, 1:2], dst_f.unsqueeze(2))
            dve.tensor_copy(nrec[:, :, 2:3], w_f.unsqueeze(2))
            dve.memset(nrec[:, :, 3:4], 0.0)
            then(dve.tensor_copy(npos, pos))
            dve.sem_inc(s_prep, 1)

            def onehot(q, g, j, key, weight=None):
                n = q * CHUNKS + g * GROUP + j
                c = g * GROUP + j
                if q == 4:
                    dve.wait_ge(a_tp, c + 1)
                else:
                    dve.wait_ge(g_free, RING - OH_RING + n + 1)
                if q == 0 and j % GROUP == 0:
                    dve.wait_ge(s_key, g + j // GROUP + 1)
                args = (key(c), weight(c), ALU.is_equal, ALU.mult) if weight else (key(c), None, ALU.is_equal)
                dve.tensor_scalar(OH[j % OH_RING], iota[:, :], *args).then_inc(oh_ready, 1)

            def weighted(g, j):
                dve.wait_ge(g_landed[j % RING],
                            16 * (5 * CHUNKS // RING + g * (GROUP // RING) + j // RING + 1))
                slot = G[:, j % RING, 0:HV * DK].rearrange("p (h k) -> p h k", h=HV)
                dve.tensor_tensor(slot, slot, rf[:, bass.ds((g * GROUP + j) * H, HV)].unsqueeze(2)
                                  .broadcast_to([P, HV, DK]), ALU.mult).then_inc(c_mul, 1)

            def sums(q, key, weight=None, bias=None, row=None):
                past = CHUNKS if q == 5 else 0
                if q == 0:
                    dve.wait_ge(s_blank_out, 16)
                    dve.wait_ge(s_tile_out, 16)
                    then(dve.memset(accf, 0.0))
                else:
                    dve.wait_ge(cleared, HALVES * (q if q < 4 else 4))
                for j in range(3):
                    onehot(q, 0, j, key, weight)
                if q == 5:
                    for j in range(2):
                        weighted(0, j)

                def groups(i, end):
                    for half in range(2):
                        g = 2 * i + half
                        tiles = regs(nc, dve, row, g * GROUP, GROUP, TILES - 1)
                        ahead = lambda j: not (end and half == 1 and j >= GROUP)
                        for j in range(GROUP):
                            n = q * CHUNKS + g * GROUP + j
                            if ahead(j + 3):
                                onehot(q, g, j + 3, key, weight)
                            if q == 5 and ahead(j + 2):
                                weighted(g, j + 2)
                            dve.wait_ge(g_free, RING + n + 1)
                            dve.wait_ge(acc_done, 4 + n - past)
                            slot = ACC[:, bass.ds(tiles[j], 1), :]
                            dve.tensor_tensor(slot, slot, psR[j % 4][:, :].unsqueeze(1), ALU.add)\
                                .then_inc(acc_done, 1)
                            if q in SELF and j == 14:
                                s = SELF[q] * TILES + g
                                dve.wait_ge(self_done, 1 + s + 1)
                                dve.tensor_tensor(R[:, bass.ds(g, 1), :], psS[:, :].unsqueeze(1),
                                                  bias.unsqueeze(1), ALU.add).then_inc(self_used, 1)

                over_groups(dve, groups)
                dve.wait_ge(acc_done, 4 + (q + 1) * CHUNKS - past)
                if q in SELF:
                    dve.wait_ge(self_used, 1 + (SELF[q] + 1) * TILES)
                if q == 0:
                    degrees()
                dve.sem_inc(agg_done, 1)

            def degrees():
                dve.wait_ge(part_copied, 2 + GROUPS)
                same, total = G[:, 6, 0:CHUNKS], G[:, 7, 0:CHUNKS]
                dve.memset(same[:, CHUNKS - 1:CHUNKS], 0.0)
                then(dve.tensor_tensor(same[:, 0:CHUNKS - 1], tile_d[:, 1:CHUNKS], tile_d[:, 0:CHUNKS - 1],
                                       ALU.is_equal))
                then(dve.tensor_tensor_scan(total[:, ::-1], same[:, ::-1], t128[:, ::-1], 0.0, ALU.mult, ALU.add))
                firsts = regs(nc, dve, chunk0_i, 0, TILES, CHUNKS - 1)
                for t in range(TILES):
                    last = dve.tensor_copy(inv[:, t:t + 1], total[:, bass.ds(firsts[t], 1)])
                then(last)
                then(dve.tensor_scalar(inv[:, :], inv[:, :], 1.0, None, ALU.max))
                then(dve.reciprocal(inv[:, :], inv[:, :]))

            lag = chain.lag

            def stats(at, of=T1):
                for h in range(2):
                    lag(dve.bn_stats(stat[h][:, 0:6], of[h]))
                chain.settle()
                for h in range(2):
                    dve.sem_inc(s_tick2, 1)
                    dve.bn_aggr(stat[h][:, 6:8], stat[h][:, 0:6]).then_inc(var_ready, 1)
                for h in range(2):
                    dve.wait_ge(std_ready, at + h + 1)
                    lag(dve.reciprocal(stat[h][:, 9:10], stat[h][:, 8:9]))

            def normed(h, dst, of=T1):
                return dve.tensor_scalar(dst, of[h], stat[h][:, 6:7], stat[h][:, 9:10], ALU.subtract, ALU.mult)

            def dense(m, steps, per, vectors, body):
                if vectors:
                    dve.wait_ge(s_v[vectors], 32)
                with dve.Fori(0, HALVES) as i:
                    chain.enter(i, steps)
                    body(2 * i, lns[0] + i * 2 * per, m)
                    dve.wait_ge(xn_ready, m * TILES + 2 * i + 2)
                    chain.leave(HALVES)
                lns[0] += per * TILES
                dve.wait_ge(y_copied, 2 + (m + 1) * TILES)
                dve.wait_ge(kept, 1 + m * TILES)
                dve.sem_inc(d_done, 1)

            def free(h, m, t):
                dve.wait_ge(xt2_ready, m * TILES + t + h + 1)
                dve.wait_ge(kept, 1 + (m - 1) * TILES + t)

            def tile_of(buf, t):
                return buf[:, bass.ds(t, 1), :]

            t1 = [T1[h].unsqueeze(1) for h in range(2)]
            by_dst = lambda c: recf[:, bass.ds(c, 1), 1]

            dve.wait_ge(s_v["sum0"], 32)
            sums(0, by_dst, bias=VEC[:, 0, :], row=tile_d)

            def mean_and_self(t):
                for h in range(2):
                    lag(dve.scalar_tensor_tensor(t1[h], tile_of(ACC, t + h), inv[:, bass.ds(t + h, 1)],
                                                 tile_of(R, t + h), ALU.mult, ALU.add))

            def layer0(t, at, m):
                mean_and_self(t)
                stats(at)
                dve.sem_inc(acc_read, 1)
                for h in range(2):
                    lag(normed(h, T2[h]))
                for h in range(2):
                    lag(dve.tensor_tensor(T2[h], T2[h], VEC[:, 0, :], ALU.mult))
                for h in range(2):
                    lag(dve.tensor_tensor(T1[h], T2[h], VEC[:, 1, :], ALU.add))
                for h in range(2):
                    lag(dve.tensor_scalar(T2[h], T1[h], 0.0, alpha, ALU.min, ALU.mult))
                for h in range(2):
                    lag(dve.scalar_tensor_tensor(T1[h], T1[h], 0.0, T2[h], ALU.max, ALU.add))
                for h in range(2):
                    lag(dve.scalar_tensor_tensor(t1[h], tile_of(X, t + h), 2.0, t1[h], ALU.mult, ALU.add))
                stats(at + 2)
                for h in range(2):
                    free(h, m, t)
                    chain.settle()
                    normed(h, XN[h]).then_inc(xn_ready, 1)

            dense(1, 22, 2, "norm0", layer0)

            dve.wait_ge(s_srcrec, 32)
            src_rec = rf[:, 0:CHUNKS * 4].rearrange("p (c f) -> p c f", f=4)
            then(dve.tensor_copy(rf[:, CHUNKS * 4:CHUNKS * 5].bitcast(I32).unsqueeze(2), src_rec[:, :, 1:2]))
            dve.sem_inc(s_srcidx, 1)
            sums(1, lambda c: src_rec[:, bass.ds(c, 1), 0], weight=lambda c: src_rec[:, bass.ds(c, 1), 2],
                 row=row2)

            def layer1(t, at, m):
                for h in range(2):
                    lag(dve.tensor_tensor(t1[h], tile_of(ACC, t + h), VEC[:, 0, :].unsqueeze(1), ALU.add))
                for h in range(2):
                    lag(dve.tensor_tensor(t1[h], tile_of(X, t + h), t1[h], ALU.add))
                stats(at)
                dve.sem_inc(acc_read, 1)
                for h in range(2):
                    free(h, m, t)
                    chain.settle()
                    normed(h, XN[h]).then_inc(xn_ready, 1)

            dense(2, 8, 1, "l1", layer1)

            sums(2, by_dst, bias=VEC[:, 1, :], row=tile_d)

            def layer2a(t, at, m):
                mean_and_self(t)
                for h in range(2):
                    free(h, m, t)
                    chain.settle()
                    dve.tensor_scalar(XN[h], T1[h], 0.0, None, ALU.max).then_inc(xn_ready, 1)
                dve.sem_inc(acc_read, 1)

            dense(3, 2, 0, None, layer2a)
            dve.wait_ge(s_v["l2b"], 16)
            sums(3, by_dst, bias=VEC[:, 0, :], row=tile_d)

            def layer2b(t, at, m):
                mean_and_self(t)
                for h in range(2):
                    lag(dve.scalar_tensor_tensor(t1[h], t1[h], 0.0, tile_of(X, t + h), ALU.max, ALU.add))
                stats(at)
                for h in range(2):
                    free(h, m, t)
                    chain.settle()
                    normed(h, XN[h]).then_inc(xn_ready, 1)

            dense(4, 8, 1, None, layer2b)

            raw = accf[:, 0:CHUNKS * H].rearrange("p (c h) -> p c h", h=H)
            okay, target = accf[:, 10000:10000 + CHUNKS], accf[:, 10416:10416 + CHUNKS]
            keys = recf[:, :, 1]
            then(dve.tensor_copy(target, tile_d[:, :]))
            then(dve.scalar_tensor_tensor(target, target, float(P), keys, ALU.mult, ALU.add))
            then(dve.tensor_scalar(okay, keys, 0.0, None, ALU.is_ge))
            then(dve.scalar_tensor_tensor(okay, keys, float(P), okay, ALU.is_lt, ALU.mult))
            then(dve.tensor_scalar(okay, okay, 1.0, FAR, ALU.subtract, ALU.mult))
            by_block = lambda v: v.rearrange("p (j g) -> p j g", g=GROUPS).unsqueeze(3)\
                .broadcast_to([P, GROUP, GROUPS, H])
            then(dve.tensor_copy(turn_order(key8), by_block(target)))
            dve.sem_inc(m_in, 1)
            for j in range(4):
                onehot(4, 0, j, by_dst)

            def product(g, j):
                dve.wait_ge(g_landed[j % RING],
                            16 * (4 * CHUNKS // RING + g * (GROUP // RING) + j // RING + 1))
                dve.wait_ge(a_q, 4 + g * GROUP + j + 1)
                dve.tensor_tensor(G[:, j % RING, :], G[:, j % RING, :], psK[j % 4][:, :], ALU.mult)\
                    .then_inc(a_mul, 1)

            def scores(i, end):
                for half in range(2):
                    g = 2 * i + half
                    for j in range(GROUP):
                        a = g * GROUP + j
                        if not (end and half == 1 and j + 4 >= GROUP):
                            onehot(4, g, j + 4, by_dst)
                        if not (end and half == 1 and j + 1 >= GROUP):
                            product(g, j + 1)
                        dve.wait_ge(a_mul, 4 + a + 1)
                        dve.tensor_reduce(raw[:, bass.ds(a, 1), 0:HS].rearrange("p a h -> p (a h)"),
                                          G[:, j % RING, 0:HS * DK].rearrange("p (h k) -> p h k", h=HS),
                                          AX.X, ALU.add).then_inc(g_free, 1)

            product(0, 0)
            over_groups(dve, scores)
            dve.wait_ge(a_sum, RING + CHUNKS)
            dve.wait_ge(g_free, RING + 5 * CHUNKS)

            dve.wait_ge(a_q, 4 + CHUNKS)
            then(dve.tensor_tensor(turn_order(ep), scan_order(accf[:, 0:CHUNKS * H]), by_block(okay), ALU.add))
            dve.sem_inc(m_in, 1)
            L = CHUNKS * H
            gate = accf[:, 0:L + 1]
            dve.memset(gate[:, 0:1], 0.0)
            dve.memset(gate[:, L:L + 1], 0.0)
            dve.wait_ge(m_cp, BATCHES)
            then(dve.tensor_tensor(gate[:, 1:L], kt[:, 1:L], kt[:, 0:L - 1], ALU.is_equal))
            then(dve.tensor_scalar(gate[:, 1:L], gate[:, 1:L], 1.0, FAR, ALU.subtract, ALU.mult))
            dve.tensor_copy(cols[:, 0:1], kt[:, 0:1])
            dve.tensor_copy(cols[:, 1:2], kt[:, L - 1:L])
            dve.tensor_reduce(cols[:, 3:4], gate[:, 1:L], AX.X, ALU.min)
            dve.wait_ge(m_cp, 2 * BATCHES)
            then(dve.tensor_tensor_scan(scratch, gate[:, 0:L], et, -FAR, ALU.add, ALU.max))
            then(dve.tensor_copy(cols[:, 2:3], scratch[:, L - 1:L]))
            then(dve.tensor_tensor_scan(scratch[:, ::-1], gate[:, L:0:-1], et[:, ::-1], -FAR, ALU.add, ALU.max))
            then(dve.tensor_copy(cols[:, 4:5], scratch[:, 0:1]))
            dve.sem_inc(m_in, 1)
            rows, first, link = G[0:1, 0, :], G[0:1, 1, 0:P], G[0:1, 1, P:2 * P]
            step = [G[0:1, 2, k * P:(k + 1) * P] for k in range(4)]
            then(dve.memset(G[0:1, 2, :], -FAR))
            dve.wait_ge(m_rows, 1)
            dve.tensor_copy(rows, bank[0][0:1, :])
            then(dve.tensor_copy(first, bank[1][0:1, 0:P]))
            then(dve.tensor_tensor(link[:, H:P], rows[:, H:P], rows[:, P:2 * P - H], ALU.is_equal))
            then(dve.tensor_scalar(link[:, H:P], link[:, H:P], 1.0, FAR, ALU.subtract, ALU.mult))
            dve.tensor_tensor(step[0][:, H:P], rows[:, 3 * P:4 * P - H], link[:, H:P], ALU.add)
            dve.tensor_tensor(step[1][:, H:P], rows[:, 2 * P:3 * P - H], link[:, H:P], ALU.add)
            dve.tensor_tensor(step[2][:, 0:P - H], rows[:, 3 * P + H:4 * P], link[:, H:P], ALU.add)
            then(dve.tensor_tensor(step[3][:, 0:P - H], first[:, H:P], link[:, H:P], ALU.add))
            for h in range(H):
                at = lambda v: v.rearrange("p (j h) -> p j h", h=H)[:, :, h]
                back = lambda v: v.rearrange("p (j h) -> p j h", h=H)[:, ::-1, h]
                dve.tensor_tensor_scan(at(carried[:, 0:P]), at(step[0]), at(step[1]), -FAR, ALU.add, ALU.max)
                last = dve.tensor_tensor_scan(back(carried[:, P:2 * P]), back(step[2]), back(step[3]), -FAR,
                                              ALU.add, ALU.max)
            then(last)
            dve.sem_inc(m_in, 1)
            dve.wait_ge(m_rows, 2)
            then(dve.tensor_copy(carry, psT[:, 0:2]))
            then(dve.tensor_tensor_scan(scratch, gate[:, 0:L], et, carry[:, 0:1], ALU.add, ALU.max))
            then(dve.tensor_tensor_scan(kt[:, ::-1], gate[:, L:0:-1], scratch[:, ::-1], carry[:, 1:2],
                                        ALU.add, ALU.max))
            dve.sem_inc(m_in, 1)
            then(dve.tensor_tensor(et, et, kt, ALU.subtract))
            dve.sem_inc(m_in, 1)
            dve.wait_ge(m_cp, 4 * BATCHES)
            sums(5, by_dst, row=tile_d)
            z = rf[:, 9984:9984 + TILES * H].rearrange("p (t h) -> p t h", h=H)
            zf = rf[:, 9984:9984 + TILES * H]
            zp = zparts.rearrange("p (c h) -> p c h", h=H)
            total = rf[:, 0:CHUNKS * H].rearrange("p (c h) -> p c h", h=H)
            same = XS[:, 0:CHUNKS]
            dve.wait_ge(part_copied, 2 + 2 * GROUPS)
            dve.memset(same[:, CHUNKS - 1:CHUNKS], 0.0)
            then(dve.tensor_tensor(same[:, 0:CHUNKS - 1], tile_d[:, 1:CHUNKS], tile_d[:, 0:CHUNKS - 1], ALU.is_equal))
            for h in range(H):
                last = dve.tensor_tensor_scan(total[:, ::-1, h], same[:, ::-1], zp[:, ::-1, h], 0.0,
                                              ALU.mult, ALU.add)
            then(last)
            firsts = regs(nc, dve, chunk0_i, 0, TILES, CHUNKS - 1)
            for t in range(TILES):
                last = dve.tensor_copy(z[:, t:t + 1, :], total[:, bass.ds(firsts[t], 1), :])
            then(last)
            then(dve.tensor_scalar(zf, zf, 1e-30, None, ALU.max))
            then(dve.reciprocal(zf, zf))
            dve.wait_ge(s_v["last"], 96)

            def rounds(a, b, following, n):
                n = lns[0] + n
                if a is not None:
                    for h in range(2):
                        dve.wait_ge(fa_out, 2 * a + h + 1)
                        lag(dve.tensor_tensor(T1A[h].unsqueeze(1), psY[h][:, :].unsqueeze(1),
                                              tile_of(X, 2 * a + h), ALU.add))
                    chain.settle()
                if following is not None:
                    for h in range(2):
                        t = 2 * following + h
                        dve.tensor_tensor(AN[h].rearrange("p (h k) -> p h k", h=H),
                                          ACC[:, bass.ds(t, 1), :].rearrange("p a (h k) -> p (a h) k", h=H),
                                          rf[:, bass.ds(t * H + 9984, H)].unsqueeze(2).broadcast_to([P, H, DK]),
                                          ALU.mult).then_inc(fa_in, 1)
                if b is not None:
                    for h in range(2):
                        dve.wait_ge(fb_hidden, 2 * b + h + 1)
                        dve.tensor_scalar(HID[h], bank[6 + h][:, 0:P], small[:, 29:30], 0.0, ALU.add, ALU.max)\
                            .then_inc(fb_relu, 1)
                    for h in range(2):
                        dve.wait_ge(fb_out, 2 * b + h + 1)
                        dve.wait_ge(fa_beside, 2 * b + h + 1)
                        lag(dve.tensor_tensor(TB[h], psA[h][:, :], XB[h], ALU.add))
                    stats(n, TB)
                    chain.settle()
                    for h in range(2):
                        normed(h, TB[h], TB).then_inc(fb_normed, 1)
                    n = n + 2
                if a is not None:
                    if b is not None:
                        dve.wait_ge(fb_normed, 2 * b + 2)
                    stats(n, T1A)
                    chain.settle()
                    for h in range(2):
                        lag(normed(h, T2A[h], T1A))
                    for h in range(2):
                        lag(dve.tensor_tensor(T2A[h], T2A[h], vec[0], ALU.mult))
                    chain.settle()
                    for h in range(2):
                        dve.tensor_tensor(XP[h], T2A[h], vec[1], ALU.add).then_inc(fa_scaled, 1)
                    n = n + 2
                if b is not None:
                    for h in range(2):
                        dve.wait_ge(fb_scaled, 2 * b + h + 1)
                        lag(dve.tensor_tensor(TB[h].unsqueeze(1), TB[h].unsqueeze(1), tile_of(X, 2 * b + h), ALU.add))
                    stats(n, TB)
                    chain.settle()
                    for h in range(2):
                        normed(h, tile_of(X, 2 * b + h), [v.unsqueeze(1) for v in TB]).then_inc(f_out, 1)

            rounds(None, None, 0, 0)
            rounds(0, None, 1, 0)
            steps = 2 * (5 + 3 + 3)
            with dve.Fori(1, HALVES - 1) as i:
                chain.enter(i - 1, steps)
                rounds(i, i - 1, i + 1, 6 * i - 4)
                chain.leave(HALVES - 2)
            rounds(HALVES - 1, HALVES - 2, None, 6 * HALVES - 10)
            rounds(None, HALVES - 1, None, 6 * HALVES - 4)


def kernel(**inputs):
    import numpy as _np
    import concourse.bacc as _bacc
    from concourse import mybir as _mybir
    from concourse.bass_utils import run_bass_kernel_spmd as _run

    get = {k: _np.asarray(v) for k, v in inputs.items()}
    src, dst, w = get["src"], get["dst"], get["edge_weight"]
    none = _np.int32(NT * P)
    pad = P * NAT - E
    edges = _np.stack([_np.concatenate([src, _np.full(P, none, src.dtype)]),
                       _np.concatenate([dst, _np.full(P, none, dst.dtype)])], axis=1)
    arrays = {
        "x": get["x"],
        "edges": edges,
        "src_nat": _np.concatenate([src, _np.full(pad, none, src.dtype)]).reshape(P, NAT),
        "dst_nat": _np.concatenate([dst, _np.full(pad, none, dst.dtype)]).reshape(P, NAT),
        "w_nat": _np.concatenate([w, _np.zeros(pad, w.dtype)]).reshape(P, NAT),
    }
    names = {
        "l0_ws": "L0_gnn_W_self", "l0_bs": "L0_gnn_b_self", "l0_wn": "L0_gnn_W_neigh",
        "l0_g": "L0_gnn_gamma", "l0_b": "L0_gnn_beta", "l0_alpha": "L0_gnn_alpha",
        "l1_w": "L1_gnn_weight", "l1_b": "L1_gnn_bias",
        "l2_ws1": "L2_gnn_W_self1", "l2_wn1": "L2_gnn_W_neigh1", "l2_b1": "L2_gnn_b1",
        "l2_ws2": "L2_gnn_W_self2", "l2_wn2": "L2_gnn_W_neigh2", "l2_b2": "L2_gnn_b2",
        "wq": "L3_gnn_Wq", "wk": "L3_gnn_Wk", "wv": "L3_gnn_Wv", "wo": "L3_gnn_Wo",
        "ln1_g": "L3_gnn_ln1_g", "ln1_b": "L3_gnn_ln1_b", "ln2_g": "L3_gnn_ln2_g", "ln2_b": "L3_gnn_ln2_b",
        "w1": "L3_gnn_W1", "b1": "L3_gnn_b1", "w2": "L3_gnn_W2", "b2": "L3_gnn_b2",
    }
    for short, name in names.items():
        arrays[short] = get[name].reshape(1, 1) if short == "l0_alpha" else get[name]
    nc = _bacc.Bacc("TRN2", target_bir_lowering=False, num_devices=1)
    maps, args = {}, {}
    for name, a in arrays.items():
        a = _np.ascontiguousarray(a)
        maps[f"in_{name}"] = a
        args[name] = nc.dram_tensor(f"in_{name}", a.shape, _mybir.dt.from_np(a.dtype), kind="ExternalInput").ap()
    args["out"] = nc.dram_tensor("out_dram", (N, D), F32, kind="ExternalOutput").ap()
    build(nc, **args)
    r = _run(nc, [maps], core_ids=[0])
    return r.results[0]["out_dram"]
```
